# Optimizing a Trainium2 kernel written in Bass

```python
import numpy as np
import jax
import jax.numpy as jnp

def _softmax(x, axis=-1):
    return jax.nn.softmax(x, axis=axis)
def _gelu(x):
    return jax.nn.gelu(x, approximate=True)
def _silu(x):
    return jax.nn.silu(x)
def _sigmoid(x):
    return jax.nn.sigmoid(x)
def _layernorm(x, axis=-1, eps=1e-5):
    m = jnp.mean(x, axis=axis, keepdims=True)
    v = jnp.var(x, axis=axis, keepdims=True)
    return (x - m) / jnp.sqrt(v + eps)
def _scatter_add(tgt, idx, src, axis=0):
    return tgt.at[idx].add(src)
def _segment_sum(src, seg, n):
    return jax.ops.segment_sum(src, seg, n)

kernel_name = 'mk_conv_preact_d2_conv_nhwc64_2f6f09'

def setup_inputs(seed: int = 0):
    np.random.seed(seed)
    _w = jnp.asarray
    def _rec_inputs():
        import jax
        import jax.numpy as jnp
        _gk = jax.random.key(seed)
        x = -0.0003929 + 0.9999 * jax.random.normal(jax.random.fold_in(_gk, 1), (1, 512, 512, 64), jnp.float32)
        return x
    x = _rec_inputs()
    def _L0_conv_setup():
        import jax, jax.numpy as jnp
        import numpy as np
        B, L, D, H = (1, 512, 64, 64)
        EPS = 1e-05

        def _ln(x, w, b):
            mu = jnp.mean(x, axis=-1, keepdims=True)
            var = jnp.var(x, axis=-1, keepdims=True)
            return (x - mu) * jax.lax.rsqrt(var + EPS) * w + b
        key = jax.random.key(seed)
        ks = jax.random.split(key, 16)
        s = 0.02
        return {'x': jax.random.normal(ks[0], (B, L, L, D), dtype=jnp.float32), 'sequence_mask': jax.random.randint(ks[1], (B, L), 0, 2, dtype=jnp.int32), 'norm_w': jnp.ones((D,), jnp.float32), 'norm_b': jnp.zeros((D,), jnp.float32), 'left_w': jax.random.normal(ks[2], (D, H), jnp.float32) * s, 'left_b': jnp.zeros((H,), jnp.float32), 'right_w': jax.random.normal(ks[3], (D, H), jnp.float32) * s, 'right_b': jnp.zeros((H,), jnp.float32), 'lgate_w': jax.random.normal(ks[4], (D, H), jnp.float32) * s, 'lgate_b': jnp.ones((H,), jnp.float32), 'rgate_w': jax.random.normal(ks[5], (D, H), jnp.float32) * s, 'rgate_b': jnp.ones((H,), jnp.float32), 'ogate_w': jax.random.normal(ks[6], (D, D), jnp.float32) * s, 'ogate_b': jnp.ones((D,), jnp.float32), 'onorm_w': jnp.ones((H,), jnp.float32), 'onorm_b': jnp.zeros((H,), jnp.float32), 'out_w': jax.random.normal(ks[7], (H, D), jnp.float32) * s, 'out_b': jnp.zeros((D,), jnp.float32)}
    _L0_conv_all = _L0_conv_setup()
    _L0_conv_in = {k: v for k, v in _L0_conv_all.items() if k in ('sequence_mask', 'norm_w', 'norm_b', 'left_w', 'left_b', 'right_w', 'right_b', 'lgate_w', 'lgate_b', 'rgate_w', 'rgate_b', 'ogate_w', 'ogate_b', 'onorm_w', 'onorm_b', 'out_w', 'out_b', )}
    del _L0_conv_all

    def _L1_conv_setup():
        import jax, jax.numpy as jnp
        import numpy as np
        MODES = 12
        IN_C = 64
        OUT_C = 64
        key = jax.random.key(seed)
        k1, k2, k3 = jax.random.split(key, 3)
        x = jax.random.normal(k1, (8, 256, 256, IN_C), dtype=jnp.float32)
        w_real = jax.random.normal(k2, (IN_C, OUT_C, MODES, MODES), dtype=jnp.float32) * 0.01
        w_imag = jax.random.normal(k3, (IN_C, OUT_C, MODES, MODES), dtype=jnp.float32) * 0.01
        return {'x': x, 'w_real': w_real, 'w_imag': w_imag}
    _L1_conv_all = _L1_conv_setup()
    _L1_conv_in = {k: v for k, v in _L1_conv_all.items() if k in ('w_real', 'w_imag', )}
    del _L1_conv_all

    return {
        "x": x,
        "L0_conv_sequence_mask": _L0_conv_in["sequence_mask"],
        "L0_conv_norm_w": _L0_conv_in["norm_w"],
        "L0_conv_norm_b": _L0_conv_in["norm_b"],
        "L0_conv_left_w": _L0_conv_in["left_w"],
        "L0_conv_left_b": _L0_conv_in["left_b"],
        "L0_conv_right_w": _L0_conv_in["right_w"],
        "L0_conv_right_b": _L0_conv_in["right_b"],
        "L0_conv_lgate_w": _L0_conv_in["lgate_w"],
        "L0_conv_lgate_b": _L0_conv_in["lgate_b"],
        "L0_conv_rgate_w": _L0_conv_in["rgate_w"],
        "L0_conv_rgate_b": _L0_conv_in["rgate_b"],
        "L0_conv_ogate_w": _L0_conv_in["ogate_w"],
        "L0_conv_ogate_b": _L0_conv_in["ogate_b"],
        "L0_conv_onorm_w": _L0_conv_in["onorm_w"],
        "L0_conv_onorm_b": _L0_conv_in["onorm_b"],
        "L0_conv_out_w": _L0_conv_in["out_w"],
        "L0_conv_out_b": _L0_conv_in["out_b"],
        "L1_conv_w_real": _L1_conv_in["w_real"],
        "L1_conv_w_imag": _L1_conv_in["w_imag"],
    }

def reference(x, L0_conv_sequence_mask, L0_conv_norm_w, L0_conv_norm_b, L0_conv_left_w, L0_conv_left_b, L0_conv_right_w, L0_conv_right_b, L0_conv_lgate_w, L0_conv_lgate_b, L0_conv_rgate_w, L0_conv_rgate_b, L0_conv_ogate_w, L0_conv_ogate_b, L0_conv_onorm_w, L0_conv_onorm_b, L0_conv_out_w, L0_conv_out_b, L1_conv_w_real, L1_conv_w_imag):
    import jax
    import jax.numpy as jnp
    def _L0_conv_ref(x, sequence_mask, norm_w, norm_b, left_w, left_b, right_w, right_b, lgate_w, lgate_b, rgate_w, rgate_b, ogate_w, ogate_b, onorm_w, onorm_b, out_w, out_b):
        import jax, jax.numpy as jnp
        import numpy as np
        B, L, D, H = (1, 512, 64, 64)
        EPS = 1e-05

        def _ln(x, w, b):
            mu = jnp.mean(x, axis=-1, keepdims=True)
            var = jnp.var(x, axis=-1, keepdims=True)
            return (x - mu) * jax.lax.rsqrt(var + EPS) * w + b
        xn = _ln(x, norm_w, norm_b)
        left = xn @ left_w + left_b
        right = xn @ right_w + right_b
        m = sequence_mask.astype(xn.dtype)
        mask = (m[:, :, None] * m[:, None, :])[..., None]
        left = left * mask
        right = right * mask
        left = left * jax.nn.sigmoid(xn @ lgate_w + lgate_b)
        right = right * jax.nn.sigmoid(xn @ rgate_w + rgate_b)
        out_gate = jax.nn.sigmoid(xn @ ogate_w + ogate_b)
        out = jnp.einsum('bkjd,bkid->bijd', left, right)
        out = _ln(out, onorm_w, onorm_b)
        out = out @ out_w + out_b
        return out * out_gate

    def _L1_conv_ref(x, w_real, w_imag):
        import jax, jax.numpy as jnp
        import numpy as np
        MODES = 12
        IN_C = 64
        OUT_C = 64
        xc = jnp.transpose(x, (0, 3, 1, 2)).astype(jnp.complex64)
        x_ft = jnp.fft.fft2(xc, axes=(-2, -1))
        x_ft = x_ft[:, :, :MODES, :MODES]
        w = w_real + 1j * w_imag
        out_ft = jnp.einsum('bcmn,comn->bomn', x_ft, w)
        B = x.shape[0]
        H, W = (x.shape[1], x.shape[2])
        out_full = jnp.zeros((B, OUT_C, H, W), dtype=jnp.complex64)
        out_full = out_full.at[:, :, :MODES, :MODES].set(out_ft)
        out = jnp.fft.ifft2(out_full, axes=(-2, -1))
        return jnp.transpose(jnp.real(out), (0, 2, 3, 1))

    def _gn(v, G=32, eps=1e-5):
        B_, H_, W_, C_ = v.shape
        g = v.reshape(B_, H_, W_, G, C_ // G)
        m = jnp.mean(g, axis=(1, 2, 4), keepdims=True)
        s = jnp.var(g, axis=(1, 2, 4), keepdims=True)
        return ((g - m) / jnp.sqrt(s + eps)).reshape(v.shape)

    def _ln_c(v, eps=1e-6):
        m = jnp.mean(v, axis=-1, keepdims=True)
        s = jnp.var(v, axis=-1, keepdims=True)
        return (v - m) / jnp.sqrt(s + eps)

    def _ln_t(v, eps=1e-5):
        m = jnp.mean(v, axis=-1, keepdims=True)
        s = jnp.var(v, axis=-1, keepdims=True)
        return (v - m) / jnp.sqrt(s + eps)

    def _to_tokens(v):
        B_, H_, W_, C_ = v.shape
        return v.reshape(B_, H_ * W_, C_)
    def _from_tokens(t, like):
        return t.reshape(like.shape)

    x = x + _L0_conv_ref(_gn(x), L0_conv_sequence_mask, L0_conv_norm_w, L0_conv_norm_b, L0_conv_left_w, L0_conv_left_b, L0_conv_right_w, L0_conv_right_b, L0_conv_lgate_w, L0_conv_lgate_b, L0_conv_rgate_w, L0_conv_rgate_b, L0_conv_ogate_w, L0_conv_ogate_b, L0_conv_onorm_w, L0_conv_onorm_b, L0_conv_out_w, L0_conv_out_b)
    x = x + _L1_conv_ref(_gn(x), L1_conv_w_real, L1_conv_w_imag)
    return x


_drawn_inputs = setup_inputs


def setup_inputs(seed=0):
    import zlib

    import numpy as np

    out = dict(_drawn_inputs(seed))
    spreads = {'L0_conv_norm_w': (1.0, 0.6),
     'L0_conv_norm_b': (0.0, 0.603),
     'L0_conv_left_b': (0.0, 0.537),
     'L0_conv_right_b': (0.0, 0.731),
     'L0_conv_lgate_b': (1.0, 0.6),
     'L0_conv_rgate_b': (1.0, 0.6),
     'L0_conv_ogate_b': (1.0, 0.6),
     'L0_conv_onorm_w': (1.0, 0.6),
     'L0_conv_onorm_b': (0.0, 0.686),
     'L0_conv_out_b': (0.0, 0.1)}
    factors = {'L0_conv_left_w': 4.187,
     'L0_conv_right_w': 3.934,
     'L0_conv_lgate_w': 23.353,
     'L0_conv_rgate_w': 31.853,
     'L0_conv_ogate_w': 8.0,
     'L1_conv_w_real': 8.0,
     'L1_conv_w_imag': 42.002}
    for name, (base, spread) in spreads.items():
        noise = np.random.default_rng([zlib.crc32(name.encode()), seed]).standard_normal(out[name].shape)
        drawn = base * np.exp(spread * noise) if base else spread * noise
        out[name] = jnp.asarray(drawn.astype(out[name].dtype))
    for name, factor in factors.items():
        out[name] = (out[name] * factor).astype(out[name].dtype)
    return out
```

```python
from contextlib import ExitStack

import numpy as np

import concourse.bass as bass
from concourse import mybir

F32 = mybir.dt.float32
BF16 = mybir.dt.bfloat16
I32 = mybir.dt.int32
ALU = mybir.AluOpType
ACT = mybir.ActivationFunctionType
AX = mybir.AxisListType

P = 128
L = 512
C = 64
G = 32
CG = C // G
MODES = 12
M2 = 2 * MODES
TOK = L * L
TR = 8
NT = L // TR
UN = TR // 2
WT = L // P
H = L // 2
EPS = 1e-5
DMA = 16
STATS_T = 256
NCHUNK = TOK // (P * STATS_T)


def host_tables():
    pos = np.arange(L)[:, None] * np.arange(MODES)[None, :] * (2 * np.pi / L)
    fourier = np.concatenate([np.cos(pos), np.sin(pos)], axis=1)
    basis = fourier.reshape(P, WT, M2).astype(np.float32)
    inverse = np.zeros((P, L), np.float32)
    inverse[:M2] = fourier.T / L
    half = np.arange(P) // C
    same = (half[:, None] == half[None, :]).astype(np.float32)
    centre = (np.eye(P) - same / C).astype(np.float32)
    average = (half[:, None] == np.arange(2)[None, :]).astype(np.float32) / C
    part_row = np.arange(3 * 8 * UN) % (8 * UN)
    blocks = np.arange(UN * WT)
    select = (part_row[:, None, None] == 2 * blocks[None, :, None] + half[None, None, :]).astype(np.float32)
    group = np.arange(C) // CG
    pair = (group[:, None] == group[None, :]).astype(np.float32) / CG
    return {
        "t_ident": np.eye(P, dtype=np.float32),
        "t_basis": basis,
        "t_inverse": inverse,
        "t_centre": centre,
        "t_average": average.astype(np.float32),
        "t_select": select,
        "t_pair": pair,
    }


class Tools:

    def __init__(self, nc, ctx, phase):
        self.nc, self.ctx, self.phase = nc, ctx, phase

    def sb(self, name, shape, dt=F32):
        return self.ctx.enter_context(self.nc.sbuf_tensor(f"{self.phase}_{name}", shape, dt))

    def ps(self, name, shape):
        n = int(np.prod(shape[1:]))
        banks = -(-n // 512)
        whole = self.ctx.enter_context(self.nc.psum_tensor(f"{self.phase}_{name}_ps", [shape[0], banks * 512], F32))
        view = whole[:, 0:n]
        if len(shape) == 2:
            return view
        names = "abcd"[:len(shape) - 1]
        return view.rearrange(f"p ({' '.join(names)}) -> p {' '.join(names)}", **dict(zip(names, shape[1:])))

    def sem(self, name):
        return self.ctx.enter_context(self.nc.semaphore(f"{self.phase}_{name}"))


def chained(eng, sem, start=0):
    n = [start]

    def link(instruction):
        n[0] += 1
        instruction.then_inc(sem, 1)
        eng.wait_ge(sem, n[0])

    return link




def statistics_of_x(nc, x, keep):
    with ExitStack() as ctx:
        t = Tools(nc, ctx, "st")
        xc = [t.sb(f"x{b}", [P, STATS_T, C]) for b in range(2)]
        stats = t.sb("stats", [P, G, NCHUNK, 6])
        part = t.sb("part", [P, G, 2])
        dev = t.sb("dev", [P, G])
        sq = t.sb("sq", [P, G])
        spread = t.sb("spread", [P, G])
        ones = t.sb("ones", [P, P])
        mean_ps = t.ps("mean", [P, 512])
        var_ps = t.ps("var", [P, 512])
        loaded = [t.sem(f"loaded{b}") for b in range(2)]
        ones_set = t.sem("ones_set")
        chunk_done = t.sem("chunk_done")
        step = t.sem("step")
        mean_ready = t.sem("mean_ready")
        var_ready = t.sem("var_ready")
        spread_ready = t.sem("spread_ready")
        x_v = x.rearrange("a h w c -> (a h w c)").rearrange("(n p t c) -> n p t c", p=P, t=STATS_T, c=C)
        block = ctx.enter_context(nc.Block())

        @block.sync
        def _(sp):
            for b in range(2):
                sp.dma_start(xc[b][:, :, :], x_v[b]).then_inc(loaded[b], DMA)
            with sp.Fori(1, NCHUNK // 2) as j:
                for b in range(2):
                    sp.wait_ge(chunk_done, 2 * j + b - 1)
                    sp.dma_start(xc[b][:, :, :], x_v[2 * j + b]).then_inc(loaded[b], DMA)

        @block.vector
        def _(dve):
            with dve.Fori(0, NCHUNK // 2) as j:
                for b in range(2):
                    dve.wait_ge(loaded[b], DMA * j + DMA)
                    for g in range(G):
                        last = dve.bn_stats(stats[:, g, 2 * j + b, :], xc[b][:, :, CG * g:CG * g + CG])
                    last.then_inc(chunk_done, 1)
            link = chained(dve, step)
            dve.wait_ge(chunk_done, NCHUNK)
            for g in range(G):
                last = dve.bn_aggr(part[:, g, :], stats[:, g, :, :].rearrange("p n s -> p (n s)"))
            link(last)
            dve.tensor_copy(dev[:, :], part[:, :, 0]).then_inc(spread_ready, 1)
            dve.wait_ge(mean_ready, 1)
            link(dve.tensor_copy(keep.mean0[:, :], mean_ps[:, 0:G]))
            link(dve.tensor_tensor(sq[:, :], part[:, :, 0], keep.mean0[:, :], ALU.subtract))
            link(dve.tensor_tensor(spread[:, :], sq[:, :], sq[:, :], ALU.mult))
            dve.tensor_tensor(spread[:, :], spread[:, :], part[:, :, 1], ALU.add).then_inc(spread_ready, 1)
            dve.wait_ge(var_ready, 1)
            dve.tensor_copy(keep.var0[:, :], var_ps[:, 0:G]).then_inc(step, 1)

        @block.gpsimd
        def _(pool):
            pool.memset(ones[:, :], 1.0 / P).then_inc(ones_set, 1)

        @block.tensor
        def _(pe):
            pe.wait_ge(ones_set, 1)
            pe.wait_ge(spread_ready, 1)
            pe.matmul(mean_ps[:, 0:G], ones[:, :], dev[:, :], start=True, stop=True).then_inc(mean_ready, 1)
            pe.wait_ge(spread_ready, 2)
            pe.matmul(var_ps[:, 0:G], ones[:, :], spread[:, :], start=True, stop=True).then_inc(var_ready, 1)




def prepare(nc, ins, tab, keep):
    with ExitStack() as ctx:
        t = Tools(nc, ctx, "pr")
        names = ["left", "lgate", "right", "rgate", "ogate"]
        w_raw = t.sb("w_raw", [P, 5, C])
        w_scaled = t.sb("w_scaled", [P, 5, C])
        w_raw_bd = t.sb("w_raw_bd", [P, 4, P])
        nw = t.sb("nw", [P, 1])
        nb = t.sb("nb", [P, 1])
        bias_in = t.sb("bias_in", [P, 4])
        centre = t.sb("centre", [P, P])
        select = t.sb("select", [3 * 8 * UN, UN * WT, P])
        onw = t.sb("onw", [P, 1])
        onb = t.sb("onb", [C, 1])
        ow = t.sb("ow", [P, C])
        ow_scaled = t.sb("ow_scaled", [P, C])
        onb_wide = t.sb("onb_wide", [C, P])
        row_in = t.sb("row_in", [1, 2, C])
        grow = t.sb("grow", [1, 3, C])
        ghi = t.sb("ghi", [1, 2, C])
        ones_row = t.sb("ones_row", [1, P])
        mask_col = t.sb("mask_col", [P, WT], I32)
        mask_row = t.sb("mask_row", [1, L], I32)
        maskf_col = t.sb("maskf_col", [P, WT])
        maskf_row = t.sb("maskf_row", [1, L])
        mask_wide = t.sb("mask_wide", [P, L])
        rstd = t.sb("rstd", [P, G])
        shift = t.sb("shift", [P, G])
        root = t.sb("root", [P, G])
        wide = t.sb("wide", [P, 2, P])
        w_ps = t.ps("w", [P, 5, C])
        b_ps = t.ps("b", [P, 4])
        ow_ps = t.ps("ow", [P, C])
        c_ps = t.ps("c", [P, C])
        g_ps = t.ps("g", [1, C])
        m_ps = t.ps("m", [P, L])
        loaded = t.sem("loaded")
        step = t.sem("step")
        pool_set = t.sem("pool_set")
        raw_ready = t.sem("raw_ready")
        scaled_ready = t.sem("scaled_ready")
        row_ready = t.sem("row_ready")
        products = t.sem("products")
        root_in = t.sem("root_in")
        root_ready = t.sem("root_ready")
        loads = []
        for i, n in enumerate(names):
            for h in range(2):
                loads.append((w_raw[h * C:(h + 1) * C, i, :], ins[f"L0_conv_{n}_w"]))
        for h in range(2):
            rows = slice(h * C, (h + 1) * C)

            def col(v):
                return v.rearrange("(c o) -> c o", o=1)

            loads.append((nw[rows, :], col(ins["L0_conv_norm_w"])))
            loads.append((nb[rows, :], col(ins["L0_conv_norm_b"])))
            loads.append((onw[rows, :], col(ins["L0_conv_onorm_w"])))
            loads.append((ow[rows, :], ins["L0_conv_out_w"]))
            for i, n in enumerate(names[:4]):
                loads.append((bias_in[rows, i:i + 1], col(ins[f"L0_conv_{n}_b"])))
        loads.append((onb[:, :], ins["L0_conv_onorm_b"].rearrange("(c o) -> c o", o=1)))
        loads.append((row_in[:, 0, :], ins["L0_conv_ogate_b"].rearrange("(o c) -> o c", o=1)))
        loads.append((row_in[:, 1, :], ins["L0_conv_out_b"].rearrange("(o c) -> o c", o=1)))
        loads.append((mask_col[:, :], ins["L0_conv_sequence_mask"].rearrange("a (p t) -> (a p) t", t=WT)))
        loads.append((mask_row[:, :], ins["L0_conv_sequence_mask"]))
        loads.append((centre[:, :], tab["t_centre"]))
        loads.append((select[:, :, :], tab["t_select"]))
        loads.append((keep.ident[:, :], tab["t_ident"]))
        loads.append((keep.basis[:, :, :], tab["t_basis"]))
        loads.append((keep.inverse[:, :], tab["t_inverse"]))
        loads.append((keep.average[:, :], tab["t_average"]))
        loads.append((keep.pair[:, :], tab["t_pair"]))
        block = ctx.enter_context(nc.Block())

        @block.sync
        def _(sp):
            for dst, src in loads:
                sp.dma_start(dst, src).then_inc(loaded, DMA)

        @block.gpsimd
        def _(pool):
            pool.memset(w_raw_bd[:, :, :], 0.0).then_inc(pool_set, 1)
            pool.memset(keep.w_bd[:, :, :], 0.0).then_inc(pool_set, 1)
            pool.memset(keep.w2_bd[:, :], 0.0).then_inc(pool_set, 1)
            pool.memset(keep.gbias3[:, :], 0.0).then_inc(pool_set, 1)
            pool.memset(keep.ones_bf[:, :], 1.0).then_inc(pool_set, 1)
            pool.memset(ones_row[:, :], 1.0).then_inc(pool_set, 1)
            pool.memset(keep.ones_col[:, :], 1.0).then_inc(pool_set, 1)

        @block.scalar
        def _(act):
            act.wait_ge(root_in, 1)
            act.activation(root[:, :], rstd[:, :], ACT.Sqrt).then_inc(root_ready, 1)

        @block.tensor
        def _(pe):
            pe.wait_ge(loaded, DMA * len(loads))
            pe.wait_ge(scaled_ready, 1)
            pe.matmul(w_ps[:, :, :], centre[:, :], w_scaled[:, :, :], start=True, stop=True)
            pe.matmul(ow_ps[:, :], centre[:, :], ow_scaled[:, :], start=True, stop=True)
            pe.wait_ge(raw_ready, 1)
            for i in range(4):
                pe.matmul(b_ps[:, i:i + 1], w_raw_bd[:, i, :], nb[:, :], start=True, stop=True)
            pe.matmul(g_ps[:, :], nb[0:C, :], w_raw[0:C, 4, :], start=True, stop=True)
            pe.wait_ge(pool_set, 7)
            pe.matmul(c_ps[:, :], onb_wide[:, :], ow[0:C, :], start=True, stop=False)
            pe.matmul(c_ps[:, :], ones_row[:, :], row_in[:, 1, :], start=False, stop=True)
            pe.wait_ge(row_ready, 1)
            pe.matmul(m_ps[:, :], ones_row[:, :], maskf_row[:, :], start=True, stop=True).then_inc(products, 1)

        @block.vector
        def _(dve):
            link = chained(dve, step)
            dve.wait_ge(loaded, DMA * len(loads))
            dve.wait_ge(pool_set, 7)
            dve.tensor_scalar(ow_scaled[:, :], ow[:, :], onw[:, 0:1], None, ALU.mult)
            dve.tensor_scalar(w_scaled[:, :, :], w_raw[:, :, :], nw[:, 0:1], None, ALU.mult).then_inc(scaled_ready, 1)
            for h in range(2):
                rows = slice(h * C, (h + 1) * C)
                dve.tensor_copy(w_raw_bd[rows, :, h * C:(h + 1) * C], w_raw[rows, 0:4, :])
            dve.tensor_copy(onb_wide[:, :], onb[:, :].to_broadcast([C, P])).then_inc(raw_ready, 1)
            dve.tensor_copy(maskf_row[:, :], mask_row[:, :]).then_inc(row_ready, 1)
            dve.tensor_copy(keep.select[:, :, :], select[:, :, :])
            link(dve.tensor_copy(maskf_col[:, :], mask_col[:, :]))
            dve.tensor_tensor(keep.mask_sq[:, :], maskf_col[:, :], maskf_col[:, :], ALU.mult)
            dve.tensor_scalar(rstd[:, :], keep.var0[:, :], EPS, None, ALU.add).then_inc(root_in, 1)
            dve.wait_ge(root_ready, 1)
            link(dve.reciprocal(shift[:, :], root[:, :]))
            link(dve.tensor_copy(wide[:, 0, :].rearrange("p (h g e) -> p h g e", h=2, e=CG),
                                 shift[:, :].unsqueeze(1).unsqueeze(3).to_broadcast([P, 2, G, CG])))
            link(dve.tensor_tensor(rstd[:, :], keep.mean0[:, :], shift[:, :], ALU.mult))
            link(dve.tensor_copy(wide[:, 1, :].rearrange("p (h g e) -> p h g e", h=2, e=CG),
                                 rstd[:, :].unsqueeze(1).unsqueeze(3).to_broadcast([P, 2, G, CG])))
            link(dve.tensor_tensor(wide[:, :, :], wide[:, :, :],
                                   keep.ident[:, :].unsqueeze(1).to_broadcast([P, 2, P]), ALU.mult))
            dve.tensor_reduce(keep.gn_scale[:, :], wide[:, 0, :], AX.X, ALU.add)
            dve.tensor_reduce(keep.gn_shift[:, :], wide[:, 1, :], AX.X, ALU.add, negate=True)
            dve.wait_ge(products, 1)
            for h in range(2):
                rows = slice(h * C, (h + 1) * C)
                dve.tensor_copy(keep.w_bd[rows, :, h * C:(h + 1) * C], w_ps[rows, :, :])
                dve.tensor_copy(keep.w2_bd[rows, h * C:(h + 1) * C], ow_ps[rows, :])
            dve.tensor_tensor(keep.bias[:, :], b_ps[:, :], bias_in[:, :], ALU.add)
            dve.tensor_copy(keep.c_row[:, :], c_ps[:, :])
            link(dve.tensor_copy(mask_wide[:, :], m_ps[:, :]))
            view = keep.mask_tok[:, :].rearrange("p (i t) -> p i t", t=WT)
            for k in range(WT):
                last = dve.tensor_scalar(view[:, :, k], mask_wide[:, :], maskf_col[:, k:k + 1], None, ALU.mult)
            link(last)
            dve.tensor_tensor(keep.mask_tok_sq[:, :], keep.mask_tok[:, :], keep.mask_tok[:, :], ALU.mult)
            link(dve.tensor_tensor(grow[:, 0, :], g_ps[:, :], row_in[:, 0, :], ALU.add))
            for k in range(3):
                row = keep.gbias3[32 * k:32 * k + 1, :].rearrange("p (n c) -> p n c", c=C)
                link(dve.tensor_copy(row, grow[:, k, :].unsqueeze(1).to_broadcast([1, 8, C])))
                if k < 2:
                    link(dve.tensor_copy(ghi[:, k, :], keep.gbias3[32 * k:32 * k + 1, 0:C]))
                    link(dve.tensor_tensor(grow[:, k + 1, :], grow[:, k, :], ghi[:, k, :], ALU.subtract))




def project(nc, x, left_d, right_d, gate_d, keep):
    with ExitStack() as ctx:
        t = Tools(nc, ctx, "pj")
        xt = [t.sb(f"x{b}", [P, TR, WT, C]) for b in range(2)]
        gn = [t.sb(f"gn{b}", [P, UN, L]) for b in range(2)]
        sq = [t.sb(f"sq{b}", [P, L]) for b in range(2)]
        xn = [t.sb(f"xn{b}", [P, L]) for b in range(2)]
        sig = [t.sb(f"sig{b}", [P, L]) for b in range(2)]
        out = [[t.sb(f"out{s}{b}", [P, UN, L]) for b in range(2)] for s in range(2)]
        gout = [t.sb(f"gout{b}", [P, TR, WT, C]) for b in range(2)]
        st = t.sb("st", [P, 64])
        m_sq = t.sb("m_sq", [P, 32])
        var = t.sb("var", [P, 32])
        var_eps = t.sb("var_eps", [P, 32])
        power = t.sb("power", [P, 32])
        rs = t.sb("rs", [P, 32])
        rst = t.sb("rst", [32, 2, P])
        parts = [t.sb(f"parts{b}", [96, P], BF16) for b in range(2)]
        x_ps = t.ps("x", [P, L])
        st_ps = t.ps("st", [P, 64 + P])
        rs_ps = t.ps("rs", [P, L])
        proj_ps = [[t.ps(f"proj{s}{k}", [P, L]) for k in range(2)] for s in range(2)]
        g_ps = t.ps("g", [P, L])

        x_loaded = [t.sem(f"x_loaded{b}") for b in range(2)]
        stored = [[t.sem(f"stored{s}{b}") for b in range(2)] for s in range(3)]
        xt_ready = t.sem("xt_ready")
        gn_ready = t.sem("gn_ready")
        st_ready = t.sem("st_ready")
        small = t.sem("small")
        power_set = t.sem("power_set")
        rs_ready = t.sem("rs_ready")
        rst_ready = t.sem("rst_ready")
        parts_ready = t.sem("parts_ready")
        bc_ready = t.sem("bc_ready")
        xn_ready = t.sem("xn_ready")
        gate_ready = [t.sem(f"gate_ready{s}") for s in range(2)]
        val_ready = [t.sem(f"val_ready{s}") for s in range(2)]
        sig_ready = [t.sem(f"sig_ready{s}") for s in range(2)]
        gated = [t.sem(f"gated{s}") for s in range(2)]
        g_ready = t.sem("g_ready")
        g_done = t.sem("g_done")

        x_v = x.rearrange("a (n r) (p t) c -> (a n) p r t c", r=TR, t=WT)
        side_v = [d.rearrange("e d (n r) j -> n (e d) (r j)", r=TR) for d in (left_d, right_d)]
        gate_v = gate_d.rearrange("(n r) (p t) c -> n p r t c", r=TR, t=WT)
        block = ctx.enter_context(nc.Block())

        def tiles(eng, body):
            for n in range(2):
                body(n, n, 0)
            with eng.Fori(1, NT // 2 - 1) as j:
                for b in range(2):
                    body(2 * j + b, b, j)
            for b in range(2):
                body(NT - 2 + b, b, NT // 2 - 1)

        def is_first(n):
            return isinstance(n, int) and n < 2

        def has_next(n):
            return not (isinstance(n, int) and n == NT - 1)

        @block.sync
        def _(sp):
            for b in range(2):
                sp.dma_start(xt[b][:, :, :, :], x_v[b]).then_inc(x_loaded[b], DMA)

            def body(n, b, j):
                if not (isinstance(n, int) and n >= NT - 2):
                    sp.wait_ge(xt_ready, UN * n + UN)
                    sp.dma_start(xt[b][:, :, :, :], x_v[n + 2]).then_inc(x_loaded[b], DMA)
                for s in range(2):
                    sp.wait_ge(gated[s], UN * n + UN)
                    sp.dma_start(side_v[s][n], out[s][b][:, :, :].rearrange("p q j -> p (q j)")).then_inc(stored[s][b], DMA)
                sp.wait_ge(g_done, UN * n + UN)
                sp.dma_start(gate_v[n], gout[b][:, :, :, :]).then_inc(stored[2][b], DMA)

            tiles(sp, body)
            for b in range(2):
                for s in range(2):
                    sp.wait_ge(stored[s][b], DMA * (NT // 2))
                sp.wait_ge(stored[2][b], DMA * (NT // 2))

        @block.tensor
        def _(pe):
            def transposes(n, q, b, j):
                if q == 0:
                    pe.wait_ge(x_loaded[b], DMA * j + DMA)
                pe.wait_ge(gn_ready, UN * n + q)
                for r in range(2):
                    for k in range(2):
                        last = pe.transpose(x_ps[:, H * r + k:H * r + H:2],
                                            xt[b][:, 2 * q + r, 2 * k:2 * k + 2, :].rearrange("p t c -> p (t c)"),
                                            keep.ident[:, :])
                last.then_inc(xt_ready, 1)

            def statistics(n, q, b):
                pe.wait_ge(gn_ready, UN * n + q + 1)
                if q == 0 and not (isinstance(n, int) and n == 0):
                    pe.wait_ge(small, 5 * n - 4)
                for k in range(WT):
                    c = 2 * WT * q + 2 * k
                    pe.matmul(st_ps[:, c:c + 2], gn[b][:, q, P * k:P * k + P], keep.average[:, :],
                              start=True, stop=True)
                    last = pe.matmul(st_ps[:, 32 + c:34 + c], sq[q % 2][:, P * k:P * k + P], keep.average[:, :],
                                     start=True, stop=True)
                last.then_inc(st_ready, 1)

            def rs_transpose(n):
                pe.wait_ge(rs_ready, n + 1)
                if not (isinstance(n, int) and n == 0):
                    pe.wait_ge(parts_ready, 5 * n)
                pe.transpose(st_ps[0:32, 64:64 + P], rs[:, :], keep.ident[:, :]).then_inc(rst_ready, 1)

            def spread(n, q, b):
                pe.wait_ge(parts_ready, 5 * n + 5)
                pe.wait_ge(xn_ready, UN * n + q)
                for k in range(WT):
                    last = pe.matmul(rs_ps[:, P * k:P * k + P], keep.select[:, WT * q + k, :], parts[b][:, :],
                                     start=True, stop=True)
                last.then_inc(bc_ready, 1)

            def side(n, q, s):
                pe.wait_ge(gated[s], UN * n + q)
                pe.matmul(proj_ps[s][1][:, :], keep.w_bd[:, 2 * s + 1, :], xn[q % 2][:, :],
                          start=True, stop=True).then_inc(gate_ready[s], 1)
                pe.matmul(proj_ps[s][0][:, :], keep.w_bd[:, 2 * s, :], xn[q % 2][:, :],
                          start=True, stop=True).then_inc(val_ready[s], 1)

            def left(n, q):
                pe.wait_ge(xn_ready, UN * n + q + 1)
                side(n, q, 0)

            def right(n, q):
                side(n, q, 1)
                pe.wait_ge(g_done, UN * n + q)
                pe.matmul(g_ps[:, :], keep.ones_bf[:, :], keep.gbias3[:, :], start=True, stop=False)
                for k in range(WT):
                    at = H * (k // 2) + k % 2
                    last = pe.matmul(g_ps[:, P * k:P * k + P], xn[q % 2][:, at:at + H - 1:2], keep.w_bd[:, 4, :],
                                     start=False, stop=(k == WT - 1))
                last.then_inc(g_ready, 1)

            for q in range(UN):
                transposes(0, q, 0, 0)
                statistics(0, q, 0)
            rs_transpose(0)
            spread(0, 0, 0)

            def body(n, b, j):
                nxt = has_next(n)
                m, c, jn = n + 1, 1 - b, j + b
                if nxt:
                    transposes(m, 0, c, jn)
                left(n, 0)
                spread(n, 1, b)
                if nxt:
                    statistics(m, 0, c)
                    transposes(m, 1, c, jn)
                right(n, 0)
                if nxt:
                    statistics(m, 1, c)
                    transposes(m, 2, c, jn)
                left(n, 1)
                spread(n, 2, b)
                if nxt:
                    statistics(m, 2, c)
                    transposes(m, 3, c, jn)
                right(n, 1)
                if nxt:
                    statistics(m, 3, c)
                left(n, 2)
                spread(n, 3, b)
                right(n, 2)
                left(n, 3)
                if nxt:
                    rs_transpose(m)
                right(n, 3)
                if nxt:
                    spread(m, 0, c)

            tiles(pe, body)

        @block.scalar
        def _(act):
            def normalise(n, q, b):
                act.wait_ge(xt_ready, UN * n + q + 1)
                if not is_first(n):
                    act.wait_ge(xn_ready, UN * (n - 2) + q + 1)
                act.activation(gn[b][:, q, :], x_ps[:, :], ACT.Identity, bias=keep.gn_shift[:, 0:1],
                               scale=keep.gn_scale[:, 0:1])
                if not (isinstance(n, int) and n == 0 and q < 2):
                    act.wait_ge(st_ready, UN * n + q - 1)
                act.activation(sq[q % 2][:, :], x_ps[:, :], ACT.Square, bias=keep.gn_shift[:, 0:1],
                               scale=keep.gn_scale[:, 0:1]).then_inc(gn_ready, 1)

            def sigmoid(n, q, s):
                act.wait_ge(gate_ready[s], UN * n + q + 1)
                act.activation(sig[s][:, :], proj_ps[s][1][:, :], ACT.Sigmoid,
                               bias=keep.bias[:, 2 * s + 1:2 * s + 2]).then_inc(sig_ready[s], 1)

            def gate(n, q, b, j):
                act.wait_ge(g_ready, UN * n + q + 1)
                if q == 0 and not is_first(n):
                    act.wait_ge(stored[2][b], DMA * j)
                act.activation(gout[b][:, 2 * q:2 * q + 2, :, :].rearrange("p r t c -> p (r t c)"),
                               g_ps[:, :], ACT.Sigmoid).then_inc(g_done, 1)

            for q in range(UN):
                normalise(0, q, 0)

            def body(n, b, j):
                nxt = has_next(n)
                m, c = n + 1, 1 - b
                if nxt:
                    normalise(m, 0, c)
                for q in range(UN):
                    sigmoid(n, q, 0)
                    if nxt and q < 2:
                        normalise(m, 2 * q + 1, c)
                    sigmoid(n, q, 1)
                    gate(n, q, b, j)
                    if nxt and q == 0:
                        normalise(m, 2, c)

            tiles(act, body)

        @block.gpsimd
        def _(pool):
            pool.memset(power[:, :], -0.5).then_inc(power_set, 1)
            pool.wait_ge(power_set, 1)

            def body(n, b, j):
                pool.wait_ge(small, 5 * n + 5)
                if not (isinstance(n, int) and n == 0):
                    pool.wait_ge(rst_ready, n)
                pool.tensor_tensor(rs[:, :], var_eps[:, :], power[:, :], ALU.pow).then_inc(rs_ready, 1)

            tiles(pool, body)

        @block.vector
        def _(dve):
            def small_chain(n):
                dve.wait_ge(st_ready, UN * n + UN)
                if not (isinstance(n, int) and n == 0):
                    dve.wait_ge(rs_ready, n)
                dve.tensor_copy(st[:, :], st_ps[:, 0:64]).then_inc(small, 1)
                dve.wait_ge(small, 5 * n + 1)
                dve.tensor_tensor(m_sq[:, :], st[:, 0:32], st[:, 0:32], ALU.mult).then_inc(small, 1)
                dve.wait_ge(small, 5 * n + 2)
                dve.tensor_tensor(var[:, :], st[:, 32:64], m_sq[:, :], ALU.subtract).then_inc(small, 1)
                dve.wait_ge(small, 5 * n + 3)
                dve.tensor_scalar(var_eps[:, :], var[:, :], 0.0, EPS, ALU.max, ALU.add).then_inc(small, 2)

            def split(n, b):
                dve.wait_ge(rst_ready, n + 1)
                dve.tensor_copy(parts[b][0:32, :], st_ps[0:32, 64:64 + P]).then_inc(parts_ready, 1)
                dve.wait_ge(parts_ready, 5 * n + 1)
                dve.tensor_tensor(rst[:, 0, :], st_ps[0:32, 64:64 + P], parts[b][0:32, :],
                                  ALU.subtract).then_inc(parts_ready, 1)
                dve.wait_ge(parts_ready, 5 * n + 2)
                dve.tensor_copy(parts[b][32:64, :], rst[:, 0, :]).then_inc(parts_ready, 1)
                dve.wait_ge(parts_ready, 5 * n + 3)
                dve.tensor_copy(rst[:, 1, :], parts[b][32:64, :]).then_inc(parts_ready, 1)
                dve.wait_ge(parts_ready, 5 * n + 4)
                dve.tensor_tensor(parts[b][64:96, :], rst[:, 0, :], rst[:, 1, :],
                                  ALU.subtract).then_inc(parts_ready, 1)

            def normal(n, q, b):
                dve.wait_ge(bc_ready, UN * n + q + 1)
                if not (isinstance(n, int) and n == 0 and q < 2):
                    dve.wait_ge(g_ready, UN * n + q - 1)
                dve.tensor_tensor(xn[q % 2][:, :], rs_ps[:, :], gn[b][:, q, :], ALU.mult).then_inc(xn_ready, 1)

            def value(n, q, s, b, j):
                dve.wait_ge(sig_ready[s], UN * n + q + 1)
                dve.wait_ge(val_ready[s], UN * n + q + 1)
                if q == 0 and not is_first(n):
                    dve.wait_ge(stored[s][b], DMA * j)
                dve.scalar_tensor_tensor(out=out[s][b][:, q, :], in0=proj_ps[s][0][:, :],
                                         scalar=keep.bias[:, 2 * s:2 * s + 1], in1=sig[s][:, :],
                                         op0=ALU.add, op1=ALU.mult).then_inc(gated[s], 1)

            small_chain(0)
            split(0, 0)
            normal(0, 0, 0)

            def body(n, b, j):
                nxt = has_next(n)
                for q in range(UN):
                    if q < UN - 1:
                        normal(n, q + 1, b)
                    value(n, q, 0, b, j)
                    if q == UN - 1 and nxt:
                        split(n + 1, 1 - b)
                    value(n, q, 1, b, j)
                    if q == 1 and nxt:
                        small_chain(n + 1)
                    if q == UN - 1 and nxt:
                        normal(n + 1, 0, 1 - b)

            tiles(dve, body)




def contract(nc, left_d, right_d, mixed_d, keep):
    with ExitStack() as ctx:
        t = Tools(nc, ctx, "ct")
        lt = [t.sb(f"l{b}", [P, 2, WT, H]) for b in range(2)]
        rt = [t.sb(f"r{b}", [P, 2, WT, H]) for b in range(2)]
        lm = [t.sb(f"lm{b}", [P, 2, WT, H]) for b in range(2)]
        om = [t.sb(f"o{b}", [P, 2, WT, H]) for b in range(2)]
        acc = [[t.ps(f"acc{b}{i}", [P, L]) for i in range(WT)] for b in range(2)]
        l_loaded = [t.sem(f"l_loaded{b}") for b in range(2)]
        r_loaded = [t.sem(f"r_loaded{b}") for b in range(2)]
        stored = [t.sem(f"stored{b}") for b in range(2)]
        masked = t.sem("masked")
        summed = t.sem("summed")
        out_dve = t.sem("out_dve")
        out_act = t.sem("out_act")
        view = [d.rearrange("e d (p t) j -> d p e (t j)", t=WT) for d in (left_d, right_d, mixed_d)]
        block = ctx.enter_context(nc.Block())

        def channels(eng, body):
            for n in range(2):
                body(n, n, 0)
            with eng.Fori(1, C // 2 - 1) as j:
                for b in range(2):
                    body(2 * j + b, b, j)
            for b in range(2):
                body(C - 2 + b, b, C // 2 - 1)

        def flat(tile):
            return tile[:, :, :, :].rearrange("p e t j -> p e (t j)")

        def is_first(n):
            return isinstance(n, int) and n < 2

        @block.sync
        def _(sp):
            for b in range(2):
                sp.dma_start(flat(lt[b]), view[0][b]).then_inc(l_loaded[b], DMA)
                sp.dma_start(flat(rt[b]), view[1][b]).then_inc(r_loaded[b], DMA)

            def body(n, b, j):
                more = not (isinstance(n, int) and n >= C - 2)
                if more:
                    sp.wait_ge(masked, n + 1)
                    sp.dma_start(flat(lt[b]), view[0][n + 2]).then_inc(l_loaded[b], DMA)
                    sp.wait_ge(summed, WT * n + WT)
                    sp.dma_start(flat(rt[b]), view[1][n + 2]).then_inc(r_loaded[b], DMA)
                sp.wait_ge(out_dve, 2 * n + 2)
                sp.wait_ge(out_act, 2 * n + 2)
                sp.dma_start(view[2][n], flat(om[b])).then_inc(stored[b], DMA)

            channels(sp, body)
            for b in range(2):
                sp.wait_ge(stored[b], DMA * (C // 2))

        @block.tensor
        def _(pe):
            def body(n, b, j):
                pe.wait_ge(r_loaded[b], DMA * j + DMA)
                pe.wait_ge(masked, n + 1)
                for i in range(WT):
                    if not is_first(n):
                        pe.wait_ge(out_dve if i % 2 == 0 else out_act, 2 * n - 3 + i // 2)
                    for k in range(WT):
                        last = pe.matmul(acc[b][i].rearrange("p (e j) -> p e j", e=2),
                                         rt[b][:, i % 2, k, i // 2:H:2], lm[b][:, :, k, :],
                                         start=(k == 0), stop=(k == WT - 1))
                    last.then_inc(summed, 1)

            channels(pe, body)

        @block.scalar
        def _(act):
            def mask(n, b, j):
                act.wait_ge(l_loaded[b], DMA * j + DMA)
                if not is_first(n):
                    act.wait_ge(summed, WT * n - WT)
                for k in range(WT):
                    last = act.activation(lm[b][:, :, k, :], lt[b][:, :, k, :], ACT.Copy, scale=keep.mask_sq[:, k:k + 1])
                last.then_inc(masked, 1)

            mask(0, 0, 0)

            def body(n, b, j):
                if not (isinstance(n, int) and n == C - 1):
                    mask(n + 1, 1 - b, j + b)
                if not is_first(n):
                    act.wait_ge(stored[b], DMA * j)
                for i in (1, 3):
                    act.wait_ge(summed, WT * n + i + 1)
                    act.activation(om[b][:, :, i, :], acc[b][i].rearrange("p (e j) -> p e j", e=2), ACT.Copy).then_inc(out_act, 1)

            channels(act, body)

        @block.vector
        def _(dve):
            def body(n, b, j):
                if not is_first(n):
                    dve.wait_ge(stored[b], DMA * j)
                for i in (0, 2):
                    dve.wait_ge(summed, WT * n + i + 1)
                    dve.tensor_copy(om[b][:, :, i, :], acc[b][i].rearrange("p (e j) -> p e j", e=2)).then_inc(out_dve, 1)

            channels(dve, body)




def finish_layer0(nc, x, mixed_d, gate_d, x1_d, fourier_d, keep):
    with ExitStack() as ctx:
        t = Tools(nc, ctx, "fi")
        xt = [t.sb(f"x{b}", [P, TR, WT, C]) for b in range(2)]
        x1 = [t.sb(f"x1{b}", [P, TR, WT, C]) for b in range(2)]
        gt = [t.sb(f"g{b}", [P, TR, WT, C]) for b in range(2)]
        mt = [t.sb(f"m{b}", [P, TR, H]) for b in range(2)]
        mt_sq = t.sb("m_sq", [P, TR, H])
        yt = [t.sb(f"y{b}", [P, TR, WT, C]) for b in range(2)]
        x1_sq = t.sb("x1_sq", [P, TR, WT, C])
        four = [t.sb(f"four{b}", [M2, TR, C]) for b in range(2)]
        st = t.sb("st", [P, 64])
        mean_sq = t.sb("mean_sq", [P, 32])
        var = t.sb("var", [P, 32])
        var_m = t.sb("var_m", [P, 32])
        var_eps = t.sb("var_eps", [P, 32])
        power = t.sb("power", [P, 32])
        rs = t.sb("rs", [P, 32])
        scale = [t.sb(f"scale{b}", [P, 32]) for b in range(2)]
        y_ps = [t.ps(f"y{k}", [P, L]) for k in range(2)]
        st_ps = t.ps("st", [P, 512])
        f_ps = t.ps("f", [M2, TR * C])
        ss_ps = t.ps("ss", [P, 512])

        m_loaded = [t.sem(f"m_loaded{b}") for b in range(2)]
        x_loaded = [t.sem(f"x_loaded{b}") for b in range(2)]
        g_loaded = [t.sem(f"g_loaded{b}") for b in range(2)]
        x1_stored = [t.sem(f"x1_stored{b}") for b in range(2)]
        f_stored = [t.sem(f"f_stored{b}") for b in range(2)]
        sq_ready = t.sem("sq_ready")
        st_ready = t.sem("st_ready")
        small = t.sem("small")
        power_set = t.sem("power_set")
        rs_ready = t.sem("rs_ready")
        y_ready = t.sem("y_ready")
        y_scaled = t.sem("y_scaled")
        y_shifted = t.sem("y_shifted")
        y_gated = t.sem("y_gated")
        x1_ready = t.sem("x1_ready")
        x1_sq_ready = t.sem("x1_sq_ready")
        f_ready = t.sem("f_ready")
        f_copied = t.sem("f_copied")
        ss_done = t.sem("ss_done")
        ss_copied = t.sem("ss_copied")

        x_v = x.rearrange("a (n r) (p t) c -> (a n) p r t c", r=TR, t=WT)
        x1_v = x1_d.rearrange("(n r) (p t) c -> n p r t c", r=TR, t=WT)
        g_v = gate_d.rearrange("(n r) (p t) c -> n p r t c", r=TR, t=WT)
        m_v = mixed_d.rearrange("e d (n r) j -> n (e d) r j", r=TR)
        f_v = fourier_d.rearrange("m (n r) c -> n m r c", r=TR)
        block = ctx.enter_context(nc.Block())

        def tiles(eng, body):
            for n in range(4):
                body(n, n % 2, n // 2)
            with eng.Fori(2, NT // 2 - 1) as j:
                for b in range(2):
                    body(2 * j + b, b, j)
            for b in range(2):
                body(NT - 2 + b, b, NT // 2 - 1)

        def is_first(n):
            return isinstance(n, int) and n < 2

        def is_zero(n):
            return isinstance(n, int) and n == 0

        def has_next(n):
            return not (isinstance(n, int) and n == NT - 1)

        @block.sync
        def _(sp):
            def load_mixed(n, b):
                sp.dma_start(mt[b][:, :, :], m_v[n]).then_inc(m_loaded[b], DMA)

            def load_rest(n, b):
                sp.dma_start(gt[b][:, :, :, :], g_v[n]).then_inc(g_loaded[b], DMA)
                sp.dma_start(xt[b][:, :, :, :], x_v[n]).then_inc(x_loaded[b], DMA)

            for b in range(2):
                load_mixed(b, b)
                load_rest(b, b)

            def stores(n, b, load):
                sp.wait_ge(x1_ready, n + 1)
                if load:
                    load_rest(n + 2, b)
                sp.dma_start(x1_v[n], x1[b][:, :, :, :]).then_inc(x1_stored[b], DMA)

            def store_rows(n, b):
                sp.wait_ge(f_copied, n + 1)
                sp.dma_start(f_v[n], four[b][:, :, :]).then_inc(f_stored[b], DMA)

            def body(n, b, j):
                if not (isinstance(n, int) and n >= NT - 2):
                    sp.wait_ge(y_ready, UN * n + UN)
                    load_mixed(n + 2, b)
                if not is_zero(n):
                    stores(n - 1, 1 - b, load=not (isinstance(n, int) and n >= NT - 1))
                if not is_first(n):
                    store_rows(n - 2, b)

            tiles(sp, body)
            stores(NT - 1, 1, load=False)
            for n in range(NT - 2, NT):
                store_rows(n, n % 2)
            for b in range(2):
                sp.wait_ge(x1_stored[b], DMA * (NT // 2))
                sp.wait_ge(f_stored[b], DMA * (NT // 2))

        @block.tensor
        def _(pe):
            def statistics(n, b, j):
                pe.wait_ge(m_loaded[b], DMA * j + DMA)
                pe.wait_ge(sq_ready, n + 1)
                if not is_zero(n):
                    pe.wait_ge(small, 5 * n - 4)
                for r in range(TR):
                    for k in range(2):
                        c = WT * r + 2 * k
                        pe.matmul(st_ps[:, c:c + 2], mt[b][:, r, k:H:2], keep.average[:, :], start=True, stop=True)
                        last = pe.matmul(st_ps[:, 32 + c:34 + c], mt_sq[:, r, k:H:2], keep.average[:, :],
                                         start=True, stop=True)
                last.then_inc(st_ready, 1)

            def output(n, q, b):
                if not (is_zero(n) and q < 2):
                    pe.wait_ge(y_scaled, UN * n + q - 1)
                for k in range(WT):
                    last = pe.matmul(y_ps[q % 2][:, P * k:P * k + P], mt[b][:, 2 * q + k // 2, k % 2:H:2], keep.w2_bd[:, :],
                                     start=True, stop=True)
                last.then_inc(y_ready, 1)

            def transform(n, b):
                pe.wait_ge(x1_ready, n + 1)
                if not is_zero(n):
                    pe.wait_ge(f_copied, n)
                for k in range(WT):
                    last = pe.matmul(f_ps[:, :].rearrange("m (r c) -> m r c", c=C), keep.basis[:, k, :],
                                     x1[b][:, :, k, :], start=(k == 0), stop=(k == WT - 1))
                last.then_inc(f_ready, 1)
                pe.wait_ge(x1_sq_ready, n + 1)
                for r in range(TR):
                    for k in range(0, WT, 2):
                        first = is_zero(n) and r == 0 and k == 0
                        final = isinstance(n, int) and n == NT - 1 and r == TR - 1 and k == WT - 2
                        last = pe.matmul(ss_ps[:, 0:1], x1_sq[:, r, k:k + 2, :].rearrange("p t c -> p (t c)"), keep.ones_col[:, 0:1],
                                         start=first, stop=final, skip_group_check=True)
                last.then_inc(ss_done, 1)

            statistics(0, 0, 0)

            def body(n, b, j):
                output(n, 0, b)
                output(n, 1, b)
                if has_next(n):
                    statistics(n + 1, 1 - b, j + b)
                output(n, 2, b)
                output(n, 3, b)
                if not is_first(n):
                    transform(n - 2, b)

            tiles(pe, body)
            for n in range(NT - 2, NT):
                transform(n, n % 2)

        @block.scalar
        def _(act):
            def square(n, b, j):
                act.wait_ge(m_loaded[b], DMA * j + DMA)
                if not is_zero(n):
                    act.wait_ge(st_ready, n)
                act.activation(mt_sq[:, :, :], mt[b][:, :, :], ACT.Square).then_inc(sq_ready, 1)

            def result(n, b, j):
                act.wait_ge(x1_ready, n + 1)
                if not is_zero(n):
                    act.wait_ge(ss_done, n)
                act.activation(x1_sq[:, :, :, :], x1[b][:, :, :, :], ACT.Square).then_inc(x1_sq_ready, 1)
                act.wait_ge(f_ready, n + 1)
                if not is_first(n):
                    act.wait_ge(f_stored[b], DMA * j)
                act.activation(four[b][:, :, :], f_ps[:, :].rearrange("m (r c) -> m r c", c=C),
                               ACT.Copy).then_inc(f_copied, 1)

            square(0, 0, 0)

            def body(n, b, j):
                if has_next(n):
                    square(n + 1, 1 - b, j + b)
                if not is_first(n):
                    result(n - 2, b, j - 1)

            tiles(act, body)
            for n in range(NT - 2, NT):
                result(n, n % 2, NT // 2 - 1)

        @block.gpsimd
        def _(pool):
            pool.memset(power[:, :], -0.5).then_inc(power_set, 1)
            pool.wait_ge(power_set, 1)

            def token_scale(n, b):
                pool.wait_ge(small, 5 * n + 5)
                pool.tensor_tensor(rs[:, :], var_eps[:, :], power[:, :], ALU.pow).then_inc(rs_ready, 1)
                pool.wait_ge(rs_ready, 2 * n + 1)
                if not is_first(n):
                    pool.wait_ge(y_scaled, UN * n - UN)
                pool.tensor_tensor(scale[b][:, :], rs[:, :], keep.mask_tok[:, bass.ts(n, 32)],
                                   ALU.mult).then_inc(rs_ready, 1)

            token_scale(0, 0)

            def body(n, b, j):
                if has_next(n):
                    token_scale(n + 1, 1 - b)
                pool.wait_ge(y_scaled, UN * n + UN)
                y3 = yt[b][:, :, :, :].rearrange("p r t c -> p (r t) c")
                pool.tensor_tensor(y3, y3, keep.c_row[:, :].unsqueeze(1).to_broadcast([P, TR * WT, C]),
                                   ALU.add).then_inc(y_shifted, 1)

            tiles(pool, body)

        @block.vector
        def _(dve):
            def small_chain(n):
                dve.wait_ge(st_ready, n + 1)
                if not is_zero(n):
                    dve.wait_ge(rs_ready, 2 * n)
                dve.tensor_copy(st[:, :], st_ps[:, 0:64]).then_inc(small, 1)
                dve.wait_ge(small, 5 * n + 1)
                dve.tensor_tensor(mean_sq[:, :], st[:, 0:32], st[:, 0:32], ALU.mult).then_inc(small, 1)
                dve.wait_ge(small, 5 * n + 2)
                dve.tensor_tensor(var[:, :], st[:, 32:64], mean_sq[:, :], ALU.subtract).then_inc(small, 1)
                dve.wait_ge(small, 5 * n + 3)
                dve.scalar_tensor_tensor(out=var_m[:, :], in0=var[:, :], scalar=0.0,
                                         in1=keep.mask_tok_sq[:, bass.ts(n, 32)], op0=ALU.max,
                                         op1=ALU.mult).then_inc(small, 1)
                dve.wait_ge(small, 5 * n + 4)
                dve.tensor_scalar(var_eps[:, :], var_m[:, :], EPS, None, ALU.add).then_inc(small, 1)

            def scaled(n, q, b):
                dve.wait_ge(y_ready, UN * n + q + 1)
                if q == 0:
                    dve.wait_ge(rs_ready, 2 * n + 2)
                    if not is_first(n):
                        dve.wait_ge(x1_ready, n - 1)
                dve.tensor_tensor(yt[b][:, 2 * q:2 * q + 2, :, :].rearrange("p r t c -> p (r t) c"),
                                  y_ps[q % 2].rearrange("p (t c) -> p t c", c=C),
                                  scale[b][:, 2 * WT * q:2 * WT * q + 2 * WT].unsqueeze(2).to_broadcast([P, 2 * WT, C]),
                                  ALU.mult).then_inc(y_scaled, 1)

            def finish(n, b, j):
                dve.wait_ge(y_shifted, n + 1)
                dve.wait_ge(g_loaded[b], DMA * j + DMA)
                dve.tensor_tensor(yt[b][:, :, :, :], yt[b][:, :, :, :], gt[b][:, :, :, :],
                                  ALU.mult).then_inc(y_gated, 1)
                dve.wait_ge(y_gated, n + 1)
                dve.wait_ge(x_loaded[b], DMA * j + DMA)
                if not is_first(n):
                    dve.wait_ge(x1_stored[b], DMA * j)
                    dve.wait_ge(x1_sq_ready, n - 1)
                    dve.wait_ge(f_ready, n - 1)
                dve.tensor_tensor(x1[b][:, :, :, :], yt[b][:, :, :, :], xt[b][:, :, :, :],
                                  ALU.add).then_inc(x1_ready, 1)

            small_chain(0)

            def body(n, b, j):
                scaled(n, 0, b)
                scaled(n, 1, b)
                if has_next(n):
                    small_chain(n + 1)
                scaled(n, 2, b)
                scaled(n, 3, b)
                if not is_zero(n):
                    finish(n - 1, 1 - b, j - 1 + b)

            tiles(dve, body)
            finish(NT - 1, 1, NT // 2 - 1)
            dve.wait_ge(ss_done, NT)
            dve.tensor_copy(keep.sum_sq[:, :], ss_ps[:, 0:1]).then_inc(ss_copied, 1)




def spectral(nc, fourier_d, w_real, w_imag, keep):
    with ExitStack() as ctx:
        t = Tools(nc, ctx, "sp")
        rows = t.sb("rows", [P, M2, WT, C])
        w = t.sb("w", [P, C, MODES, MODES])
        four = t.sb("four", [C, M2, M2])
        xr = t.sb("xr", [C, MODES, MODES])
        xi = t.sb("xi", [C, MODES, MODES])
        xm = t.sb("xm", [P, MODES * MODES, 2])
        mean_in = t.sb("mean_in", [C, 1])
        sq_in = t.sb("sq_in", [P, 1])
        sums = t.sb("sums", [C, 2])
        v = t.sb("v", [C, 8])
        root = t.sb("root", [C, 1])
        fold = t.sb("fold", [P, C])
        z = t.sb("z", [C, MODES * MODES, 2])
        q = t.sb("q", [C, M2, M2])
        f_ps = t.ps("f", [C, 2, 512])
        s_ps = t.ps("s", [C, 512])
        z_ps = t.ps("z", [C, MODES * MODES, 2])
        q_ps = t.ps("q", [M2, 3, 8, C])
        loaded = t.sem("loaded")
        step = t.sem("step")
        f_ready = t.sem("f_ready")
        sums_in = t.sem("sums_in")
        sums_ready = t.sem("sums_ready")
        root_in = t.sem("root_in")
        root_ready = t.sem("root_ready")
        x_ready = t.sem("x_ready")
        z_ready = t.sem("z_ready")
        q_in = t.sem("q_in")
        q_ready = t.sem("q_ready")
        block = ctx.enter_context(nc.Block())
        NM = MODES

        @block.sync
        def _(sp):
            sp.dma_start(rows[:, :, :, :], fourier_d.rearrange("m (p t) c -> p m t c", t=WT)).then_inc(loaded, DMA)
            sp.dma_start(w[0:C, :, :, :], w_real).then_inc(loaded, DMA)
            sp.dma_start(w[C:P, :, :, :], w_imag).then_inc(loaded, DMA)
            for h in range(2):
                sp.dma_start(fold[h * C:(h + 1) * C, :], keep.pair_d).then_inc(loaded, DMA)

        @block.tensor
        def _(pe):
            pe.wait_ge(loaded, 5 * DMA)
            for n in range(M2):
                for k in range(WT):
                    last = pe.matmul(f_ps[:, n // NM, M2 * (n % NM):M2 * (n % NM) + M2],
                                     rows[:, n, k, :],
                                     keep.basis[:, k, :], start=(k == 0), stop=(k == WT - 1))
            last.then_inc(f_ready, 1)
            pe.wait_ge(sums_in, 1)
            pe.matmul(s_ps[:, 0:1], fold[0:C, :], mean_in[:, :], start=True, stop=True)
            pe.matmul(s_ps[:, 1:2], fold[:, :], sq_in[:, :], start=True, stop=True).then_inc(sums_ready, 1)
            pe.wait_ge(x_ready, 1)
            for n in range(NM):
                for m in range(NM):
                    last = pe.matmul(z_ps[:, n * NM + m, :], w[:, :, m, n], xm[:, n * NM + m, :],
                                     start=True, stop=True)
            last.then_inc(z_ready, 1)
            pe.wait_ge(q_in, 1)
            for n in range(M2):
                last = pe.transpose(q_ps[:, n // 8, n % 8, :], q[:, n, :], keep.ident[0:C, 0:C])
            last.then_inc(q_ready, 1)

        @block.scalar
        def _(act):
            act.wait_ge(root_in, 1)
            act.activation(root[:, :], v[:, 5:6], ACT.Sqrt).then_inc(root_ready, 1)

        @block.vector
        def _(dve):
            link = chained(dve, step)
            dve.wait_ge(f_ready, 1)
            link(dve.tensor_copy(four[:, :, :].rearrange("p (a n) m -> p a (n m)", a=2), f_ps[:, :, 0:NM * M2]))
            dve.tensor_tensor(xr[:, :, :], four[:, 0:NM, 0:NM], four[:, NM:M2, NM:M2], ALU.subtract)
            dve.tensor_tensor(xi[:, :, :], four[:, 0:NM, NM:M2], four[:, NM:M2, 0:NM], ALU.add)
            dve.tensor_scalar(mean_in[:, :], four[:, 0, 0:1], 1.0 / TOK, None, ALU.mult)
            dve.tensor_scalar(sq_in[:, :], keep.sum_sq[:, :], 1.0 / TOK, None, ALU.mult).then_inc(sums_in, 1)
            dve.wait_ge(sums_ready, 1)
            link(dve.tensor_copy(sums[:, :], s_ps[:, 0:2]))
            link(dve.tensor_tensor(v[:, 0:1], sums[:, 0:1], sums[:, 0:1], ALU.mult))
            link(dve.tensor_tensor(v[:, 1:2], sums[:, 1:2], v[:, 0:1], ALU.subtract))
            dve.tensor_scalar(v[:, 5:6], v[:, 1:2], 0.0, EPS, ALU.max, ALU.add).then_inc(root_in, 1)
            link(dve.tensor_scalar(v[:, 2:3], sums[:, 0:1], float(TOK), None, ALU.mult))
            dve.wait_ge(root_ready, 1)
            link(dve.reciprocal(v[:, 3:4], root[:, :]))
            link(dve.tensor_tensor(xr[:, 0, 0:1], xr[:, 0, 0:1], v[:, 2:3], ALU.subtract))
            link(dve.tensor_scalar(v[:, 4:5], v[:, 3:4], -1.0, None, ALU.mult))
            xr_f = xr[:, :, :].rearrange("p n m -> p (n m)")
            xi_f = xi[:, :, :].rearrange("p n m -> p (n m)")
            dve.tensor_scalar(xm[0:C, :, 0], xr_f, v[:, 3:4], None, ALU.mult)
            dve.tensor_scalar(xm[0:C, :, 1], xi_f, v[:, 4:5], None, ALU.mult)
            dve.tensor_scalar(xm[C:P, :, 0], xi_f, v[:, 3:4], None, ALU.mult)
            dve.tensor_scalar(xm[C:P, :, 1], xr_f, v[:, 3:4], None, ALU.mult).then_inc(x_ready, 1)
            dve.wait_ge(z_ready, 1)
            link(dve.tensor_copy(z[:, :, :], z_ps[:, :, :]))
            zr = z[:, :, 0].rearrange("o (n m) -> o n m", m=NM)
            zi = z[:, :, 1].rearrange("o (n m) -> o n m", m=NM)
            dve.tensor_copy(q[:, 0:NM, 0:NM], zr)
            dve.tensor_scalar(q[:, 0:NM, NM:M2], zi, -1.0, None, ALU.mult)
            dve.tensor_scalar(q[:, NM:M2, 0:NM], zi, -1.0, None, ALU.mult)
            dve.tensor_scalar(q[:, NM:M2, NM:M2], zr, -1.0, None, ALU.mult).then_inc(q_in, 1)
            dve.wait_ge(q_ready, 1)
            for a in range(3):
                dve.tensor_copy(keep.spectrum[:, :, 8 * a:8 * a + 8].rearrange("m o n -> m n o"), q_ps[:, a, :, :])




def finish_layer1(nc, x1_d, out, keep):
    with ExitStack() as ctx:
        t = Tools(nc, ctx, "la")
        col = t.sb("col", [P, L, C])
        xt = [t.sb(f"x{b}", [P, TR, WT, C]) for b in range(2)]
        yo = [t.sb(f"yo{b}", [P, TR, WT, C]) for b in range(2)]
        ps = [t.ps(f"ps{k}", [P, L]) for k in range(8)]
        loaded = [t.sem(f"loaded{b}") for b in range(2)]
        stored = [t.sem(f"stored{b}") for b in range(2)]
        col_zero = [t.sem(f"col_zero{h}") for h in range(2)]
        col_ready = t.sem("col_ready")
        col_dve = t.sem("col_dve")
        col_act = t.sem("col_act")
        y_ready = t.sem("y_ready")
        y_done = t.sem("y_done")
        x_v = x1_d.rearrange("(n r) (p t) c -> n p r t c", r=TR, t=WT)
        o_v = out.rearrange("a (n r) (p t) c -> (a n) p r t c", r=TR, t=WT)
        block = ctx.enter_context(nc.Block())

        def tiles(eng, body):
            for n in range(2):
                body(n, n, 0)
            with eng.Fori(1, NT // 2 - 1) as j:
                for b in range(2):
                    body(2 * j + b, b, j)
            for b in range(2):
                body(NT - 2 + b, b, NT // 2 - 1)

        def is_first(n):
            return isinstance(n, int) and n < 2

        @block.sync
        def _(sp):
            for b in range(2):
                sp.dma_start(xt[b][:, :, :, :], x_v[b]).then_inc(loaded[b], DMA)

            def body(n, b, j):
                sp.wait_ge(y_done, WT * n + WT)
                if not (isinstance(n, int) and n >= NT - 2):
                    sp.dma_start(xt[b][:, :, :, :], x_v[n + 2]).then_inc(loaded[b], DMA)
                sp.dma_start(o_v[n], yo[b][:, :, :, :]).then_inc(stored[b], DMA)

            tiles(sp, body)
            for b in range(2):
                sp.wait_ge(stored[b], DMA * (NT // 2))

        @block.tensor
        def _(pe):
            for o in range(C):
                if o >= 8:
                    pe.wait_ge(col_dve if o % 2 == 0 else col_act, (o - 8) // 2 + 1)
                pe.matmul(ps[o % 8][0:M2, :], keep.spectrum[:, o, :], keep.inverse[0:M2, :],
                          start=True, stop=True).then_inc(col_ready, 1)
            pe.wait_ge(col_dve, C // 2)
            pe.wait_ge(col_act, C // 2)

            def body(n, b, j):
                for k in range(WT):
                    if not is_first(n):
                        pe.wait_ge(y_done, WT * (n - 2) + k + 1)
                    pe.matmul(ps[WT * b + k][:, :], keep.inverse[:, k:L:WT],
                              col[:, bass.ts(n, TR), :].rearrange("m r c -> m (r c)"),
                              start=True, stop=True).then_inc(y_ready, 1)

            tiles(pe, body)

        @block.gpsimd
        def _(pool):
            pool.memset(col[:, 0:H, :], 0.0).then_inc(col_zero[0], 1)

        @block.scalar
        def _(act):
            act.wait_ge(col_zero[0], 1)
            act.wait_ge(col_zero[1], 1)
            for o in range(1, C, 2):
                act.wait_ge(col_ready, o + 1)
                act.activation(col[0:M2, :, o], ps[o % 8][0:M2, :], ACT.Copy).then_inc(col_act, 1)

        @block.vector
        def _(dve):
            dve.memset(col[:, H:L, :], 0.0).then_inc(col_zero[1], 1)
            dve.wait_ge(col_zero[0], 1)
            dve.wait_ge(col_zero[1], 1)
            for o in range(0, C, 2):
                dve.wait_ge(col_ready, o + 1)
                dve.tensor_copy(col[0:M2, :, o], ps[o % 8][0:M2, :]).then_inc(col_dve, 1)

            def body(n, b, j):
                dve.wait_ge(loaded[b], DMA * j + DMA)
                if not is_first(n):
                    dve.wait_ge(stored[b], DMA * j)
                for k in range(WT):
                    dve.wait_ge(y_ready, WT * n + k + 1)
                    dve.tensor_tensor(yo[b][:, :, k, :], ps[WT * b + k][:, :].rearrange("p (r c) -> p r c", c=C),
                                      xt[b][:, :, k, :], ALU.add).then_inc(y_done, 1)

            tiles(dve, body)


class Keep:
    pass


def program(nc, ins, tab, out):
    x = ins["x"]
    left_d = nc.dram_tensor("left_d", [2, C, L, H], F32, kind="Internal").ap()
    right_d = nc.dram_tensor("right_d", [2, C, L, H], F32, kind="Internal").ap()
    mixed_d = nc.dram_tensor("mixed_d", [2, C, L, H], F32, kind="Internal").ap()
    gate_d = nc.dram_tensor("gate_d", [L, L, C], F32, kind="Internal").ap()
    x1_d = nc.dram_tensor("x1_d", [L, L, C], F32, kind="Internal").ap()
    fourier_d = nc.dram_tensor("fourier_d", [M2, L, C], F32, kind="Internal").ap()
    with ExitStack() as ctx:
        t = Tools(nc, ctx, "keep")
        k = Keep()
        k.pair_d = tab["t_pair"]
        k.mean0 = t.sb("mean0", [P, G])
        k.var0 = t.sb("var0", [P, G])
        k.gn_scale = t.sb("gn_scale", [P, 1])
        k.gn_shift = t.sb("gn_shift", [P, 1])
        k.ident = t.sb("ident", [P, P])
        k.basis = t.sb("basis", [P, WT, M2])
        k.inverse = t.sb("inverse", [P, L])
        k.average = t.sb("average", [P, 2])
        k.pair = t.sb("pair", [C, C])
        k.select = t.sb("select", [3 * 8 * UN, UN * WT, P], BF16)
        k.w_bd = t.sb("w_bd", [P, 5, P])
        k.bias = t.sb("bias", [P, 4])
        k.w2_bd = t.sb("w2_bd", [P, P])
        k.c_row = t.sb("c_row", [P, C])
        k.gbias3 = t.sb("gbias3", [P, L], BF16)
        k.ones_bf = t.sb("ones_bf", [P, P], BF16)
        k.ones_col = t.sb("ones_col", [P, 1])
        k.mask_sq = t.sb("mask_sq", [P, WT])
        k.mask_tok = t.sb("mask_tok", [P, NT * 32])
        k.mask_tok_sq = t.sb("mask_tok_sq", [P, NT * 32])
        k.sum_sq = t.sb("sum_sq", [P, 1])
        k.spectrum = t.sb("spectrum", [M2, C, M2])
        statistics_of_x(nc, x, k)
        prepare(nc, ins, tab, k)
        project(nc, x, left_d, right_d, gate_d, k)
        contract(nc, left_d, right_d, mixed_d, k)
        finish_layer0(nc, x, mixed_d, gate_d, x1_d, fourier_d, k)
        spectral(nc, fourier_d, ins["L1_conv_w_real"], ins["L1_conv_w_imag"], k)
        finish_layer1(nc, x1_d, out, k)


def kernel(**inputs):
    import concourse.bacc as bacc
    from concourse.bass_utils import run_bass_kernel_spmd

    nc = bacc.Bacc("TRN2", target_bir_lowering=False, num_devices=1)
    arrays, ins, tab = {}, {}, {}
    for name, value in inputs.items():
        a = np.ascontiguousarray(value)
        arrays[f"in_{name}"] = a
        ins[name] = nc.dram_tensor(f"in_{name}", a.shape, mybir.dt.from_np(a.dtype), kind="ExternalInput").ap()
    for name, a in host_tables().items():
        a = np.ascontiguousarray(a)
        arrays[name] = a
        tab[name] = nc.dram_tensor(name, a.shape, mybir.dt.from_np(a.dtype), kind="ExternalInput").ap()
    out = nc.dram_tensor("out_0", (1, L, L, C), F32, kind="ExternalOutput").ap()
    program(nc, ins, tab, out)
    r = run_bass_kernel_spmd(nc, [arrays], core_ids=[0])
    return r.results[0]["out_0"]
```

```python
from contextlib import ExitStack

import numpy as np

import concourse.bass as bass
from concourse import mybir

F32 = mybir.dt.float32
F32R = mybir.dt.float32r
BF16 = mybir.dt.bfloat16
I32 = mybir.dt.int32
ALU = mybir.AluOpType
ACT = mybir.ActivationFunctionType
AX = mybir.AxisListType

P = 128
L = 512
C = 64
G = 32
CG = C // G
MODES = 12
M2 = 2 * MODES
TOK = L * L
TR = 8
NT = L // TR
UN = TR // 2
WT = L // P
H = L // 2
EPS = 1e-5
DMA = 16
STATS_T = 256
NCHUNK = TOK // (P * STATS_T)


def host_tables():
    pos = np.arange(L)[:, None] * np.arange(MODES)[None, :] * (2 * np.pi / L)
    fourier = np.concatenate([np.cos(pos), np.sin(pos)], axis=1)
    basis = fourier.reshape(P, WT, M2).astype(np.float32)
    inverse = np.zeros((P, L), np.float32)
    inverse[:M2] = fourier.T / L
    half = np.arange(P) // C
    same = (half[:, None] == half[None, :]).astype(np.float32)
    centre = (np.eye(P) - same / C).astype(np.float32)
    group = np.arange(C) // CG
    pair = (group[:, None] == group[None, :]).astype(np.float32) / CG
    return {
        "t_ident": np.eye(P, dtype=np.float32),
        "t_basis": basis,
        "t_inverse": inverse,
        "t_centre": centre,
        "t_pair": pair,
    }


class Tools:

    def __init__(self, nc, ctx, phase):
        self.nc, self.ctx, self.phase = nc, ctx, phase

    def sb(self, name, shape, dt=F32):
        return self.ctx.enter_context(self.nc.sbuf_tensor(f"{self.phase}_{name}", shape, dt))

    def ps(self, name, shape):
        n = int(np.prod(shape[1:]))
        banks = -(-n // 512)
        whole = self.ctx.enter_context(self.nc.psum_tensor(f"{self.phase}_{name}_ps", [shape[0], banks * 512], F32))
        view = whole[:, 0:n]
        if len(shape) == 2:
            return view
        names = "abcd"[:len(shape) - 1]
        return view.rearrange(f"p ({' '.join(names)}) -> p {' '.join(names)}", **dict(zip(names, shape[1:])))

    def sem(self, name):
        return self.ctx.enter_context(self.nc.semaphore(f"{self.phase}_{name}"))


def chained(eng, sem, start=0):
    n = [start]

    def link(instruction):
        n[0] += 1
        instruction.then_inc(sem, 1)
        eng.wait_ge(sem, n[0])

    return link




def statistics_of_x(nc, x, keep):
    with ExitStack() as ctx:
        t = Tools(nc, ctx, "st")
        xc = [t.sb(f"x{b}", [P, STATS_T, C]) for b in range(2)]
        stats = t.sb("stats", [P, G, NCHUNK, 6])
        part = t.sb("part", [P, G, 2])
        dev = t.sb("dev", [P, G])
        sq = t.sb("sq", [P, G])
        spread = t.sb("spread", [P, G])
        ones = t.sb("ones", [P, P])
        mean_ps = t.ps("mean", [P, 512])
        var_ps = t.ps("var", [P, 512])
        loaded = [t.sem(f"loaded{b}") for b in range(2)]
        ones_set = t.sem("ones_set")
        chunk_done = t.sem("chunk_done")
        step = t.sem("step")
        mean_ready = t.sem("mean_ready")
        var_ready = t.sem("var_ready")
        spread_ready = t.sem("spread_ready")
        x_v = x.rearrange("a h w c -> (a h w c)").rearrange("(n p t c) -> n p t c", p=P, t=STATS_T, c=C)
        block = ctx.enter_context(nc.Block())

        @block.sync
        def _(sp):
            for b in range(2):
                sp.dma_start(xc[b][:, :, :], x_v[b]).then_inc(loaded[b], DMA)
            with sp.Fori(1, NCHUNK // 2) as j:
                for b in range(2):
                    sp.wait_ge(chunk_done, 2 * j + b - 1)
                    sp.dma_start(xc[b][:, :, :], x_v[2 * j + b]).then_inc(loaded[b], DMA)

        @block.vector
        def _(dve):
            with dve.Fori(0, NCHUNK // 2) as j:
                for b in range(2):
                    dve.wait_ge(loaded[b], DMA * j + DMA)
                    for g in range(G):
                        last = dve.bn_stats(stats[:, g, 2 * j + b, :], xc[b][:, :, CG * g:CG * g + CG])
                    last.then_inc(chunk_done, 1)
            link = chained(dve, step)
            dve.wait_ge(chunk_done, NCHUNK)
            for g in range(G):
                last = dve.bn_aggr(part[:, g, :], stats[:, g, :, :].rearrange("p n s -> p (n s)"))
            link(last)
            dve.tensor_copy(dev[:, :], part[:, :, 0]).then_inc(spread_ready, 1)
            dve.wait_ge(mean_ready, 1)
            link(dve.tensor_copy(keep.mean0[:, :], mean_ps[:, 0:G]))
            link(dve.tensor_tensor(sq[:, :], part[:, :, 0], keep.mean0[:, :], ALU.subtract))
            link(dve.tensor_tensor(spread[:, :], sq[:, :], sq[:, :], ALU.mult))
            dve.tensor_tensor(spread[:, :], spread[:, :], part[:, :, 1], ALU.add).then_inc(spread_ready, 1)
            dve.wait_ge(var_ready, 1)
            dve.tensor_copy(keep.var0[:, :], var_ps[:, 0:G]).then_inc(step, 1)

        @block.gpsimd
        def _(pool):
            pool.memset(ones[:, :], 1.0 / P).then_inc(ones_set, 1)

        @block.tensor
        def _(pe):
            pe.wait_ge(ones_set, 1)
            pe.wait_ge(spread_ready, 1)
            pe.matmul(mean_ps[:, 0:G], ones[:, :], dev[:, :], start=True, stop=True).then_inc(mean_ready, 1)
            pe.wait_ge(spread_ready, 2)
            pe.matmul(var_ps[:, 0:G], ones[:, :], spread[:, :], start=True, stop=True).then_inc(var_ready, 1)




def prepare(nc, ins, tab, keep):
    with ExitStack() as ctx:
        t = Tools(nc, ctx, "pr")
        names = ["left", "lgate", "right", "rgate", "ogate"]
        w_raw = t.sb("w_raw", [P, 5, C])
        w_scaled = t.sb("w_scaled", [P, 5, C])
        w_raw_bd = t.sb("w_raw_bd", [P, 4, P])
        w_bd = t.sb("w_bd", [P, 5, P])
        nw = t.sb("nw", [P, 1])
        nb = t.sb("nb", [P, 1])
        bias_in = t.sb("bias_in", [P, 4])
        centre = t.sb("centre", [P, P])
        onw = t.sb("onw", [P, 1])
        onb = t.sb("onb", [C, 1])
        ow = t.sb("ow", [P, C])
        ow_scaled = t.sb("ow_scaled", [P, C])
        onb_wide = t.sb("onb_wide", [C, P])
        row_in = t.sb("row_in", [1, 2, C])
        grow = t.sb("grow", [1, 3, C])
        ghi = t.sb("ghi", [1, 2, C])
        ones_row = t.sb("ones_row", [1, P])
        mask_col = t.sb("mask_col", [P, WT], I32)
        mask_row = t.sb("mask_row", [1, L], I32)
        maskf_col = t.sb("maskf_col", [P, WT])
        maskf_row = t.sb("maskf_row", [1, L])
        mask_wide = t.sb("mask_wide", [P, L])
        rstd = t.sb("rstd", [P, G])
        scale = t.sb("scale", [P, G])
        shift = t.sb("shift", [P, G])
        root = t.sb("root", [P, G])
        w_ps = t.ps("w", [P, 5, C])
        b_ps = t.ps("b", [P, 4])
        ow_ps = t.ps("ow", [P, C])
        c_ps = t.ps("c", [P, C])
        g_ps = t.ps("g", [1, C])
        m_ps = t.ps("m", [P, L])
        loaded = t.sem("loaded")
        step = t.sem("step")
        pool_set = t.sem("pool_set")
        raw_ready = t.sem("raw_ready")
        scaled_ready = t.sem("scaled_ready")
        row_ready = t.sem("row_ready")
        products = t.sem("products")
        root_in = t.sem("root_in")
        root_ready = t.sem("root_ready")
        loads = []
        for i, n in enumerate(names):
            for h in range(2):
                loads.append((w_raw[h * C:(h + 1) * C, i, :], ins[f"L0_conv_{n}_w"]))
        for h in range(2):
            rows = slice(h * C, (h + 1) * C)

            def col(v):
                return v.rearrange("(c o) -> c o", o=1)

            loads.append((nw[rows, :], col(ins["L0_conv_norm_w"])))
            loads.append((nb[rows, :], col(ins["L0_conv_norm_b"])))
            loads.append((onw[rows, :], col(ins["L0_conv_onorm_w"])))
            loads.append((ow[rows, :], ins["L0_conv_out_w"]))
            for i, n in enumerate(names[:4]):
                loads.append((bias_in[rows, i:i + 1], col(ins[f"L0_conv_{n}_b"])))
        loads.append((onb[:, :], ins["L0_conv_onorm_b"].rearrange("(c o) -> c o", o=1)))
        loads.append((row_in[:, 0, :], ins["L0_conv_ogate_b"].rearrange("(o c) -> o c", o=1)))
        loads.append((row_in[:, 1, :], ins["L0_conv_out_b"].rearrange("(o c) -> o c", o=1)))
        loads.append((mask_col[:, :], ins["L0_conv_sequence_mask"].rearrange("a (p t) -> (a p) t", t=WT)))
        loads.append((mask_row[:, :], ins["L0_conv_sequence_mask"]))
        loads.append((centre[:, :], tab["t_centre"]))
        loads.append((keep.ident[:, :], tab["t_ident"]))
        loads.append((keep.basis[:, :, :], tab["t_basis"]))
        loads.append((keep.inverse[:, :], tab["t_inverse"]))
        loads.append((keep.pair[:, :], tab["t_pair"]))
        block = ctx.enter_context(nc.Block())

        @block.sync
        def _(sp):
            for dst, src in loads:
                sp.dma_start(dst, src).then_inc(loaded, DMA)

        @block.gpsimd
        def _(pool):
            pool.memset(w_raw_bd[:, :, :], 0.0).then_inc(pool_set, 1)
            pool.memset(w_bd[:, :, :], 0.0).then_inc(pool_set, 1)
            pool.memset(keep.w2_bd[:, :], 0.0).then_inc(pool_set, 1)
            pool.memset(keep.gbias3[:, :], 0.0).then_inc(pool_set, 1)
            pool.memset(keep.ones_bf[:, :], 1.0).then_inc(pool_set, 1)
            pool.memset(ones_row[:, :], 1.0).then_inc(pool_set, 1)
            pool.memset(keep.ones[:, :], 1.0).then_inc(pool_set, 1)

        @block.scalar
        def _(act):
            act.wait_ge(root_in, 1)
            act.activation(root[:, :], rstd[:, :], ACT.Sqrt).then_inc(root_ready, 1)

        @block.tensor
        def _(pe):
            pe.wait_ge(loaded, DMA * len(loads))
            pe.wait_ge(scaled_ready, 1)
            pe.matmul(w_ps[:, :, :], centre[:, :], w_scaled[:, :, :], start=True, stop=True)
            pe.matmul(ow_ps[:, :], centre[:, :], ow_scaled[:, :], start=True, stop=True)
            pe.wait_ge(raw_ready, 1)
            for i in range(4):
                pe.matmul(b_ps[:, i:i + 1], w_raw_bd[:, i, :], nb[:, :], start=True, stop=True)
            pe.matmul(g_ps[:, :], nb[0:C, :], w_raw[0:C, 4, :], start=True, stop=True)
            pe.wait_ge(pool_set, 7)
            pe.matmul(c_ps[:, :], onb_wide[:, :], ow[0:C, :], start=True, stop=False)
            pe.matmul(c_ps[:, :], ones_row[:, :], row_in[:, 1, :], start=False, stop=True)
            pe.wait_ge(row_ready, 1)
            pe.matmul(m_ps[:, :], ones_row[:, :], maskf_row[:, :], start=True, stop=True).then_inc(products, 1)

        @block.vector
        def _(dve):
            link = chained(dve, step)
            dve.wait_ge(loaded, DMA * len(loads))
            dve.wait_ge(pool_set, 7)
            dve.tensor_scalar(ow_scaled[:, :], ow[:, :], onw[:, 0:1], None, ALU.mult)
            dve.tensor_scalar(w_scaled[:, :, :], w_raw[:, :, :], nw[:, 0:1], None, ALU.mult).then_inc(scaled_ready, 1)
            for h in range(2):
                rows = slice(h * C, (h + 1) * C)
                dve.tensor_copy(w_raw_bd[rows, :, h * C:(h + 1) * C], w_raw[rows, 0:4, :])
            dve.tensor_copy(onb_wide[:, :], onb[:, :].to_broadcast([C, P])).then_inc(raw_ready, 1)
            dve.tensor_copy(maskf_row[:, :], mask_row[:, :]).then_inc(row_ready, 1)
            link(dve.tensor_copy(maskf_col[:, :], mask_col[:, :]))
            dve.tensor_tensor(keep.mask_sq[:, :], maskf_col[:, :], maskf_col[:, :], ALU.mult)
            dve.tensor_scalar(rstd[:, :], keep.var0[:, :], EPS, None, ALU.add).then_inc(root_in, 1)
            dve.wait_ge(root_ready, 1)
            link(dve.reciprocal(scale[:, :], root[:, :]))
            dve.tensor_copy(keep.gn_scale[:, :].rearrange("p (g e) -> p g e", e=CG),
                            scale[:, :].unsqueeze(2).to_broadcast([P, G, CG]))
            link(dve.scalar_tensor_tensor(out=shift[:, :], in0=keep.mean0[:, :], scalar=-1.0, in1=scale[:, :],
                                          op0=ALU.mult, op1=ALU.mult))
            dve.tensor_copy(keep.gn_shift[:, :].rearrange("p (g e) -> p g e", e=CG),
                            shift[:, :].unsqueeze(2).to_broadcast([P, G, CG]))
            dve.wait_ge(products, 1)
            for h in range(2):
                rows = slice(h * C, (h + 1) * C)
                dve.tensor_copy(w_bd[rows, :, h * C:(h + 1) * C], w_ps[rows, :, :])
                dve.tensor_copy(keep.w2_bd[rows, h * C:(h + 1) * C], ow_ps[rows, :])
            dve.tensor_tensor(keep.bias[:, :], b_ps[:, :], bias_in[:, :], ALU.add)
            dve.tensor_copy(keep.c_row[:, :], c_ps[:, :])
            link(dve.tensor_copy(mask_wide[:, :], m_ps[:, :]))
            link(dve.tensor_copy(keep.w_high[:, :, :], w_bd[:, :, :]))
            dve.tensor_tensor(keep.w_low[:, :, :], w_bd[:, :, :], keep.w_high[:, :, :], ALU.subtract)
            view = keep.mask_tok[:, :].rearrange("p (i t) -> p i t", t=WT)
            for k in range(WT):
                last = dve.tensor_scalar(view[:, :, k], mask_wide[:, :], maskf_col[:, k:k + 1], None, ALU.mult)
            link(last)
            dve.tensor_tensor(keep.mask_tok_sq[:, :], keep.mask_tok[:, :], keep.mask_tok[:, :], ALU.mult)
            link(dve.tensor_tensor(grow[:, 0, :], g_ps[:, :], row_in[:, 0, :], ALU.add))
            for k in range(3):
                row = keep.gbias3[32 * k:32 * k + 1, :].rearrange("p (n c) -> p n c", c=C)
                link(dve.tensor_copy(row, grow[:, k, :].unsqueeze(1).to_broadcast([1, 8, C])))
                if k < 2:
                    link(dve.tensor_copy(ghi[:, k, :], keep.gbias3[32 * k:32 * k + 1, 0:C]))
                    link(dve.tensor_tensor(grow[:, k + 1, :], grow[:, k, :], ghi[:, k, :], ALU.subtract))




def project(nc, x, left_d, right_d, gate_d, keep):
    HT = TR * WT // 2
    with ExitStack() as ctx:
        t = Tools(nc, ctx, "pj")
        xt = [t.sb(f"x{b}", [P, 2 * HT, C]) for b in range(2)]
        gn = [t.sb(f"gn{b}", [P, 2 * HT, C]) for b in range(2)]
        sq = t.sb("sq", [P, 2 * HT, C])
        xn = [t.sb(f"xn{b}", [P, 2 * HT, C]) for b in range(2)]
        high = [t.sb(f"high{b}", [P, L], F32R) for b in range(2)]
        low = [t.sb(f"low{b}", [P, L], F32R) for b in range(2)]
        sig = [t.sb(f"sig{b}", [P, L]) for b in range(2)]
        out = [[t.sb(f"out{s}{b}", [P, UN, L]) for b in range(2)] for s in range(2)]
        gout = [t.sb(f"gout{b}", [P, UN, L]) for b in range(2)]
        sums = t.sb("sums", [P, 2, HT])
        sums_sq = t.sb("sums_sq", [P, 2, HT])
        mean_sq = t.sb("mean_sq", [P, 2, HT])
        var = t.sb("var", [P, 2, HT])
        var_eps = t.sb("var_eps", [P, 2, HT])
        power = t.sb("power", [P, HT])
        rs = t.sb("rs", [P, 2, HT])
        x_ps = [t.ps(f"x{k}", [P, L]) for k in range(2)]
        proj_ps = [[t.ps(f"proj{s}{k}", [P, L]) for k in range(2)] for s in range(2)]
        g_ps = [t.ps(f"g{k}", [P, L]) for k in range(2)]

        x_loaded = [t.sem(f"x_loaded{b}") for b in range(2)]
        stored = [[t.sem(f"stored{s}{b}") for b in range(2)] for s in range(3)]
        gn_scaled = t.sem("gn_scaled")
        gn_ready = t.sem("gn_ready")
        sq_ready = t.sem("sq_ready")
        small = t.sem("small")
        power_set = t.sem("power_set")
        rs_ready = t.sem("rs_ready")
        xn_ready = t.sem("xn_ready")
        xt_ready = t.sem("xt_ready")
        high_ready = t.sem("high_ready")
        low_ready = t.sem("low_ready")
        gate_ready = [t.sem(f"gate_ready{s}") for s in range(2)]
        val_ready = [t.sem(f"val_ready{s}") for s in range(2)]
        sig_ready = [t.sem(f"sig_ready{s}") for s in range(2)]
        gated = [t.sem(f"gated{s}") for s in range(2)]
        g_ready = t.sem("g_ready")
        g_done = t.sem("g_done")

        x_v = x.rearrange("a (n r) (p t) c -> (a n) p r t c", r=TR, t=WT)
        side_v = [d.rearrange("e d (n r) j -> n (e d) (r j)", r=TR) for d in (left_d, right_d)]
        gate_v = gate_d.rearrange("(n r) (p t) c -> n p r t c", r=TR, t=WT)
        block = ctx.enter_context(nc.Block())

        def tiles(eng, body):
            for n in range(2):
                body(n, n, 0)
            with eng.Fori(1, NT // 2 - 1) as j:
                for b in range(2):
                    body(2 * j + b, b, j)
            for b in range(2):
                body(NT - 2 + b, b, NT // 2 - 1)

        def is_first(n):
            return isinstance(n, int) and n < 2

        def is_zero(n):
            return isinstance(n, int) and n == 0

        def has_next(n, ahead=1):
            return not (isinstance(n, int) and n + ahead >= NT)

        def by_token(tile):
            return tile[:, :, :].rearrange("p (r t) c -> p r t c", t=WT)

        def half(tile, h):
            return tile[:, HT * h:HT * h + HT, :]

        @block.sync
        def _(sp):
            for b in range(2):
                sp.dma_start(by_token(xt[b]), x_v[b]).then_inc(x_loaded[b], DMA)

            def load(n, b):
                sp.wait_ge(gn_scaled, 2 * n - 2)
                sp.dma_start(by_token(xt[b]), x_v[n]).then_inc(x_loaded[b], DMA)

            load(2, 0)

            def body(n, b, j):
                if has_next(n, 3):
                    load(n + 3, 1 - b)
                for s in range(2):
                    sp.wait_ge(gated[s], UN * n + UN)
                    sp.dma_start(side_v[s][n], out[s][b][:, :, :].rearrange("p q j -> p (q j)")).then_inc(stored[s][b], DMA)
                sp.wait_ge(g_done, UN * n + UN)
                sp.dma_start(gate_v[n], gout[b][:, :, :].rearrange("p q (r t c) -> p (q r) t c", r=2, t=WT)
                             ).then_inc(stored[2][b], DMA)

            for n in range(2):
                body(n, n, 0)
            with sp.Fori(1, NT // 2 - 2) as j:
                for b in range(2):
                    body(2 * j + b, b, j)
            for n in range(NT - 4, NT):
                body(n, n % 2, n // 2)
            for b in range(2):
                for s in range(3):
                    sp.wait_ge(stored[s][b], DMA * (NT // 2))

        @block.gpsimd
        def _(pool):
            pool.memset(power[:, :], -0.5).then_inc(power_set, 1)
            pool.wait_ge(power_set, 1)

            def scale(n, b, j):
                pool.wait_ge(x_loaded[b], DMA * j + DMA)
                if not is_first(n):
                    pool.wait_ge(xn_ready, UN * n - UN)
                for h in range(2):
                    pool.tensor_tensor(half(gn[b], h), half(xt[b], h),
                                       keep.gn_scale[:, :].unsqueeze(1).to_broadcast([P, HT, C]),
                                       ALU.mult).then_inc(gn_scaled, 1)

            def shift(n, b):
                for h in range(2):
                    pool.wait_ge(gn_scaled, 2 * n + h + 1)
                    pool.tensor_tensor(half(gn[b], h), half(gn[b], h),
                                       keep.gn_shift[:, :].unsqueeze(1).to_broadcast([P, HT, C]),
                                       ALU.add).then_inc(gn_ready, 1)

            def root(n):
                for h in range(2):
                    pool.wait_ge(small, 10 * n + 5 * h + 5)
                    if not is_zero(n):
                        pool.wait_ge(xn_ready, UN * n - UN + 2 * h + 2)
                    pool.tensor_tensor(rs[:, h, :], var_eps[:, h, :], power[:, :], ALU.pow).then_inc(rs_ready, 1)

            scale(0, 0, 0)
            shift(0, 0)
            scale(1, 1, 0)
            root(0)
            shift(1, 1)

            def body(n, b, j):
                if has_next(n, 2):
                    scale(n + 2, b, j + 1)
                if has_next(n):
                    root(n + 1)
                if has_next(n, 2):
                    shift(n + 2, b)

            tiles(pool, body)

        @block.tensor
        def _(pe):
            def transposes(n, q, b):
                pe.wait_ge(xn_ready, UN * n + q + 1)
                if not (is_zero(n) and q < 2):
                    pe.wait_ge(low_ready, UN * n + q - 1)
                for r in range(2):
                    for k in range(2):
                        at = 2 * WT * q + WT * r + 2 * k
                        last = pe.transpose(x_ps[q % 2][:, H * r + k:H * r + H:2],
                                            xn[b][:, at:at + 2, :].rearrange("p t c -> p (t c)"),
                                            keep.ident[:, :])
                last.then_inc(xt_ready, 1)

            def product(bank, i, q):
                pe.matmul(bank[:, :], keep.w_high[:, i, :], high[q % 2][:, :], start=True, stop=False)
                pe.matmul(bank[:, :], keep.w_high[:, i, :], low[q % 2][:, :], start=False, stop=False)
                return pe.matmul(bank[:, :], keep.w_low[:, i, :], high[q % 2][:, :], start=False, stop=True)

            def side(n, q, s):
                if s == 0:
                    pe.wait_ge(high_ready, UN * n + q + 1)
                    pe.wait_ge(low_ready, UN * n + q + 1)
                if not (is_zero(n) and q == 0):
                    pe.wait_ge(gated[s], UN * n + q)
                product(proj_ps[s][1], 2 * s + 1, q).then_inc(gate_ready[s], 1)
                product(proj_ps[s][0], 2 * s, q).then_inc(val_ready[s], 1)

            def output_gate(n, q):
                if not (is_zero(n) and q < 2):
                    pe.wait_ge(g_done, UN * n + q - 1)
                bank = g_ps[q % 2]
                pe.matmul(bank[:, :], keep.ones_bf[:, :], keep.gbias3[:, :], start=True, stop=False)
                for k in range(WT):
                    at = H * (k // 2) + k % 2
                    cols = slice(at, at + H - 1, 2)
                    block_k = bank[:, P * k:P * k + P]
                    pe.matmul(block_k, high[q % 2][:, cols], keep.w_high[:, 4, :], start=False, stop=False)
                    pe.matmul(block_k, high[q % 2][:, cols], keep.w_low[:, 4, :], start=False, stop=False)
                    last = pe.matmul(block_k, low[q % 2][:, cols], keep.w_high[:, 4, :], start=False,
                                     stop=(k == WT - 1))
                last.then_inc(g_ready, 1)

            transposes(0, 0, 0)

            def body(n, b, j):
                for q in range(UN):
                    if q < UN - 1:
                        transposes(n, q + 1, b)
                    side(n, q, 0)
                    if q == UN - 1 and has_next(n):
                        transposes(n + 1, 0, 1 - b)
                    side(n, q, 1)
                    output_gate(n, q)

            tiles(pe, body)

        @block.scalar
        def _(act):
            def square(n, b, h):
                act.wait_ge(gn_ready, 2 * n + h + 1)
                if not is_zero(n):
                    act.wait_ge(small, 10 * n - 8 + 5 * h)
                act.activation(half(sq, h), half(gn[b], h), ACT.Square).then_inc(sq_ready, 1)

            def high_part(n, q):
                act.wait_ge(xt_ready, UN * n + q + 1)
                if not (is_zero(n) and q < 2):
                    act.wait_ge(g_ready, UN * n + q - 1)
                act.activation(high[q % 2][:, :], x_ps[q % 2][:, :], ACT.Copy).then_inc(high_ready, 1)

            def sigmoid(n, q, s):
                act.wait_ge(gate_ready[s], UN * n + q + 1)
                act.activation(sig[s][:, :], proj_ps[s][1][:, :], ACT.Sigmoid,
                               bias=keep.bias[:, 2 * s + 1:2 * s + 2]).then_inc(sig_ready[s], 1)

            def gate(n, q, b, j):
                act.wait_ge(g_ready, UN * n + q + 1)
                if q == 0 and not is_first(n):
                    act.wait_ge(stored[2][b], DMA * j)
                act.activation(gout[b][:, q, :], g_ps[q % 2][:, :], ACT.Sigmoid).then_inc(g_done, 1)

            square(0, 0, 0)
            square(0, 0, 1)
            high_part(0, 0)

            def body(n, b, j):
                for q in range(UN):
                    if q < UN - 1:
                        high_part(n, q + 1)
                    sigmoid(n, q, 0)
                    if q == UN - 1 and has_next(n):
                        high_part(n + 1, 0)
                    sigmoid(n, q, 1)
                    if q < 2 and has_next(n):
                        square(n + 1, 1 - b, q)
                    gate(n, q, b, j)

            tiles(act, body)

        @block.vector
        def _(dve):
            def sum_values(n, b, h):
                dve.wait_ge(gn_ready, 2 * n + h + 1)
                dve.tensor_reduce(sums[:, h, :], half(gn[b], h), AX.X, ALU.add).then_inc(small, 1)

            def sum_squares(n, h):
                dve.wait_ge(sq_ready, 2 * n + h + 1)
                dve.tensor_reduce(sums_sq[:, h, :], half(sq, h), AX.X, ALU.add).then_inc(small, 1)

            def variance(n, h):
                i = 10 * n + 5 * h
                dve.wait_ge(small, i + 1)
                dve.scalar_tensor_tensor(out=mean_sq[:, h, :], in0=sums[:, h, :], scalar=1.0 / C ** 2,
                                         in1=sums[:, h, :], op0=ALU.mult, op1=ALU.mult).then_inc(small, 1)
                dve.wait_ge(small, i + 3)
                dve.scalar_tensor_tensor(out=var[:, h, :], in0=sums_sq[:, h, :], scalar=1.0 / C,
                                         in1=mean_sq[:, h, :], op0=ALU.mult, op1=ALU.subtract).then_inc(small, 1)
                dve.wait_ge(small, i + 4)
                dve.tensor_scalar(var_eps[:, h, :], var[:, h, :], 0.0, EPS, ALU.max, ALU.add).then_inc(small, 1)

            def normalise(n, q, b):
                if q % 2 == 0:
                    dve.wait_ge(rs_ready, 2 * n + q // 2 + 1)
                if not is_first(n):
                    dve.wait_ge(xt_ready, UN * (n - 2) + q + 1)
                tok = slice(2 * WT * q, 2 * WT * q + 2 * WT)
                in_half = 2 * WT * (q % 2)
                dve.tensor_tensor(xn[b][:, tok, :], gn[b][:, tok, :],
                                  rs[:, q // 2, in_half:in_half + 2 * WT].unsqueeze(2).to_broadcast([P, 2 * WT, C]),
                                  ALU.mult).then_inc(xn_ready, 1)

            def low_part(n, q):
                dve.wait_ge(high_ready, UN * n + q + 1)
                dve.tensor_tensor(low[q % 2][:, :], x_ps[q % 2][:, :], high[q % 2][:, :],
                                  ALU.subtract).then_inc(low_ready, 1)

            def value(n, q, s, b, j):
                dve.wait_ge(sig_ready[s], UN * n + q + 1)
                dve.wait_ge(val_ready[s], UN * n + q + 1)
                if q == 0 and not is_first(n):
                    dve.wait_ge(stored[s][b], DMA * j)
                dve.scalar_tensor_tensor(out=out[s][b][:, q, :], in0=proj_ps[s][0][:, :],
                                         scalar=keep.bias[:, 2 * s:2 * s + 1], in1=sig[s][:, :],
                                         op0=ALU.add, op1=ALU.mult).then_inc(gated[s], 1)

            for h in range(2):
                sum_values(0, 0, h)
                sum_squares(0, h)
                variance(0, h)
            for q in range(UN):
                normalise(0, q, 0)
            low_part(0, 0)

            def body(n, b, j):
                nxt = has_next(n)
                for q in range(UN):
                    if q < UN - 1:
                        low_part(n, q + 1)
                    elif nxt:
                        normalise(n + 1, 0, 1 - b)
                        normalise(n + 1, 1, 1 - b)
                    value(n, q, 0, b, j)
                    if nxt and q < 2:
                        sum_values(n + 1, 1 - b, q)
                    if nxt and q == UN - 1:
                        low_part(n + 1, 0)
                        normalise(n + 1, 2, 1 - b)
                    value(n, q, 1, b, j)
                    if nxt and q < 2:
                        sum_squares(n + 1, q)
                        variance(n + 1, q)
                    if nxt and q == UN - 1:
                        normalise(n + 1, 3, 1 - b)

            tiles(dve, body)




def contract(nc, left_d, right_d, mixed_d, keep):
    with ExitStack() as ctx:
        t = Tools(nc, ctx, "ct")
        lt = [t.sb(f"l{b}", [P, 2, WT, H]) for b in range(2)]
        rt = [t.sb(f"r{b}", [P, 2, WT, H]) for b in range(2)]
        l_hi = [t.sb(f"l_hi{b}", [P, 2, WT, H], F32R) for b in range(2)]
        l_lo = [t.sb(f"l_lo{b}", [P, 2, WT, H], F32R) for b in range(2)]
        r_hi = [t.sb(f"r_hi{b}", [P, 2, WT, H], F32R) for b in range(2)]
        r_lo = [t.sb(f"r_lo{b}", [P, 2, WT, H], F32R) for b in range(2)]
        om = [t.sb(f"o{b}", [P, 2, WT, H]) for b in range(2)]
        om_sq = t.sb("o_sq", [P, 2, WT, H])
        total = t.sb("total", [P, 2, WT, H])
        total_sq = t.sb("total_sq", [P, 2, WT, H])
        acc = [[t.ps(f"acc{b}{i}", [P, L]) for i in range(WT)] for b in range(2)]
        l_loaded = [t.sem(f"l_loaded{b}") for b in range(2)]
        r_loaded = [t.sem(f"r_loaded{b}") for b in range(2)]
        stored = [t.sem(f"stored{b}") for b in range(2)]
        l_high = t.sem("l_high")
        r_high = t.sem("r_high")
        l_low = t.sem("l_low")
        r_low = t.sem("r_low")
        summed = t.sem("summed")
        out_dve = t.sem("out_dve")
        out_act = t.sem("out_act")
        totals_set = t.sem("totals_set")
        squared = t.sem("squared")
        total_done = t.sem("total_done")
        total_sq_done = t.sem("total_sq_done")
        step = t.sem("step")
        var_in = t.sem("var_in")
        var_turned = t.sem("var_turned")
        root_in = t.sem("root_in")
        root_ready = t.sem("root_ready")
        view = [d.rearrange("e d (p t) j -> d p e (t j)", t=WT) for d in (left_d, right_d, mixed_d)]
        block = ctx.enter_context(nc.Block())

        def channels(eng, body):
            for n in range(2):
                body(n, n, 0)
            with eng.Fori(1, C // 2 - 1) as j:
                for b in range(2):
                    body(2 * j + b, b, j)
            for b in range(2):
                body(C - 2 + b, b, C // 2 - 1)

        def flat(tile):
            return tile[:, :, :, :].rearrange("p e t j -> p e (t j)")

        def is_first(n):
            return isinstance(n, int) and n < 2

        def is_zero(n):
            return isinstance(n, int) and n == 0

        def has_next(n):
            return not (isinstance(n, int) and n == C - 1)

        @block.sync
        def _(sp):
            for b in range(2):
                sp.dma_start(flat(lt[b]), view[0][b]).then_inc(l_loaded[b], DMA)
                sp.dma_start(flat(rt[b]), view[1][b]).then_inc(r_loaded[b], DMA)

            def body(n, b, j):
                if not (isinstance(n, int) and n >= C - 2):
                    sp.wait_ge(l_low, n + 1)
                    sp.dma_start(flat(lt[b]), view[0][n + 2]).then_inc(l_loaded[b], DMA)
                    sp.wait_ge(r_low, n + 1)
                    sp.dma_start(flat(rt[b]), view[1][n + 2]).then_inc(r_loaded[b], DMA)
                sp.wait_ge(out_dve, 2 * n + 2)
                sp.wait_ge(out_act, 2 * n + 2)
                sp.dma_start(view[2][n], flat(om[b])).then_inc(stored[b], DMA)

            channels(sp, body)
            for b in range(2):
                sp.wait_ge(stored[b], DMA * (C // 2))

        @block.tensor
        def _(pe):
            def body(n, b, j):
                pe.wait_ge(l_high, n + 1)
                pe.wait_ge(r_high, n + 1)
                pe.wait_ge(l_low, n + 1)
                pe.wait_ge(r_low, n + 1)
                for i in range(WT):
                    if not is_first(n):
                        pe.wait_ge(out_dve if i % 2 == 0 else out_act, 2 * n - 3 + i // 2)
                    bank = acc[b][i].rearrange("p (e j) -> p e j", e=2)
                    for k in range(WT):
                        high = r_hi[b][:, i % 2, k, i // 2:H:2]
                        low = r_lo[b][:, i % 2, k, i // 2:H:2]
                        pe.matmul(bank, high, l_hi[b][:, :, k, :], start=(k == 0), stop=False)
                        pe.matmul(bank, high, l_lo[b][:, :, k, :], start=False, stop=False)
                        last = pe.matmul(bank, low, l_hi[b][:, :, k, :], start=False, stop=(k == WT - 1))
                    last.then_inc(summed, 1)

            channels(pe, body)
            pe.wait_ge(var_in, 1)
            for i in range(WT):
                for k in range(WT):
                    last = pe.transpose(acc[0][i][:, P * k:P * k + P], total_sq[:, k % 2, i, k // 2:H:2],
                                        keep.ident[:, :])
                last.then_inc(var_turned, 1)

        @block.scalar
        def _(act):
            def high(n, b, j):
                act.wait_ge(l_loaded[b], DMA * j + DMA)
                if not is_first(n):
                    act.wait_ge(summed, WT * n - WT)
                for k in range(WT):
                    last = act.activation(l_hi[b][:, :, k, :], lt[b][:, :, k, :], ACT.Copy, scale=keep.mask_sq[:, k:k + 1])
                last.then_inc(l_high, 1)
                act.wait_ge(r_loaded[b], DMA * j + DMA)
                act.activation(r_hi[b][:, :, :, :], rt[b][:, :, :, :], ACT.Copy).then_inc(r_high, 1)

            high(0, 0, 0)

            def body(n, b, j):
                if has_next(n):
                    high(n + 1, 1 - b, j + b)
                if not is_first(n):
                    act.wait_ge(stored[b], DMA * j)
                    act.wait_ge(total_done, n - 1)
                for i in (1, 3):
                    act.wait_ge(summed, WT * n + i + 1)
                    act.activation(om[b][:, :, i, :], acc[b][i].rearrange("p (e j) -> p e j", e=2), ACT.Copy).then_inc(out_act, 1)
                act.wait_ge(out_dve, 2 * n + 2)
                act.wait_ge(out_act, 2 * n + 2)
                if not is_zero(n):
                    act.wait_ge(total_sq_done, n)
                act.activation(om_sq[:, :, :, :], om[b][:, :, :, :], ACT.Square).then_inc(squared, 1)

            channels(act, body)
            act.wait_ge(root_in, 1)
            act.activation(keep.mask_tok_sq[:, :], keep.mask_tok_sq[:, :], ACT.Sqrt).then_inc(root_ready, 1)

        @block.gpsimd
        def _(pool):
            pool.memset(total[:, :, :, :], 0.0).then_inc(totals_set, 1)
            pool.memset(total_sq[:, :, :, :], 0.0).then_inc(totals_set, 1)
            pool.wait_ge(totals_set, 2)

            def body(n, b, j):
                pool.wait_ge(squared, n + 1)
                if not is_zero(n):
                    pool.wait_ge(total_sq_done, n)
                pool.tensor_tensor(total_sq[:, :, :, :], total_sq[:, :, :, :], om_sq[:, :, :, :],
                                   ALU.add).then_inc(total_sq_done, 1)

            channels(pool, body)

        @block.vector
        def _(dve):
            def low(n, b, j):
                dve.wait_ge(l_loaded[b], DMA * j + DMA)
                dve.wait_ge(l_high, n + 1)
                if not is_first(n):
                    dve.wait_ge(summed, WT * n - WT)
                for k in range(WT):
                    last = dve.scalar_tensor_tensor(out=l_lo[b][:, :, k, :], in0=lt[b][:, :, k, :],
                                                    scalar=keep.mask_sq[:, k:k + 1], in1=l_hi[b][:, :, k, :],
                                                    op0=ALU.mult, op1=ALU.subtract)
                last.then_inc(l_low, 1)
                dve.wait_ge(r_loaded[b], DMA * j + DMA)
                dve.wait_ge(r_high, n + 1)
                dve.tensor_tensor(r_lo[b][:, :, :, :], rt[b][:, :, :, :], r_hi[b][:, :, :, :],
                                  ALU.subtract).then_inc(r_low, 1)

            low(0, 0, 0)
            dve.wait_ge(totals_set, 1)

            def body(n, b, j):
                if has_next(n):
                    low(n + 1, 1 - b, j + b)
                if not is_first(n):
                    dve.wait_ge(stored[b], DMA * j)
                    dve.wait_ge(squared, n - 1)
                for i in (0, 2):
                    dve.wait_ge(summed, WT * n + i + 1)
                    dve.tensor_copy(om[b][:, :, i, :], acc[b][i].rearrange("p (e j) -> p e j", e=2)).then_inc(out_dve, 1)
                dve.wait_ge(out_dve, 2 * n + 2)
                dve.wait_ge(out_act, 2 * n + 2)
                if not is_zero(n):
                    dve.wait_ge(total_done, n)
                dve.tensor_tensor(total[:, :, :, :], total[:, :, :, :], om[b][:, :, :, :],
                                  ALU.add).then_inc(total_done, 1)

            channels(dve, body)
            link = chained(dve, step)
            dve.wait_ge(total_done, C)
            dve.wait_ge(total_sq_done, C)
            link(dve.tensor_scalar(total[:, :, :, :], total[:, :, :, :], 1.0 / C, None, ALU.mult))
            link(dve.tensor_tensor(total[:, :, :, :], total[:, :, :, :], total[:, :, :, :], ALU.mult))
            whole = [v[:, :, :, :].rearrange("p e t j -> p (e t j)") for v in (total, total_sq)]
            dve.scalar_tensor_tensor(out=whole[1], in0=whole[1], scalar=1.0 / C, in1=whole[0],
                                     op0=ALU.mult, op1=ALU.subtract).then_inc(var_in, 1)
            by_row = keep.mask_tok_sq[:, :].rearrange("p (i f t) -> p f i t", f=WT, t=WT)
            for i in range(WT):
                dve.wait_ge(var_turned, i + 1)
                last = dve.scalar_tensor_tensor(out=by_row[:, i, :, :], in0=acc[0][i].rearrange("p (t i) -> p i t", t=WT),
                                                scalar=0.0, in1=by_row[:, i, :, :], op0=ALU.max, op1=ALU.mult)
            link(last)
            dve.tensor_scalar(keep.mask_tok_sq[:, :], keep.mask_tok_sq[:, :], EPS, None, ALU.add).then_inc(root_in, 1)
            dve.wait_ge(root_ready, 1)
            link(dve.reciprocal(keep.mask_tok_sq[:, :], keep.mask_tok_sq[:, :]))
            link(dve.tensor_tensor(keep.token_scale[:, :], keep.mask_tok[:, :], keep.mask_tok_sq[:, :], ALU.mult))




def finish_layer0(nc, x, mixed_d, gate_d, x1_d, fourier_d, keep):
    with ExitStack() as ctx:
        t = Tools(nc, ctx, "fi")
        xt = [t.sb(f"x{b}", [P, TR, WT, C]) for b in range(2)]
        x1 = [t.sb(f"x1{b}", [P, TR, WT, C]) for b in range(2)]
        gt = [t.sb(f"g{b}", [P, TR, WT, C]) for b in range(2)]
        mt = [t.sb(f"m{b}", [P, TR, H]) for b in range(2)]
        yt = [t.sb(f"y{b}", [P, TR, WT, C]) for b in range(2)]
        x1_sq = t.sb("x1_sq", [P, TR, WT, C])
        four = [t.sb(f"four{b}", [M2, TR, C]) for b in range(2)]
        row_sum = t.sb("row_sum", [C, C])
        y_ps = [t.ps(f"y{k}", [P, L]) for k in range(UN)]
        f_ps = [t.ps(f"f{b}", [M2, TR * C]) for b in range(2)]
        ss_ps = t.ps("ss", [C, TR * C])

        m_loaded = [t.sem(f"m_loaded{b}") for b in range(2)]
        x_loaded = [t.sem(f"x_loaded{b}") for b in range(2)]
        g_loaded = [t.sem(f"g_loaded{b}") for b in range(2)]
        x1_stored = [t.sem(f"x1_stored{b}") for b in range(2)]
        f_stored = [t.sem(f"f_stored{b}") for b in range(2)]
        y_ready = t.sem("y_ready")
        y_scaled = t.sem("y_scaled")
        y_shifted = t.sem("y_shifted")
        y_gated = t.sem("y_gated")
        x1_ready = t.sem("x1_ready")
        x1_sq_ready = t.sem("x1_sq_ready")
        f_ready = t.sem("f_ready")
        f_copied = t.sem("f_copied")
        ss_done = t.sem("ss_done")
        step = t.sem("step")

        x_v = x.rearrange("a (n r) (p t) c -> (a n) p r t c", r=TR, t=WT)
        x1_v = x1_d.rearrange("(n r) (p t) c -> n p r t c", r=TR, t=WT)
        g_v = gate_d.rearrange("(n r) (p t) c -> n p r t c", r=TR, t=WT)
        m_v = mixed_d.rearrange("e d (n r) j -> n (e d) r j", r=TR)
        f_v = fourier_d.rearrange("m (n r) c -> n m r c", r=TR)
        block = ctx.enter_context(nc.Block())

        def tiles(eng, body):
            for n in range(4):
                body(n, n % 2, n // 2)
            with eng.Fori(2, NT // 2 - 1) as j:
                for b in range(2):
                    body(2 * j + b, b, j)
            for b in range(2):
                body(NT - 2 + b, b, NT // 2 - 1)

        def is_first(n):
            return isinstance(n, int) and n < 2

        def is_zero(n):
            return isinstance(n, int) and n == 0

        def has_next(n):
            return not (isinstance(n, int) and n == NT - 1)

        @block.sync
        def _(sp):
            def load_mixed(n, b):
                sp.dma_start(mt[b][:, :, :], m_v[n]).then_inc(m_loaded[b], DMA)

            def load_rest(n, b):
                sp.dma_start(gt[b][:, :, :, :], g_v[n]).then_inc(g_loaded[b], DMA)
                sp.dma_start(xt[b][:, :, :, :], x_v[n]).then_inc(x_loaded[b], DMA)

            for b in range(2):
                load_mixed(b, b)
                load_rest(b, b)

            def stores(n, b, load):
                sp.wait_ge(x1_ready, n + 1)
                if load:
                    load_rest(n + 2, b)
                sp.dma_start(x1_v[n], x1[b][:, :, :, :]).then_inc(x1_stored[b], DMA)

            def store_rows(n, b):
                sp.wait_ge(f_copied, n + 1)
                sp.dma_start(f_v[n], four[b][:, :, :]).then_inc(f_stored[b], DMA)

            def body(n, b, j):
                if not (isinstance(n, int) and n >= NT - 2):
                    sp.wait_ge(y_ready, UN * n + UN)
                    load_mixed(n + 2, b)
                if not is_zero(n):
                    stores(n - 1, 1 - b, load=not (isinstance(n, int) and n >= NT - 1))
                if not is_first(n):
                    store_rows(n - 2, b)

            tiles(sp, body)
            stores(NT - 1, 1, load=False)
            for n in range(NT - 2, NT):
                store_rows(n, n % 2)
            for b in range(2):
                sp.wait_ge(x1_stored[b], DMA * (NT // 2))
                sp.wait_ge(f_stored[b], DMA * (NT // 2))

        @block.tensor
        def _(pe):
            def output(n, q, b):
                if not is_zero(n):
                    pe.wait_ge(y_scaled, UN * n + q - UN + 1)
                for k in range(WT):
                    last = pe.matmul(y_ps[q][:, P * k:P * k + P], mt[b][:, 2 * q + k // 2, k % 2:H:2], keep.w2_bd[:, :],
                                     start=True, stop=True)
                last.then_inc(y_ready, 1)

            def transform(n, b):
                pe.wait_ge(x1_ready, n + 1)
                if not is_first(n):
                    pe.wait_ge(f_copied, n - 1)
                for k in range(WT):
                    last = pe.matmul(f_ps[b].rearrange("m (r c) -> m r c", c=C), keep.basis[:, k, :],
                                     x1[b][:, :, k, :], start=(k == 0), stop=(k == WT - 1))
                last.then_inc(f_ready, 1)
                pe.wait_ge(x1_sq_ready, n + 1)
                for k in range(WT):
                    first = is_zero(n) and k == 0
                    final = isinstance(n, int) and n == NT - 1 and k == WT - 1
                    last = pe.matmul(ss_ps[:, :].rearrange("m (r c) -> m r c", c=C), keep.ones[:, :],
                                     x1_sq[:, :, k, :], start=first, stop=final, skip_group_check=True)
                last.then_inc(ss_done, 1)

            def body(n, b, j):
                pe.wait_ge(m_loaded[b], DMA * j + DMA)
                for q in range(UN):
                    output(n, q, b)
                if not is_first(n):
                    transform(n - 2, b)

            tiles(pe, body)
            for n in range(NT - 2, NT):
                transform(n, n % 2)

        @block.scalar
        def _(act):
            def result(n, b, j):
                act.wait_ge(x1_ready, n + 1)
                if not is_zero(n):
                    act.wait_ge(ss_done, n)
                act.activation(x1_sq[:, :, :, :], x1[b][:, :, :, :], ACT.Square).then_inc(x1_sq_ready, 1)
                act.wait_ge(f_ready, n + 1)
                if not is_first(n):
                    act.wait_ge(f_stored[b], DMA * j)
                act.activation(four[b][:, :, :], f_ps[b].rearrange("m (r c) -> m r c", c=C),
                               ACT.Copy).then_inc(f_copied, 1)

            def body(n, b, j):
                if not is_first(n):
                    result(n - 2, b, j - 1)

            tiles(act, body)
            for n in range(NT - 2, NT):
                result(n, n % 2, NT // 2 - 1)

        @block.gpsimd
        def _(pool):
            def body(n, b, j):
                pool.wait_ge(y_scaled, UN * n + UN)
                y3 = yt[b][:, :, :, :].rearrange("p r t c -> p (r t) c")
                pool.tensor_tensor(y3, y3, keep.c_row[:, :].unsqueeze(1).to_broadcast([P, TR * WT, C]),
                                   ALU.add).then_inc(y_shifted, 1)

            tiles(pool, body)

        @block.vector
        def _(dve):
            def scaled(n, q, b):
                dve.wait_ge(y_ready, UN * n + q + 1)
                if q == 0 and not is_first(n):
                    dve.wait_ge(x1_ready, n - 1)
                dve.tensor_tensor(yt[b][:, 2 * q:2 * q + 2, :, :].rearrange("p r t c -> p (r t) c"),
                                  y_ps[q].rearrange("p (t c) -> p t c", c=C),
                                  keep.token_scale[:, bass.ds(TR * WT * n + 2 * WT * q, 2 * WT)].unsqueeze(2).to_broadcast([P, 2 * WT, C]),
                                  ALU.mult).then_inc(y_scaled, 1)

            def finish(n, b, j):
                dve.wait_ge(y_shifted, n + 1)
                dve.wait_ge(g_loaded[b], DMA * j + DMA)
                dve.tensor_tensor(yt[b][:, :, :, :], yt[b][:, :, :, :], gt[b][:, :, :, :],
                                  ALU.mult).then_inc(y_gated, 1)
                dve.wait_ge(y_gated, n + 1)
                dve.wait_ge(x_loaded[b], DMA * j + DMA)
                if not is_first(n):
                    dve.wait_ge(x1_stored[b], DMA * j)
                    dve.wait_ge(x1_sq_ready, n - 1)
                    dve.wait_ge(f_ready, n - 1)
                dve.tensor_tensor(x1[b][:, :, :, :], yt[b][:, :, :, :], xt[b][:, :, :, :],
                                  ALU.add).then_inc(x1_ready, 1)

            def body(n, b, j):
                for q in range(UN):
                    scaled(n, q, b)
                if not is_zero(n):
                    finish(n - 1, 1 - b, j - 1 + b)

            tiles(dve, body)
            finish(NT - 1, 1, NT // 2 - 1)
            link = chained(dve, step)
            dve.wait_ge(ss_done, NT)
            link(dve.tensor_reduce(row_sum[:, :], ss_ps[:, :].rearrange("m (r c) -> m c r", c=C), AX.X, ALU.add))
            link(dve.tensor_tensor(row_sum[:, :], row_sum[:, :], keep.ident[0:C, 0:C], ALU.mult))
            link(dve.tensor_reduce(keep.sum_sq[:, :], row_sum[:, :], AX.X, ALU.add))




def spectral(nc, fourier_d, w_real, w_imag, keep):
    with ExitStack() as ctx:
        t = Tools(nc, ctx, "sp")
        rows = t.sb("rows", [P, M2, WT, C])
        w = t.sb("w", [P, C, MODES, MODES])
        four = t.sb("four", [C, M2, M2])
        xr = t.sb("xr", [C, MODES, MODES])
        xi = t.sb("xi", [C, MODES, MODES])
        xm = t.sb("xm", [P, MODES * MODES, 2])
        mean_in = t.sb("mean_in", [C, 1])
        sq_in = t.sb("sq_in", [C, 1])
        sums = t.sb("sums", [C, 2])
        v = t.sb("v", [C, 8])
        root = t.sb("root", [C, 1])
        z = t.sb("z", [C, MODES * MODES, 2])
        q = t.sb("q", [C, M2, M2])
        f_ps = t.ps("f", [C, 2, 512])
        s_ps = t.ps("s", [C, 512])
        z_ps = t.ps("z", [C, MODES * MODES, 2])
        q_ps = t.ps("q", [M2, 3, 8, C])
        loaded = t.sem("loaded")
        step = t.sem("step")
        f_ready = t.sem("f_ready")
        sums_in = t.sem("sums_in")
        sums_ready = t.sem("sums_ready")
        root_in = t.sem("root_in")
        root_ready = t.sem("root_ready")
        x_ready = t.sem("x_ready")
        z_ready = t.sem("z_ready")
        q_in = t.sem("q_in")
        q_ready = t.sem("q_ready")
        block = ctx.enter_context(nc.Block())
        NM = MODES

        @block.sync
        def _(sp):
            sp.dma_start(rows[:, :, :, :], fourier_d.rearrange("m (p t) c -> p m t c", t=WT)).then_inc(loaded, DMA)
            sp.dma_start(w[0:C, :, :, :], w_real).then_inc(loaded, DMA)
            sp.dma_start(w[C:P, :, :, :], w_imag).then_inc(loaded, DMA)

        @block.tensor
        def _(pe):
            pe.wait_ge(loaded, 3 * DMA)
            for n in range(M2):
                for k in range(WT):
                    last = pe.matmul(f_ps[:, n // NM, M2 * (n % NM):M2 * (n % NM) + M2],
                                     rows[:, n, k, :],
                                     keep.basis[:, k, :], start=(k == 0), stop=(k == WT - 1))
            last.then_inc(f_ready, 1)
            pe.wait_ge(sums_in, 1)
            pe.matmul(s_ps[:, 0:1], keep.pair[:, :], mean_in[:, :], start=True, stop=True)
            pe.matmul(s_ps[:, 1:2], keep.pair[:, :], sq_in[:, :], start=True, stop=True).then_inc(sums_ready, 1)
            pe.wait_ge(x_ready, 1)
            for n in range(NM):
                for m in range(NM):
                    last = pe.matmul(z_ps[:, n * NM + m, :], w[:, :, m, n], xm[:, n * NM + m, :],
                                     start=True, stop=True)
            last.then_inc(z_ready, 1)
            pe.wait_ge(q_in, 1)
            for n in range(M2):
                last = pe.transpose(q_ps[:, n // 8, n % 8, :], q[:, n, :], keep.ident[0:C, 0:C])
            last.then_inc(q_ready, 1)

        @block.scalar
        def _(act):
            act.wait_ge(root_in, 1)
            act.activation(root[:, :], v[:, 5:6], ACT.Sqrt).then_inc(root_ready, 1)

        @block.vector
        def _(dve):
            link = chained(dve, step)
            dve.wait_ge(f_ready, 1)
            link(dve.tensor_copy(four[:, :, :].rearrange("p (a n) m -> p a (n m)", a=2), f_ps[:, :, 0:NM * M2]))
            dve.tensor_tensor(xr[:, :, :], four[:, 0:NM, 0:NM], four[:, NM:M2, NM:M2], ALU.subtract)
            dve.tensor_tensor(xi[:, :, :], four[:, 0:NM, NM:M2], four[:, NM:M2, 0:NM], ALU.add)
            dve.tensor_scalar(mean_in[:, :], four[:, 0, 0:1], 1.0 / TOK, None, ALU.mult)
            dve.tensor_scalar(sq_in[:, :], keep.sum_sq[:, :], 1.0 / TOK, None, ALU.mult).then_inc(sums_in, 1)
            dve.wait_ge(sums_ready, 1)
            link(dve.tensor_copy(sums[:, :], s_ps[:, 0:2]))
            link(dve.tensor_tensor(v[:, 0:1], sums[:, 0:1], sums[:, 0:1], ALU.mult))
            link(dve.tensor_tensor(v[:, 1:2], sums[:, 1:2], v[:, 0:1], ALU.subtract))
            dve.tensor_scalar(v[:, 5:6], v[:, 1:2], 0.0, EPS, ALU.max, ALU.add).then_inc(root_in, 1)
            link(dve.tensor_scalar(v[:, 2:3], sums[:, 0:1], float(TOK), None, ALU.mult))
            dve.wait_ge(root_ready, 1)
            link(dve.reciprocal(v[:, 3:4], root[:, :]))
            link(dve.tensor_tensor(xr[:, 0, 0:1], xr[:, 0, 0:1], v[:, 2:3], ALU.subtract))
            link(dve.tensor_scalar(v[:, 4:5], v[:, 3:4], -1.0, None, ALU.mult))
            xr_f = xr[:, :, :].rearrange("p n m -> p (n m)")
            xi_f = xi[:, :, :].rearrange("p n m -> p (n m)")
            dve.tensor_scalar(xm[0:C, :, 0], xr_f, v[:, 3:4], None, ALU.mult)
            dve.tensor_scalar(xm[0:C, :, 1], xi_f, v[:, 4:5], None, ALU.mult)
            dve.tensor_scalar(xm[C:P, :, 0], xi_f, v[:, 3:4], None, ALU.mult)
            dve.tensor_scalar(xm[C:P, :, 1], xr_f, v[:, 3:4], None, ALU.mult).then_inc(x_ready, 1)
            dve.wait_ge(z_ready, 1)
            link(dve.tensor_copy(z[:, :, :], z_ps[:, :, :]))
            zr = z[:, :, 0].rearrange("o (n m) -> o n m", m=NM)
            zi = z[:, :, 1].rearrange("o (n m) -> o n m", m=NM)
            dve.tensor_copy(q[:, 0:NM, 0:NM], zr)
            dve.tensor_scalar(q[:, 0:NM, NM:M2], zi, -1.0, None, ALU.mult)
            dve.tensor_scalar(q[:, NM:M2, 0:NM], zi, -1.0, None, ALU.mult)
            dve.tensor_scalar(q[:, NM:M2, NM:M2], zr, -1.0, None, ALU.mult).then_inc(q_in, 1)
            dve.wait_ge(q_ready, 1)
            for a in range(3):
                dve.tensor_copy(keep.spectrum[:, :, 8 * a:8 * a + 8].rearrange("m o n -> m n o"), q_ps[:, a, :, :])




def finish_layer1(nc, x1_d, out, keep):
    with ExitStack() as ctx:
        t = Tools(nc, ctx, "la")
        col = t.sb("col", [P, L, C])
        xt = [t.sb(f"x{b}", [P, TR, WT, C]) for b in range(2)]
        yo = [t.sb(f"yo{b}", [P, TR, WT, C]) for b in range(2)]
        ps = [t.ps(f"ps{k}", [P, L]) for k in range(8)]
        loaded = [t.sem(f"loaded{b}") for b in range(2)]
        stored = [t.sem(f"stored{b}") for b in range(2)]
        col_zero = [t.sem(f"col_zero{h}") for h in range(2)]
        col_ready = t.sem("col_ready")
        col_dve = t.sem("col_dve")
        col_act = t.sem("col_act")
        y_ready = t.sem("y_ready")
        y_done = t.sem("y_done")
        x_v = x1_d.rearrange("(n r) (p t) c -> n p r t c", r=TR, t=WT)
        o_v = out.rearrange("a (n r) (p t) c -> (a n) p r t c", r=TR, t=WT)
        block = ctx.enter_context(nc.Block())

        def tiles(eng, body):
            for n in range(2):
                body(n, n, 0)
            with eng.Fori(1, NT // 2 - 1) as j:
                for b in range(2):
                    body(2 * j + b, b, j)
            for b in range(2):
                body(NT - 2 + b, b, NT // 2 - 1)

        def is_first(n):
            return isinstance(n, int) and n < 2

        @block.sync
        def _(sp):
            for b in range(2):
                sp.dma_start(xt[b][:, :, :, :], x_v[b]).then_inc(loaded[b], DMA)

            def body(n, b, j):
                sp.wait_ge(y_done, WT * n + WT)
                if not (isinstance(n, int) and n >= NT - 2):
                    sp.dma_start(xt[b][:, :, :, :], x_v[n + 2]).then_inc(loaded[b], DMA)
                sp.dma_start(o_v[n], yo[b][:, :, :, :]).then_inc(stored[b], DMA)

            tiles(sp, body)
            for b in range(2):
                sp.wait_ge(stored[b], DMA * (NT // 2))

        @block.tensor
        def _(pe):
            for o in range(C):
                if o >= 8:
                    pe.wait_ge(col_dve if o % 2 == 0 else col_act, (o - 8) // 2 + 1)
                pe.matmul(ps[o % 8][0:M2, :], keep.spectrum[:, o, :], keep.inverse[0:M2, :],
                          start=True, stop=True).then_inc(col_ready, 1)
            pe.wait_ge(col_dve, C // 2)
            pe.wait_ge(col_act, C // 2)

            def body(n, b, j):
                for k in range(WT):
                    if not is_first(n):
                        pe.wait_ge(y_done, WT * (n - 2) + k + 1)
                    pe.matmul(ps[WT * b + k][:, :], keep.inverse[:, k:L:WT],
                              col[:, bass.ts(n, TR), :].rearrange("m r c -> m (r c)"),
                              start=True, stop=True).then_inc(y_ready, 1)

            tiles(pe, body)

        @block.gpsimd
        def _(pool):
            pool.memset(col[:, 0:H, :], 0.0).then_inc(col_zero[0], 1)

        @block.scalar
        def _(act):
            act.wait_ge(col_zero[0], 1)
            act.wait_ge(col_zero[1], 1)
            for o in range(1, C, 2):
                act.wait_ge(col_ready, o + 1)
                act.activation(col[0:M2, :, o], ps[o % 8][0:M2, :], ACT.Copy).then_inc(col_act, 1)

        @block.vector
        def _(dve):
            dve.memset(col[:, H:L, :], 0.0).then_inc(col_zero[1], 1)
            dve.wait_ge(col_zero[0], 1)
            dve.wait_ge(col_zero[1], 1)
            for o in range(0, C, 2):
                dve.wait_ge(col_ready, o + 1)
                dve.tensor_copy(col[0:M2, :, o], ps[o % 8][0:M2, :]).then_inc(col_dve, 1)

            def body(n, b, j):
                dve.wait_ge(loaded[b], DMA * j + DMA)
                if not is_first(n):
                    dve.wait_ge(stored[b], DMA * j)
                for k in range(WT):
                    dve.wait_ge(y_ready, WT * n + k + 1)
                    dve.tensor_tensor(yo[b][:, :, k, :], ps[WT * b + k][:, :].rearrange("p (r c) -> p r c", c=C),
                                      xt[b][:, :, k, :], ALU.add).then_inc(y_done, 1)

            tiles(dve, body)


class Keep:
    pass


def program(nc, ins, tab, out):
    x = ins["x"]
    left_d = nc.dram_tensor("left_d", [2, C, L, H], F32, kind="Internal").ap()
    right_d = nc.dram_tensor("right_d", [2, C, L, H], F32, kind="Internal").ap()
    mixed_d = nc.dram_tensor("mixed_d", [2, C, L, H], F32, kind="Internal").ap()
    gate_d = nc.dram_tensor("gate_d", [L, L, C], F32, kind="Internal").ap()
    x1_d = nc.dram_tensor("x1_d", [L, L, C], F32, kind="Internal").ap()
    fourier_d = nc.dram_tensor("fourier_d", [M2, L, C], F32, kind="Internal").ap()
    with ExitStack() as ctx:
        t = Tools(nc, ctx, "keep")
        k = Keep()
        k.mean0 = t.sb("mean0", [P, G])
        k.var0 = t.sb("var0", [P, G])
        k.gn_scale = t.sb("gn_scale", [P, C])
        k.gn_shift = t.sb("gn_shift", [P, C])
        k.ident = t.sb("ident", [P, P])
        k.basis = t.sb("basis", [P, WT, M2])
        k.inverse = t.sb("inverse", [P, L])
        k.pair = t.sb("pair", [C, C])
        k.w_high = t.sb("w_high", [P, 5, P], F32R)
        k.w_low = t.sb("w_low", [P, 5, P], F32R)
        k.bias = t.sb("bias", [P, 4])
        k.w2_bd = t.sb("w2_bd", [P, P])
        k.c_row = t.sb("c_row", [P, C])
        k.gbias3 = t.sb("gbias3", [P, L], BF16)
        k.ones_bf = t.sb("ones_bf", [P, P], BF16)
        k.ones = t.sb("ones", [P, C])
        k.mask_sq = t.sb("mask_sq", [P, WT])
        k.mask_tok = t.sb("mask_tok", [P, NT * 32])
        k.mask_tok_sq = t.sb("mask_tok_sq", [P, NT * 32])
        k.token_scale = k.mask_tok
        k.sum_sq = t.sb("sum_sq", [C, 1])
        k.spectrum = t.sb("spectrum", [M2, C, M2])
        statistics_of_x(nc, x, k)
        prepare(nc, ins, tab, k)
        project(nc, x, left_d, right_d, gate_d, k)
        contract(nc, left_d, right_d, mixed_d, k)
        finish_layer0(nc, x, mixed_d, gate_d, x1_d, fourier_d, k)
        spectral(nc, fourier_d, ins["L1_conv_w_real"], ins["L1_conv_w_imag"], k)
        finish_layer1(nc, x1_d, out, k)


def kernel(**inputs):
    import concourse.bacc as bacc
    from concourse.bass_utils import run_bass_kernel_spmd

    nc = bacc.Bacc("TRN2", target_bir_lowering=False, num_devices=1)
    arrays, ins, tab = {}, {}, {}
    for name, value in inputs.items():
        a = np.ascontiguousarray(value)
        arrays[f"in_{name}"] = a
        ins[name] = nc.dram_tensor(f"in_{name}", a.shape, mybir.dt.from_np(a.dtype), kind="ExternalInput").ap()
    for name, a in host_tables().items():
        a = np.ascontiguousarray(a)
        arrays[name] = a
        tab[name] = nc.dram_tensor(name, a.shape, mybir.dt.from_np(a.dtype), kind="ExternalInput").ap()
    out = nc.dram_tensor("out_0", (1, L, L, C), F32, kind="ExternalOutput").ap()
    program(nc, ins, tab, out)
    r = run_bass_kernel_spmd(nc, [arrays], core_ids=[0])
    return r.results[0]["out_0"]
```

```python
from contextlib import ExitStack

import numpy as np

import concourse.bass as bass
from concourse import mybir

F32 = mybir.dt.float32
F32R = mybir.dt.float32r
I32 = mybir.dt.int32
ALU = mybir.AluOpType
ACT = mybir.ActivationFunctionType
AX = mybir.AxisListType

P = 128
L = 512
C = 64
G = 32
CG = C // G
MODES = 12
M2 = 2 * MODES
TOK = L * L
TR = 8
NT = L // TR
UN = TR // 2
WT = L // P
H = L // 2
EPS = 1e-5
DMA = 16
STATS_T = 128
NCHUNK = TOK // (P * STATS_T)


def host_tables():
    pos = np.arange(L)[:, None] * np.arange(MODES)[None, :] * (2 * np.pi / L)
    fourier = np.concatenate([np.cos(pos), np.sin(pos)], axis=1)
    basis = fourier.reshape(P, WT, M2).astype(np.float32)
    inverse = (fourier.T / L).astype(np.float32)
    inverse_rows = np.zeros((4, P // 4, L // 4), np.float32)
    inverse_rows[:, :M2] = inverse.reshape(M2, 4, L // 4).transpose(1, 0, 2)
    inverse_columns = np.zeros((4, P // 4, 4, L), np.float32)
    for g in range(4):
        inverse_columns[g, :M2, g] = inverse
    half = np.arange(P) // C
    same = (half[:, None] == half[None, :]).astype(np.float32)
    centre = (np.eye(P) - same / C).astype(np.float32)
    group = np.arange(C) // CG
    pair = (group[:, None] == group[None, :]).astype(np.float32) / CG
    return {
        "t_ident": np.eye(P, dtype=np.float32),
        "t_basis": basis,
        "t_inverse_rows": inverse_rows.reshape(P, L // 4),
        "t_inverse_columns": inverse_columns.reshape(P, 4, L),
        "t_centre": centre,
        "t_pair": pair,
    }


class Tools:

    def __init__(self, nc, ctx, phase):
        self.nc, self.ctx, self.phase = nc, ctx, phase

    def sb(self, name, shape, dt=F32):
        return self.ctx.enter_context(self.nc.sbuf_tensor(f"{self.phase}_{name}", shape, dt))

    def ps(self, name, shape):
        n = int(np.prod(shape[1:]))
        banks = -(-n // 512)
        whole = self.ctx.enter_context(self.nc.psum_tensor(f"{self.phase}_{name}_ps", [shape[0], banks * 512], F32))
        view = whole[:, 0:n]
        if len(shape) == 2:
            return view
        names = "abcd"[:len(shape) - 1]
        return view.rearrange(f"p ({' '.join(names)}) -> p {' '.join(names)}", **dict(zip(names, shape[1:])))

    def sem(self, name):
        return self.ctx.enter_context(self.nc.semaphore(f"{self.phase}_{name}"))


def chained(eng, sem, start=0):
    n = [start]

    def link(instruction):
        n[0] += 1
        instruction.then_inc(sem, 1)
        eng.wait_ge(sem, n[0])

    return link




def prepare(nc, x, ins, tab, keep):
    with ExitStack() as ctx:
        t = Tools(nc, ctx, "pr")
        xc = [t.sb(f"x{b}", [P, STATS_T, C]) for b in range(2)]
        stats = t.sb("stats", [P, G, NCHUNK, 6])
        part = t.sb("part", [P, G, 2])
        mean0 = t.sb("mean0", [P, G])
        var0 = t.sb("var0", [P, G])
        dev = t.sb("dev", [P, G])
        sq = t.sb("sq", [P, G])
        spread = t.sb("spread", [P, G])
        ones = t.sb("ones", [P, P])
        mean_ps = t.ps("mean", [P, 256])
        x_loaded = [t.sem(f"x_loaded{b}") for b in range(2)]
        ones_set = t.sem("ones_set")
        chunk_done = t.sem("chunk_done")
        mean_ready = t.sem("mean_ready")
        var_ready = t.sem("var_ready")
        spread_ready = t.sem("spread_ready")
        x_v = x.rearrange("a h w c -> (a h w c)").rearrange("(n p t c) -> n p t c", p=P, t=STATS_T, c=C)
        names = ["left", "lgate", "right", "rgate", "ogate"]
        w_raw = t.sb("w_raw", [P, 5, C])
        w_scaled = t.sb("w_scaled", [P, 5, C])
        w_raw_bd = t.sb("w_raw_bd", [P, 5, P])
        w_bd = t.sb("w_bd", [P, 5, P])
        nw = t.sb("nw", [P, 1])
        nb = t.sb("nb", [P, 1])
        bias_in = t.sb("bias_in", [P, 5])
        centre = t.sb("centre", [P, P])
        onw = t.sb("onw", [P, 1])
        onb = t.sb("onb", [C, 1])
        ow = t.sb("ow", [P, C])
        ow_scaled = t.sb("ow_scaled", [P, C])
        onb_wide = t.sb("onb_wide", [C, P])
        row_in = t.sb("row_in", [1, C])
        ones_row = t.sb("ones_row", [1, P])
        mask_col = t.sb("mask_col", [P, WT], I32)
        mask_row = t.sb("mask_row", [1, L], I32)
        maskf_col = t.sb("maskf_col", [P, WT])
        maskf_row = t.sb("maskf_row", [1, L])
        mask_wide = t.sb("mask_wide", [P, L])
        rstd = t.sb("rstd", [P, G])
        scale = t.sb("scale", [P, G])
        shift = t.sb("shift", [P, G])
        root = t.sb("root", [P, G])
        w_ps = t.ps("w", [P, 5, C])
        b_ps = t.ps("b", [P, 5])
        ow_ps = t.ps("ow", [P, C])
        c_ps = t.ps("c", [P, C])
        m_ps = t.ps("m", [P, L])
        loaded = t.sem("loaded")
        step = t.sem("step")
        pool_set = t.sem("pool_set")
        raw_ready = t.sem("raw_ready")
        scaled_ready = t.sem("scaled_ready")
        row_ready = t.sem("row_ready")
        products = t.sem("products")
        root_in = t.sem("root_in")
        root_ready = t.sem("root_ready")
        loads = []
        for i, n in enumerate(names):
            for h in range(2):
                loads.append((w_raw[h * C:(h + 1) * C, i, :], ins[f"L0_conv_{n}_w"]))
        for h in range(2):
            rows = slice(h * C, (h + 1) * C)

            def col(v):
                return v.rearrange("(c o) -> c o", o=1)

            loads.append((nw[rows, :], col(ins["L0_conv_norm_w"])))
            loads.append((nb[rows, :], col(ins["L0_conv_norm_b"])))
            loads.append((onw[rows, :], col(ins["L0_conv_onorm_w"])))
            loads.append((ow[rows, :], ins["L0_conv_out_w"]))
            for i, n in enumerate(names):
                loads.append((bias_in[rows, i:i + 1], col(ins[f"L0_conv_{n}_b"])))
        loads.append((onb[:, :], ins["L0_conv_onorm_b"].rearrange("(c o) -> c o", o=1)))
        loads.append((row_in[:, :], ins["L0_conv_out_b"].rearrange("(o c) -> o c", o=1)))
        loads.append((mask_col[:, :], ins["L0_conv_sequence_mask"].rearrange("a (p t) -> (a p) t", t=WT)))
        loads.append((mask_row[:, :], ins["L0_conv_sequence_mask"]))
        loads.append((centre[:, :], tab["t_centre"]))
        loads.append((keep.ident[:, :], tab["t_ident"]))
        loads.append((keep.basis[:, :, :], tab["t_basis"]))
        loads.append((keep.pair[:, :], tab["t_pair"]))
        block = ctx.enter_context(nc.Block())

        @block.sync
        def _(sp):
            for b in range(2):
                sp.dma_start(xc[b][:, :, :], x_v[b]).then_inc(x_loaded[b], DMA)
            with sp.Fori(1, NCHUNK // 2) as j:
                for b in range(2):
                    sp.wait_ge(chunk_done, 2 * j + b - 1)
                    sp.dma_start(xc[b][:, :, :], x_v[2 * j + b]).then_inc(x_loaded[b], DMA)

        @block.gpsimd
        def _(pool):
            pool.memset(w_raw_bd[:, :, :], 0.0).then_inc(pool_set, 1)
            pool.memset(w_bd[:, :, :], 0.0).then_inc(pool_set, 1)
            pool.memset(keep.w2_bd[:, :], 0.0).then_inc(pool_set, 1)
            pool.memset(ones_row[:, :], 1.0).then_inc(pool_set, 1)
            pool.memset(keep.ones[:, :], 1.0).then_inc(pool_set, 1)
            pool.memset(ones[:, :], 1.0 / P).then_inc(ones_set, 1)

        @block.scalar
        def _(act):
            for dst, src in loads:
                act.dma_start(dst, src).then_inc(loaded, DMA)
            act.wait_ge(root_in, 1)
            act.activation(root[:, :], rstd[:, :], ACT.Sqrt).then_inc(root_ready, 1)

        @block.tensor
        def _(pe):
            pe.wait_ge(loaded, DMA * len(loads))
            pe.wait_ge(scaled_ready, 1)
            pe.matmul(w_ps[:, :, :], centre[:, :], w_scaled[:, :, :], start=True, stop=True)
            pe.matmul(ow_ps[:, :], centre[:, :], ow_scaled[:, :], start=True, stop=True)
            pe.wait_ge(raw_ready, 1)
            for i in range(5):
                pe.matmul(b_ps[:, i:i + 1], w_raw_bd[:, i, :], nb[:, :], start=True, stop=True)
            pe.wait_ge(pool_set, 5)
            pe.matmul(c_ps[:, :], onb_wide[:, :], ow[0:C, :], start=True, stop=False)
            pe.matmul(c_ps[:, :], ones_row[:, :], row_in[:, :], start=False, stop=True)
            pe.wait_ge(row_ready, 1)
            pe.matmul(m_ps[:, :], ones_row[:, :], maskf_row[:, :], start=True, stop=True).then_inc(products, 1)
            pe.wait_ge(ones_set, 1)
            pe.wait_ge(spread_ready, 1)
            pe.matmul(mean_ps[:, 0:G], ones[:, :], dev[:, :], start=True, stop=True).then_inc(mean_ready, 1)
            pe.wait_ge(spread_ready, 2)
            pe.matmul(mean_ps[:, G:2 * G], ones[:, :], spread[:, :], start=True, stop=True).then_inc(var_ready, 1)

        @block.vector
        def _(dve):
            link = chained(dve, step)

            def statistics(n, b, j):
                dve.wait_ge(x_loaded[b], DMA * j + DMA)
                for g in range(G):
                    last = dve.bn_stats(stats[:, g, n, :], xc[b][:, :, CG * g:CG * g + CG])
                last.then_inc(chunk_done, 1)

            def chunks(first, end):
                with dve.Fori(first, end) as j:
                    for b in range(2):
                        statistics(2 * j + b, b, j)

            chunks(0, NCHUNK // 4)
            dve.wait_ge(loaded, DMA * len(loads))
            dve.wait_ge(pool_set, 5)
            dve.tensor_scalar(ow_scaled[:, :], ow[:, :], onw[:, 0:1], None, ALU.mult)
            dve.tensor_scalar(w_scaled[:, :, :], w_raw[:, :, :], nw[:, 0:1], None, ALU.mult).then_inc(scaled_ready, 1)
            for h in range(2):
                rows = slice(h * C, (h + 1) * C)
                dve.tensor_copy(w_raw_bd[rows, :, h * C:(h + 1) * C], w_raw[rows, :, :])
            dve.tensor_copy(onb_wide[:, :], onb[:, :].to_broadcast([C, P])).then_inc(raw_ready, 1)
            dve.tensor_copy(maskf_row[:, :], mask_row[:, :]).then_inc(row_ready, 1)
            link(dve.tensor_copy(maskf_col[:, :], mask_col[:, :]))
            dve.tensor_tensor(keep.mask_sq[:, :], maskf_col[:, :], maskf_col[:, :], ALU.mult)
            dve.wait_ge(products, 1)
            for h in range(2):
                rows = slice(h * C, (h + 1) * C)
                dve.tensor_copy(w_bd[rows, :, h * C:(h + 1) * C], w_ps[rows, :, :])
                dve.tensor_copy(keep.w2_bd[rows, h * C:(h + 1) * C], ow_ps[rows, :])
            dve.tensor_tensor(keep.bias[:, :], b_ps[:, :], bias_in[:, :], ALU.add)
            dve.tensor_copy(keep.c_row[:, :], c_ps[:, :])
            link(dve.tensor_copy(mask_wide[:, :], m_ps[:, :]))
            link(dve.tensor_copy(keep.w_high[:, :, :], w_bd[:, :, :]))
            dve.tensor_tensor(keep.w_low[:, :, :], w_bd[:, :, :], keep.w_high[:, :, :], ALU.subtract)
            view = keep.mask_tok[:, :].rearrange("p (i t) -> p i t", t=WT)
            for k in range(WT):
                last = dve.tensor_scalar(view[:, :, k], mask_wide[:, :], maskf_col[:, k:k + 1], None, ALU.mult)
            link(last)
            dve.tensor_tensor(keep.mask_tok_sq[:, :], keep.mask_tok[:, :], keep.mask_tok[:, :], ALU.mult)
            chunks(NCHUNK // 4, NCHUNK // 2)
            dve.wait_ge(chunk_done, NCHUNK)
            for g in range(G):
                last = dve.bn_aggr(part[:, g, :], stats[:, g, :, :].rearrange("p n s -> p (n s)"))
            link(last)
            dve.tensor_copy(dev[:, :], part[:, :, 0]).then_inc(spread_ready, 1)
            dve.wait_ge(mean_ready, 1)
            link(dve.tensor_copy(mean0[:, :], mean_ps[:, 0:G]))
            link(dve.tensor_tensor(sq[:, :], part[:, :, 0], mean0[:, :], ALU.subtract))
            link(dve.tensor_tensor(spread[:, :], sq[:, :], sq[:, :], ALU.mult))
            dve.tensor_tensor(spread[:, :], spread[:, :], part[:, :, 1], ALU.add).then_inc(spread_ready, 1)
            dve.wait_ge(var_ready, 1)
            link(dve.tensor_copy(var0[:, :], mean_ps[:, G:2 * G]))
            dve.tensor_scalar(rstd[:, :], var0[:, :], EPS, None, ALU.add).then_inc(root_in, 1)
            dve.wait_ge(root_ready, 1)
            link(dve.reciprocal(scale[:, :], root[:, :]))
            dve.tensor_copy(keep.gn_scale[:, :].rearrange("p (g e) -> p g e", e=CG),
                            scale[:, :].unsqueeze(2).to_broadcast([P, G, CG]))
            link(dve.scalar_tensor_tensor(out=shift[:, :], in0=mean0[:, :], scalar=-1.0, in1=scale[:, :],
                                          op0=ALU.mult, op1=ALU.mult))
            dve.tensor_copy(keep.gn_shift[:, :].rearrange("p (g e) -> p g e", e=CG),
                            shift[:, :].unsqueeze(2).to_broadcast([P, G, CG]))




def project(nc, x, left_d, right_d, gate_d, keep):
    HT = TR * WT // 2
    NEWTON = 3
    RS_STEPS = 5 + 3 * (NEWTON - 1)
    with ExitStack() as ctx:
        t = Tools(nc, ctx, "pj")
        xt = [t.sb(f"x{b}", [P, 2 * HT, C]) for b in range(2)]
        gn = [t.sb(f"gn{b}", [P, 2 * HT, C]) for b in range(2)]
        sq = t.sb("sq", [P, 2 * HT, C])
        xn = [t.sb(f"xn{b}", [P, 2 * HT, C]) for b in range(2)]
        high = [t.sb(f"high{b}", [P, L], F32R) for b in range(2)]
        low = [t.sb(f"low{b}", [P, L], F32R) for b in range(2)]
        sig = [t.sb(f"sig{b}", [P, L]) for b in range(2)]
        out = [[t.sb(f"out{s}{b}", [P, UN, L]) for b in range(2)] for s in range(2)]
        gout = [t.sb(f"gout{b}", [P, UN, L]) for b in range(2)]
        sums = t.sb("sums", [P, 2, HT])
        sums_sq = t.sb("sums_sq", [P, 2, HT])
        mean_sq = t.sb("mean_sq", [P, 2 * HT])
        var = t.sb("var", [P, 2 * HT])
        var_eps = t.sb("var_eps", [P, 2 * HT])
        halved = t.sb("halved", [P, 2 * HT], I32)
        guess = t.sb("guess", [P, 2 * HT])
        guess_sq = t.sb("guess_sq", [P, 2 * HT])
        rest = t.sb("rest", [P, 2 * HT])
        last_sq = t.sb("last_sq", [P, 2 * HT])
        last_prod = t.sb("last_prod", [P, 2 * HT])
        last_rest = t.sb("last_rest", [P, 2 * HT])
        three = t.sb("three", [P, 2 * HT])
        one_half = t.sb("one_half", [P, 2 * HT])
        rs = t.sb("rs", [P, 2 * HT])
        x_ps = [t.ps(f"x{k}", [P, L]) for k in range(2)]
        proj_ps = [[t.ps(f"proj{s}{k}", [P, L]) for k in range(2)] for s in range(2)]
        g_ps = [t.ps(f"g{k}", [P, L]) for k in range(2)]

        x_loaded = [t.sem(f"x_loaded{b}") for b in range(2)]
        stored = [[t.sem(f"stored{s}{b}") for b in range(2)] for s in range(3)]
        gn_scaled = t.sem("gn_scaled")
        gn_ready = t.sem("gn_ready")
        sq_ready = t.sem("sq_ready")
        summed = t.sem("summed")
        summed_sq = t.sem("summed_sq")
        small = t.sem("small")
        constants = t.sem("constants")
        root_step = t.sem("root_step")
        xn_ready = t.sem("xn_ready")
        xt_ready = t.sem("xt_ready")
        high_ready = t.sem("high_ready")
        low_ready = t.sem("low_ready")
        gate_ready = [t.sem(f"gate_ready{s}") for s in range(2)]
        val_ready = [t.sem(f"val_ready{s}") for s in range(2)]
        sig_ready = [t.sem(f"sig_ready{s}") for s in range(2)]
        gated = [t.sem(f"gated{s}") for s in range(2)]
        g_ready = t.sem("g_ready")
        g_done = t.sem("g_done")

        x_v = x.rearrange("a (n r) (p t) c -> (a n) p r t c", r=TR, t=WT)
        side_v = [d.rearrange("e d (n r) j -> n (e d) (r j)", r=TR) for d in (left_d, right_d, gate_d)]
        block = ctx.enter_context(nc.Block())

        def tiles(eng, body):
            for n in range(2):
                body(n, n, 0)
            with eng.Fori(1, NT // 2 - 1) as j:
                for b in range(2):
                    body(2 * j + b, b, j)
            for b in range(2):
                body(NT - 2 + b, b, NT // 2 - 1)

        def is_first(n):
            return isinstance(n, int) and n < 2

        def is_zero(n):
            return isinstance(n, int) and n == 0

        def has_next(n, ahead=1):
            return not (isinstance(n, int) and n + ahead >= NT)

        def by_token(tile):
            return tile[:, :, :].rearrange("p (r t) c -> p r t c", t=WT)

        def half(tile, h):
            return tile[:, HT * h:HT * h + HT, :]

        @block.sync
        def _(sp):
            for b in range(2):
                sp.dma_start(by_token(xt[b]), x_v[b]).then_inc(x_loaded[b], DMA)

            def load(n, b):
                sp.wait_ge(gn_scaled, 2 * n - 2)
                sp.dma_start(by_token(xt[b]), x_v[n]).then_inc(x_loaded[b], DMA)

            load(2, 0)
            load(3, 1)

            def body(n, b, j):
                if has_next(n, 4):
                    load(n + 4, b)
                for s in range(2):
                    sp.wait_ge(gated[s], UN * n + UN)
                    sp.dma_start(side_v[s][n], out[s][b][:, :, :].rearrange("p q j -> p (q j)")).then_inc(stored[s][b], DMA)
                sp.wait_ge(g_done, UN * n + UN)
                sp.dma_start(side_v[2][n], gout[b][:, :, :].rearrange("p q j -> p (q j)")).then_inc(stored[2][b], DMA)

            for n in range(2):
                body(n, n, 0)
            with sp.Fori(1, NT // 2 - 2) as j:
                for b in range(2):
                    body(2 * j + b, b, j)
            for n in range(NT - 4, NT):
                body(n, n % 2, n // 2)
            for b in range(2):
                for s in range(3):
                    sp.wait_ge(stored[s][b], DMA * (NT // 2))

        @block.gpsimd
        def _(pool):
            def group_norm(n, b, j):
                pool.wait_ge(x_loaded[b], DMA * j + DMA)
                if not is_first(n):
                    pool.wait_ge(xn_ready, UN * n - UN)
                for h in range(2):
                    pool.tensor_tensor(half(gn[b], h), half(xt[b], h),
                                       keep.gn_scale[:, :].unsqueeze(1).to_broadcast([P, HT, C]),
                                       ALU.mult).then_inc(gn_scaled, 1)
                for h in range(2):
                    pool.wait_ge(gn_scaled, 2 * n + h + 1)
                    pool.tensor_tensor(half(gn[b], h), half(gn[b], h),
                                       keep.gn_shift[:, :].unsqueeze(1).to_broadcast([P, HT, C]),
                                       ALU.add).then_inc(gn_ready, 1)

            def root(n):
                pool.wait_ge(small, RS_STEPS * n + RS_STEPS)
                pool.tensor_tensor(last_sq[:, :], guess[:, :], guess[:, :], ALU.mult).then_inc(root_step, 1)
                pool.wait_ge(root_step, 5 * n + 1)
                pool.tensor_tensor(last_prod[:, :], last_sq[:, :], var_eps[:, :], ALU.mult).then_inc(root_step, 1)
                pool.wait_ge(root_step, 5 * n + 2)
                pool.tensor_tensor(last_rest[:, :], three[:, :], last_prod[:, :], ALU.subtract).then_inc(root_step, 1)
                pool.wait_ge(root_step, 5 * n + 3)
                pool.tensor_tensor(last_sq[:, :], last_rest[:, :], guess[:, :], ALU.mult).then_inc(root_step, 1)
                pool.wait_ge(root_step, 5 * n + 4)
                if not is_zero(n):
                    pool.wait_ge(xn_ready, UN * n)
                pool.tensor_tensor(rs[:, :], last_sq[:, :], one_half[:, :], ALU.mult).then_inc(root_step, 1)

            def normalise(n, b):
                pool.wait_ge(root_step, 5 * n + 5)
                for q in range(UN):
                    if not is_first(n):
                        pool.wait_ge(xt_ready, UN * (n - 2) + q + 1)
                    tok = slice(2 * WT * q, 2 * WT * q + 2 * WT)
                    pool.tensor_tensor(xn[b][:, tok, :], gn[b][:, tok, :],
                                       rs[:, tok].unsqueeze(2).to_broadcast([P, 2 * WT, C]),
                                       ALU.mult).then_inc(xn_ready, 1)

            pool.memset(three[:, :], 3.0).then_inc(constants, 1)
            pool.memset(one_half[:, :], 0.5).then_inc(constants, 1)
            pool.wait_ge(constants, 2)
            group_norm(0, 0, 0)
            group_norm(1, 1, 0)
            root(0)
            normalise(0, 0)
            group_norm(2, 0, 1)

            def body(n, b, j):
                if has_next(n):
                    root(n + 1)
                    normalise(n + 1, 1 - b)
                if has_next(n, 3):
                    group_norm(n + 3, 1 - b, j + 1 + b)

            for n in range(2):
                body(n, n, 0)
            with pool.Fori(1, NT // 2 - 2) as j:
                for b in range(2):
                    body(2 * j + b, b, j)
            for n in range(NT - 4, NT):
                body(n, n % 2, n // 2)

        @block.tensor
        def _(pe):
            def transposes(n, q, b):
                pe.wait_ge(xn_ready, UN * n + q + 1)
                if not (is_zero(n) and q < 2):
                    pe.wait_ge(low_ready, UN * n + q - 1)
                for r in range(2):
                    for k in range(2):
                        at = 2 * WT * q + WT * r + 2 * k
                        last = pe.transpose(x_ps[q % 2][:, H * r + k:H * r + H:2],
                                            xn[b][:, at:at + 2, :].rearrange("p t c -> p (t c)"),
                                            keep.ident[:, :])
                last.then_inc(xt_ready, 1)

            def product(bank, i, q):
                pe.matmul(bank[:, :], keep.w_high[:, i, :], high[q % 2][:, :], start=True, stop=False)
                pe.matmul(bank[:, :], keep.w_high[:, i, :], low[q % 2][:, :], start=False, stop=False)
                return pe.matmul(bank[:, :], keep.w_low[:, i, :], high[q % 2][:, :], start=False, stop=True)

            def side(n, q, s):
                if s == 0:
                    pe.wait_ge(high_ready, UN * n + q + 1)
                    pe.wait_ge(low_ready, UN * n + q + 1)
                if not (is_zero(n) and q == 0):
                    pe.wait_ge(gated[s], UN * n + q)
                product(proj_ps[s][1], 2 * s + 1, q).then_inc(gate_ready[s], 1)
                product(proj_ps[s][0], 2 * s, q).then_inc(val_ready[s], 1)

            def output_gate(n, q):
                if not (is_zero(n) and q < 2):
                    pe.wait_ge(g_done, UN * n + q - 1)
                product(g_ps[q % 2], 4, q).then_inc(g_ready, 1)

            transposes(0, 0, 0)

            def body(n, b, j):
                for q in range(UN):
                    if q < UN - 1:
                        transposes(n, q + 1, b)
                    side(n, q, 0)
                    if q == UN - 1 and has_next(n):
                        transposes(n + 1, 0, 1 - b)
                    side(n, q, 1)
                    output_gate(n, q)

            tiles(pe, body)

        @block.scalar
        def _(act):
            def square(n, b, h):
                act.wait_ge(gn_ready, 2 * n + h + 1)
                if not is_zero(n):
                    act.wait_ge(summed_sq, 2 * n + h - 1)
                act.activation(half(sq, h), half(gn[b], h), ACT.Square).then_inc(sq_ready, 1)

            def high_part(n, q):
                act.wait_ge(xt_ready, UN * n + q + 1)
                if not (is_zero(n) and q < 2):
                    act.wait_ge(g_ready, UN * n + q - 1)
                act.activation(high[q % 2][:, :], x_ps[q % 2][:, :], ACT.Copy).then_inc(high_ready, 1)

            def sigmoid(n, q, s):
                act.wait_ge(gate_ready[s], UN * n + q + 1)
                act.activation(sig[s][:, :], proj_ps[s][1][:, :], ACT.Sigmoid,
                               bias=keep.bias[:, 2 * s + 1:2 * s + 2]).then_inc(sig_ready[s], 1)

            def gate(n, q, b, j):
                act.wait_ge(g_ready, UN * n + q + 1)
                if q == 0 and not is_first(n):
                    act.wait_ge(stored[2][b], DMA * j)
                act.activation(gout[b][:, q, :], g_ps[q % 2][:, :], ACT.Sigmoid,
                               bias=keep.bias[:, 4:5]).then_inc(g_done, 1)

            for n in range(2):
                square(n, n, 0)
                square(n, n, 1)
            high_part(0, 0)

            def body(n, b, j):
                for q in range(UN):
                    if q < UN - 1:
                        high_part(n, q + 1)
                    sigmoid(n, q, 0)
                    if q == UN - 1 and has_next(n):
                        high_part(n + 1, 0)
                    sigmoid(n, q, 1)
                    if q < 2 and has_next(n, 2):
                        square(n + 2, b, q)
                    gate(n, q, b, j)

            tiles(act, body)

        @block.vector
        def _(dve):
            def sum_values(n, b, h):
                dve.wait_ge(gn_ready, 2 * n + h + 1)
                if not is_zero(n):
                    dve.wait_ge(small, RS_STEPS * n - RS_STEPS + 2)
                dve.tensor_reduce(sums[:, h, :], half(gn[b], h), AX.X, ALU.add).then_inc(summed, 1)

            def sum_squares(n, h):
                dve.wait_ge(sq_ready, 2 * n + h + 1)
                dve.tensor_reduce(sums_sq[:, h, :], half(sq, h), AX.X, ALU.add).then_inc(summed_sq, 1)

            def variance(n):
                sums_f, sums_sq_f = [v[:, :, :].rearrange("p h t -> p (h t)") for v in (sums, sums_sq)]
                done = RS_STEPS * n
                dve.wait_ge(summed, 2 * n + 2)
                dve.scalar_tensor_tensor(out=mean_sq[:, :], in0=sums_f, scalar=1.0 / C ** 2, in1=sums_f,
                                         op0=ALU.mult, op1=ALU.mult).then_inc(small, 1)
                dve.wait_ge(summed_sq, 2 * n + 2)
                dve.wait_ge(small, done + 1)
                dve.scalar_tensor_tensor(out=var[:, :], in0=sums_sq_f, scalar=1.0 / C, in1=mean_sq[:, :],
                                         op0=ALU.mult, op1=ALU.subtract).then_inc(small, 1)
                dve.wait_ge(small, done + 2)
                if not is_zero(n):
                    dve.wait_ge(root_step, 5 * n)
                dve.tensor_scalar(var_eps[:, :], var[:, :], 0.0, EPS, ALU.max, ALU.add).then_inc(small, 1)

            def first_guess(n):
                done = RS_STEPS * n + 3
                dve.wait_ge(small, done)
                dve.tensor_scalar(halved[:, :], var_eps[:, :].bitcast(I32), 1, None,
                                  ALU.logical_shift_right).then_inc(small, 1)
                dve.wait_ge(small, done + 1)
                dve.tensor_scalar(guess[:, :].bitcast(I32), halved[:, :], -1, 0x5F3759DF, ALU.mult,
                                  ALU.add).then_inc(small, 1)

            def newton(n, k):
                done = RS_STEPS * n + 5 + 3 * k
                dve.wait_ge(small, done)
                dve.tensor_tensor(guess_sq[:, :], guess[:, :], guess[:, :], ALU.mult).then_inc(small, 1)
                dve.wait_ge(small, done + 1)
                dve.scalar_tensor_tensor(out=rest[:, :], in0=guess_sq[:, :], scalar=-0.5, in1=var_eps[:, :],
                                         op0=ALU.mult, op1=ALU.mult).then_inc(small, 1)
                dve.wait_ge(small, done + 2)
                dve.scalar_tensor_tensor(out=guess[:, :], in0=rest[:, :], scalar=1.5,
                                         in1=guess[:, :], op0=ALU.add, op1=ALU.mult).then_inc(small, 1)

            def low_part(n, q):
                dve.wait_ge(high_ready, UN * n + q + 1)
                dve.tensor_tensor(low[q % 2][:, :], x_ps[q % 2][:, :], high[q % 2][:, :],
                                  ALU.subtract).then_inc(low_ready, 1)

            def value(n, q, s, b, j):
                dve.wait_ge(sig_ready[s], UN * n + q + 1)
                dve.wait_ge(val_ready[s], UN * n + q + 1)
                if q == 0 and not is_first(n):
                    dve.wait_ge(stored[s][b], DMA * j)
                dve.scalar_tensor_tensor(out=out[s][b][:, q, :], in0=proj_ps[s][0][:, :],
                                         scalar=keep.bias[:, 2 * s:2 * s + 1], in1=sig[s][:, :],
                                         op0=ALU.add, op1=ALU.mult).then_inc(gated[s], 1)

            def root(n):
                for h in range(2):
                    sum_values(n, n, h)
                    sum_squares(n, h)
                variance(n)
                first_guess(n)
                for k in range(NEWTON - 1):
                    newton(n, k)

            root(0)
            low_part(0, 0)
            root(1)

            def body(n, b, j):
                ahead = has_next(n, 2)
                low_part(n, 1)
                value(n, 0, 0, b, j)
                value(n, 0, 1, b, j)
                if ahead:
                    sum_values(n + 2, b, 0)
                low_part(n, 2)
                value(n, 1, 0, b, j)
                if ahead:
                    sum_squares(n + 2, 0)
                value(n, 1, 1, b, j)
                if ahead:
                    sum_values(n + 2, b, 1)
                low_part(n, 3)
                value(n, 2, 0, b, j)
                value(n, 2, 1, b, j)
                if ahead:
                    sum_squares(n + 2, 1)
                    variance(n + 2)
                value(n, 3, 0, b, j)
                if ahead:
                    first_guess(n + 2)
                    newton(n + 2, 0)
                if has_next(n):
                    low_part(n + 1, 0)
                value(n, 3, 1, b, j)
                if ahead:
                    newton(n + 2, 1)

            tiles(dve, body)




def contract(nc, left_d, right_d, mixed_d, keep):
    with ExitStack() as ctx:
        t = Tools(nc, ctx, "ct")
        lt = [t.sb(f"l{b}", [P, 2, WT, H]) for b in range(2)]
        rt = [t.sb(f"r{b}", [P, 2, WT, H]) for b in range(2)]
        l_hi = [t.sb(f"l_hi{b}", [P, 2, WT, H], F32R) for b in range(2)]
        l_lo = [t.sb(f"l_lo{b}", [P, 2, WT, H], F32R) for b in range(2)]
        r_hi = [t.sb(f"r_hi{b}", [P, 2, WT, H], F32R) for b in range(2)]
        r_lo = [t.sb(f"r_lo{b}", [P, 2, WT, H], F32R) for b in range(2)]
        om = [t.sb(f"o{b}", [P, 2, WT, H]) for b in range(2)]
        om_sq = t.sb("o_sq", [P, 2, WT, H])
        total = t.sb("total", [P, 2, WT, H])
        total_sq = t.sb("total_sq", [P, 2, WT, H])
        acc = [[t.ps(f"acc{b}{i}", [P, L]) for i in range(WT)] for b in range(2)]
        l_loaded = [t.sem(f"l_loaded{b}") for b in range(2)]
        r_loaded = [t.sem(f"r_loaded{b}") for b in range(2)]
        stored = [t.sem(f"stored{b}") for b in range(2)]
        l_high = t.sem("l_high")
        r_high = t.sem("r_high")
        l_low = t.sem("l_low")
        r_low = t.sem("r_low")
        summed = t.sem("summed")
        out_dve = t.sem("out_dve")
        out_act = t.sem("out_act")
        totals_set = t.sem("totals_set")
        squared = t.sem("squared")
        total_done = t.sem("total_done")
        total_sq_done = t.sem("total_sq_done")
        step = t.sem("step")
        var_in = t.sem("var_in")
        var_turned = t.sem("var_turned")
        root_in = t.sem("root_in")
        root_ready = t.sem("root_ready")
        view = [d.rearrange("e d (p t) j -> d p e (t j)", t=WT) for d in (left_d, right_d, mixed_d)]
        block = ctx.enter_context(nc.Block())

        def channels(eng, body):
            for n in range(2):
                body(n, n, 0)
            with eng.Fori(1, C // 2 - 1) as j:
                for b in range(2):
                    body(2 * j + b, b, j)
            for b in range(2):
                body(C - 2 + b, b, C // 2 - 1)

        def flat(tile):
            return tile[:, :, :, :].rearrange("p e t j -> p e (t j)")

        def is_first(n):
            return isinstance(n, int) and n < 2

        def is_zero(n):
            return isinstance(n, int) and n == 0

        def has_next(n):
            return not (isinstance(n, int) and n == C - 1)

        @block.sync
        def _(sp):
            for b in range(2):
                sp.dma_start(flat(lt[b]), view[0][b]).then_inc(l_loaded[b], DMA)
                sp.dma_start(flat(rt[b]), view[1][b]).then_inc(r_loaded[b], DMA)

            def body(n, b, j):
                if not (isinstance(n, int) and n >= C - 2):
                    sp.wait_ge(l_low, n + 1)
                    sp.dma_start(flat(lt[b]), view[0][n + 2]).then_inc(l_loaded[b], DMA)
                    sp.wait_ge(r_low, n + 1)
                    sp.dma_start(flat(rt[b]), view[1][n + 2]).then_inc(r_loaded[b], DMA)
                sp.wait_ge(out_dve, 2 * n + 2)
                sp.wait_ge(out_act, 2 * n + 2)
                sp.dma_start(view[2][n], flat(om[b])).then_inc(stored[b], DMA)

            channels(sp, body)
            for b in range(2):
                sp.wait_ge(stored[b], DMA * (C // 2))

        @block.tensor
        def _(pe):
            def body(n, b, j):
                pe.wait_ge(l_high, n + 1)
                pe.wait_ge(r_high, n + 1)
                pe.wait_ge(l_low, n + 1)
                pe.wait_ge(r_low, n + 1)
                for i in range(WT):
                    if not is_first(n):
                        pe.wait_ge(out_dve if i % 2 == 0 else out_act, 2 * n - 3 + i // 2)
                    bank = acc[b][i].rearrange("p (e j) -> p e j", e=2)
                    for k in range(WT):
                        high = r_hi[b][:, i % 2, k, i // 2:H:2]
                        low = r_lo[b][:, i % 2, k, i // 2:H:2]
                        pe.matmul(bank, high, l_hi[b][:, :, k, :], start=(k == 0), stop=False)
                        pe.matmul(bank, high, l_lo[b][:, :, k, :], start=False, stop=False)
                        last = pe.matmul(bank, low, l_hi[b][:, :, k, :], start=False, stop=(k == WT - 1))
                    last.then_inc(summed, 1)

            channels(pe, body)
            pe.wait_ge(var_in, 1)
            for i in range(WT):
                for k in range(WT):
                    last = pe.transpose(acc[0][i][:, P * k:P * k + P], total_sq[:, k % 2, i, k // 2:H:2],
                                        keep.ident[:, :])
                last.then_inc(var_turned, 1)

        @block.scalar
        def _(act):
            def high(n, b, j):
                act.wait_ge(l_loaded[b], DMA * j + DMA)
                if not is_first(n):
                    act.wait_ge(summed, WT * n - WT)
                for k in range(WT):
                    last = act.activation(l_hi[b][:, :, k, :], lt[b][:, :, k, :], ACT.Copy, scale=keep.mask_sq[:, k:k + 1])
                last.then_inc(l_high, 1)
                act.wait_ge(r_loaded[b], DMA * j + DMA)
                act.activation(r_hi[b][:, :, :, :], rt[b][:, :, :, :], ACT.Copy).then_inc(r_high, 1)

            high(0, 0, 0)

            def body(n, b, j):
                if has_next(n):
                    high(n + 1, 1 - b, j + b)
                if not is_first(n):
                    act.wait_ge(stored[b], DMA * j)
                    act.wait_ge(total_done, n - 1)
                for i in (1, 3):
                    act.wait_ge(summed, WT * n + i + 1)
                    act.activation(om[b][:, :, i, :], acc[b][i].rearrange("p (e j) -> p e j", e=2), ACT.Copy).then_inc(out_act, 1)
                act.wait_ge(out_dve, 2 * n + 2)
                act.wait_ge(out_act, 2 * n + 2)
                if not is_zero(n):
                    act.wait_ge(total_sq_done, n)
                act.activation(om_sq[:, :, :, :], om[b][:, :, :, :], ACT.Square).then_inc(squared, 1)

            channels(act, body)
            act.wait_ge(root_in, 1)
            act.activation(keep.token_root[:, :], keep.token_root[:, :], ACT.Sqrt).then_inc(root_ready, 1)

        @block.gpsimd
        def _(pool):
            pool.memset(total[:, :, :, :], 0.0).then_inc(totals_set, 1)
            pool.memset(total_sq[:, :, :, :], 0.0).then_inc(totals_set, 1)
            pool.wait_ge(totals_set, 2)

            def body(n, b, j):
                pool.wait_ge(squared, n + 1)
                if not is_zero(n):
                    pool.wait_ge(total_sq_done, n)
                pool.tensor_tensor(total_sq[:, :, :, :], total_sq[:, :, :, :], om_sq[:, :, :, :],
                                   ALU.add).then_inc(total_sq_done, 1)

            channels(pool, body)

        @block.vector
        def _(dve):
            def low(n, b, j):
                dve.wait_ge(l_loaded[b], DMA * j + DMA)
                dve.wait_ge(l_high, n + 1)
                if not is_first(n):
                    dve.wait_ge(summed, WT * n - WT)
                for k in range(WT):
                    last = dve.scalar_tensor_tensor(out=l_lo[b][:, :, k, :], in0=lt[b][:, :, k, :],
                                                    scalar=keep.mask_sq[:, k:k + 1], in1=l_hi[b][:, :, k, :],
                                                    op0=ALU.mult, op1=ALU.subtract)
                last.then_inc(l_low, 1)
                dve.wait_ge(r_loaded[b], DMA * j + DMA)
                dve.wait_ge(r_high, n + 1)
                dve.tensor_tensor(r_lo[b][:, :, :, :], rt[b][:, :, :, :], r_hi[b][:, :, :, :],
                                  ALU.subtract).then_inc(r_low, 1)

            low(0, 0, 0)
            dve.wait_ge(totals_set, 1)

            def body(n, b, j):
                if has_next(n):
                    low(n + 1, 1 - b, j + b)
                if not is_first(n):
                    dve.wait_ge(stored[b], DMA * j)
                    dve.wait_ge(squared, n - 1)
                for i in (0, 2):
                    dve.wait_ge(summed, WT * n + i + 1)
                    dve.tensor_copy(om[b][:, :, i, :], acc[b][i].rearrange("p (e j) -> p e j", e=2)).then_inc(out_dve, 1)
                dve.wait_ge(out_dve, 2 * n + 2)
                dve.wait_ge(out_act, 2 * n + 2)
                if not is_zero(n):
                    dve.wait_ge(total_done, n)
                dve.tensor_tensor(total[:, :, :, :], total[:, :, :, :], om[b][:, :, :, :],
                                  ALU.add).then_inc(total_done, 1)

            channels(dve, body)
            link = chained(dve, step)
            dve.wait_ge(total_done, C)
            whole = [v[:, :, :, :].rearrange("p e t j -> p (e t j)") for v in (total, total_sq)]
            link(dve.scalar_tensor_tensor(out=whole[0], in0=whole[0], scalar=1.0 / C ** 2, in1=whole[0],
                                          op0=ALU.mult, op1=ALU.mult))
            dve.wait_ge(total_sq_done, C)
            dve.scalar_tensor_tensor(out=whole[1], in0=whole[1], scalar=1.0 / C, in1=whole[0],
                                     op0=ALU.mult, op1=ALU.subtract).then_inc(var_in, 1)
            by_row = keep.mask_tok_sq[:, :].rearrange("p (i f t) -> p f i t", f=WT, t=WT)
            for i in range(WT):
                dve.wait_ge(var_turned, i + 1)
                last = dve.scalar_tensor_tensor(out=by_row[:, i, :, :], in0=acc[0][i].rearrange("p (t i) -> p i t", t=WT),
                                                scalar=0.0, in1=by_row[:, i, :, :], op0=ALU.max, op1=ALU.mult)
            link(last)
            dve.tensor_scalar(keep.token_root[:, :], keep.mask_tok_sq[:, :], EPS, None, ALU.add).then_inc(root_in, 1)




def finish_layer0(nc, x, mixed_d, gate_d, x1_d, fourier_d, keep):
    with ExitStack() as ctx:
        t = Tools(nc, ctx, "fi")
        xt = [t.sb(f"x{b}", [P, TR, WT, C]) for b in range(2)]
        x1 = [t.sb(f"x1{b}", [P, TR, WT, C]) for b in range(2)]
        gt = [t.sb(f"g{b}", [P, TR, H]) for b in range(2)]
        mt = [t.sb(f"m{b}", [P, TR, H]) for b in range(2)]
        yt = [t.sb(f"y{b}", [P, TR, WT, C]) for b in range(2)]
        x1_sq = t.sb("x1_sq", [P, TR, WT, C])
        four = [t.sb(f"four{b}", [M2, TR, C]) for b in range(2)]
        inv_root = t.sb("inv_root", [P, TR * WT])
        scale = [t.sb(f"scale{b}", [P, TR * WT]) for b in range(2)]
        square_sum = t.sb("square_sum", [P, TR, WT, C])
        row_sum = t.sb("row_sum", [C, C])
        y_ps = [t.ps(f"y{k}", [P, L]) for k in range(UN)]
        f_ps = [t.ps(f"f{b}", [M2, TR * C]) for b in range(2)]
        g_ps = [t.ps(f"g{k}", [P, L]) for k in range(2)]

        m_loaded = [t.sem(f"m_loaded{b}") for b in range(2)]
        x_loaded = [t.sem(f"x_loaded{b}") for b in range(2)]
        g_loaded = [t.sem(f"g_loaded{b}") for b in range(2)]
        x1_stored = [t.sem(f"x1_stored{b}") for b in range(2)]
        f_stored = [t.sem(f"f_stored{b}") for b in range(2)]
        y_ready = t.sem("y_ready")
        scale_step = t.sem("scale_step")
        y_scaled = t.sem("y_scaled")
        y_shifted = t.sem("y_shifted")
        y_gated = t.sem("y_gated")
        x1_ready = t.sem("x1_ready")
        x1_sq_ready = t.sem("x1_sq_ready")
        f_ready = t.sem("f_ready")
        f_copied = t.sem("f_copied")
        g_ready = t.sem("g_ready")
        sum_set = t.sem("sum_set")
        sum_done = t.sem("sum_done")
        ss_done = t.sem("ss_done")
        step = t.sem("step")

        x_v = x.rearrange("a (n r) (p t) c -> (a n) p r t c", r=TR, t=WT)
        x1_v = x1_d.rearrange("(n r) (p t) c -> n p r t c", r=TR, t=WT)
        g_v = gate_d.rearrange("e d (n r) j -> n (e d) r j", r=TR)
        m_v = mixed_d.rearrange("e d (n r) j -> n (e d) r j", r=TR)
        f_v = fourier_d.rearrange("m (n r) c -> n m r c", r=TR)
        block = ctx.enter_context(nc.Block())

        def tiles(eng, body):
            for n in range(4):
                body(n, n % 2, n // 2)
            with eng.Fori(2, NT // 2 - 1) as j:
                for b in range(2):
                    body(2 * j + b, b, j)
            for b in range(2):
                body(NT - 2 + b, b, NT // 2 - 1)

        def is_first(n):
            return isinstance(n, int) and n < 2

        def is_zero(n):
            return isinstance(n, int) and n == 0

        def has_next(n):
            return not (isinstance(n, int) and n == NT - 1)

        @block.sync
        def _(sp):
            def load_mixed(n, b):
                sp.dma_start(mt[b][:, :, :], m_v[n]).then_inc(m_loaded[b], DMA)

            def load_rest(n, b):
                sp.dma_start(gt[b][:, :, :], g_v[n]).then_inc(g_loaded[b], DMA)
                sp.dma_start(xt[b][:, :, :, :], x_v[n]).then_inc(x_loaded[b], DMA)

            for b in range(2):
                load_mixed(b, b)
                load_rest(b, b)

            def stores(n, b, load):
                sp.wait_ge(x1_ready, n + 1)
                if load:
                    load_rest(n + 2, b)
                sp.dma_start(x1_v[n], x1[b][:, :, :, :]).then_inc(x1_stored[b], DMA)

            def store_rows(n, b):
                sp.wait_ge(f_copied, n + 1)
                sp.dma_start(f_v[n], four[b][:, :, :]).then_inc(f_stored[b], DMA)

            def body(n, b, j):
                if not (isinstance(n, int) and n >= NT - 2):
                    sp.wait_ge(y_ready, UN * n + UN)
                    load_mixed(n + 2, b)
                if not is_zero(n):
                    stores(n - 1, 1 - b, load=not (isinstance(n, int) and n >= NT - 1))
                if not is_first(n):
                    store_rows(n - 2, b)

            tiles(sp, body)
            stores(NT - 1, 1, load=False)
            for n in range(NT - 2, NT):
                store_rows(n, n % 2)
            for b in range(2):
                sp.wait_ge(x1_stored[b], DMA * (NT // 2))
                sp.wait_ge(f_stored[b], DMA * (NT // 2))

        @block.tensor
        def _(pe):
            def output(n, q, b):
                if not is_zero(n):
                    pe.wait_ge(y_scaled, UN * n + q - UN + 1)
                for k in range(WT):
                    last = pe.matmul(y_ps[q][:, P * k:P * k + P], mt[b][:, 2 * q + k // 2, k % 2:H:2], keep.w2_bd[:, :],
                                     start=True, stop=True)
                last.then_inc(y_ready, 1)

            def transform(n, b):
                pe.wait_ge(x1_ready, n + 1)
                if not is_first(n):
                    pe.wait_ge(f_copied, n - 1)
                for k in range(WT):
                    last = pe.matmul(f_ps[b].rearrange("m (r c) -> m r c", c=C), keep.basis[:, k, :],
                                     x1[b][:, :, k, :], start=(k == 0), stop=(k == WT - 1))
                last.then_inc(f_ready, 1)

            def gate(n, q, b, j):
                if q == 0:
                    pe.wait_ge(g_loaded[b], DMA * j + DMA)
                if not (is_zero(n) and q < 2):
                    pe.wait_ge(y_gated, UN * n + q - 1)
                for k in range(WT):
                    last = pe.transpose(g_ps[q % 2][:, P * k:P * k + P], gt[b][:, 2 * q + k // 2, k % 2:H:2],
                                        keep.ident[:, :])
                last.then_inc(g_ready, 1)

            def body(n, b, j):
                pe.wait_ge(m_loaded[b], DMA * j + DMA)
                for q in range(UN):
                    output(n, q, b)
                if not is_zero(n):
                    for q in range(2, UN):
                        gate(n - 1, q, 1 - b, j - 1 + b)
                if not is_first(n):
                    transform(n - 2, b)
                for q in range(2):
                    gate(n, q, b, j)

            tiles(pe, body)
            for q in range(2, UN):
                gate(NT - 1, q, 1, NT // 2 - 1)
            for n in range(NT - 2, NT):
                transform(n, n % 2)
            bank = g_ps[0][0:C, :].rearrange("m (r c) -> m r c", c=C)
            pe.wait_ge(sum_done, NT - 1)
            for k in range(WT):
                pe.matmul(bank, keep.ones[:, :], square_sum[:, :, k, :], start=(k == 0), stop=False)
            pe.wait_ge(x1_sq_ready, NT)
            for k in range(WT):
                last = pe.matmul(bank, keep.ones[:, :], x1_sq[:, :, k, :], start=False, stop=(k == WT - 1))
            last.then_inc(ss_done, 1)

        @block.scalar
        def _(act):
            def result(n, b, j):
                act.wait_ge(x1_ready, n + 1)
                if not is_zero(n):
                    act.wait_ge(sum_done, n)
                act.activation(x1_sq[:, :, :, :], x1[b][:, :, :, :], ACT.Square).then_inc(x1_sq_ready, 1)
                act.wait_ge(f_ready, n + 1)
                if not is_first(n):
                    act.wait_ge(f_stored[b], DMA * j)
                act.activation(four[b][:, :, :], f_ps[b].rearrange("m (r c) -> m r c", c=C),
                               ACT.Copy).then_inc(f_copied, 1)

            def body(n, b, j):
                if not is_first(n):
                    result(n - 2, b, j - 1)

            tiles(act, body)
            for n in range(NT - 2, NT):
                result(n, n % 2, NT // 2 - 1)

        @block.gpsimd
        def _(pool):
            pool.memset(square_sum[:, :, :, :], 0.0).then_inc(sum_set, 1)
            pool.wait_ge(sum_set, 1)

            def add_squares(n):
                pool.wait_ge(x1_sq_ready, n + 1)
                if not is_zero(n):
                    pool.wait_ge(sum_done, n)
                pool.tensor_tensor(square_sum[:, :, :, :], square_sum[:, :, :, :], x1_sq[:, :, :, :],
                                   ALU.add).then_inc(sum_done, 1)

            def body(n, b, j):
                pool.wait_ge(y_scaled, UN * n + UN)
                y3 = yt[b][:, :, :, :].rearrange("p r t c -> p (r t) c")
                pool.tensor_tensor(y3, y3, keep.c_row[:, :].unsqueeze(1).to_broadcast([P, TR * WT, C]),
                                   ALU.add).then_inc(y_shifted, 1)
                if not is_first(n):
                    add_squares(n - 2)

            tiles(pool, body)
            add_squares(NT - 2)

        @block.vector
        def _(dve):
            def token_scale(n, b):
                if not is_zero(n):
                    dve.wait_ge(scale_step, 2 * n)
                dve.reciprocal(inv_root[:, :], keep.token_root[:, bass.ts(n, TR * WT)]).then_inc(scale_step, 1)
                dve.wait_ge(scale_step, 2 * n + 1)
                if not is_first(n):
                    dve.wait_ge(y_scaled, UN * n - UN)
                dve.tensor_tensor(scale[b][:, :], inv_root[:, :], keep.mask_tok[:, bass.ts(n, TR * WT)],
                                  ALU.mult).then_inc(scale_step, 1)

            def scaled(n, q, b):
                dve.wait_ge(scale_step, 2 * n + 2)
                dve.wait_ge(y_ready, UN * n + q + 1)
                if q == 0 and not is_first(n):
                    dve.wait_ge(x1_ready, n - 1)
                dve.tensor_tensor(yt[b][:, 2 * q:2 * q + 2, :, :].rearrange("p r t c -> p (r t) c"),
                                  y_ps[q].rearrange("p (t c) -> p t c", c=C),
                                  scale[b][:, 2 * WT * q:2 * WT * q + 2 * WT].unsqueeze(2).to_broadcast([P, 2 * WT, C]),
                                  ALU.mult).then_inc(y_scaled, 1)

            def finish(n, b, j):
                dve.wait_ge(y_shifted, n + 1)
                for q in range(UN):
                    dve.wait_ge(g_ready, UN * n + q + 1)
                    y_q = yt[b][:, 2 * q:2 * q + 2, :, :].rearrange("p r t c -> p (r t c)")
                    dve.tensor_tensor(y_q, g_ps[q % 2][:, :], y_q, ALU.mult).then_inc(y_gated, 1)
                dve.wait_ge(y_gated, UN * n + UN)
                dve.wait_ge(x_loaded[b], DMA * j + DMA)
                if not is_first(n):
                    dve.wait_ge(x1_stored[b], DMA * j)
                    dve.wait_ge(x1_sq_ready, n - 1)
                    dve.wait_ge(f_ready, n - 1)
                dve.tensor_tensor(x1[b][:, :, :, :], yt[b][:, :, :, :], xt[b][:, :, :, :],
                                  ALU.add).then_inc(x1_ready, 1)

            def body(n, b, j):
                token_scale(n, b)
                for q in range(UN):
                    scaled(n, q, b)
                if not is_zero(n):
                    finish(n - 1, 1 - b, j - 1 + b)

            tiles(dve, body)
            finish(NT - 1, 1, NT // 2 - 1)
            link = chained(dve, step)
            dve.wait_ge(ss_done, 1)
            link(dve.tensor_reduce(row_sum[:, :], g_ps[0][0:C, :].rearrange("m (r c) -> m c r", c=C), AX.X, ALU.add))
            link(dve.tensor_tensor(row_sum[:, :], row_sum[:, :], keep.ident[0:C, 0:C], ALU.mult))
            link(dve.tensor_reduce(keep.sum_sq[:, :], row_sum[:, :], AX.X, ALU.add))




def layer1(nc, fourier_d, x1_d, w_real, w_imag, inverse_rows, inverse_columns, out, keep):
    NM = MODES
    NG = 4
    GR = L // NG
    GP = P // NG
    GT = NT // NG
    CB = L // GR
    with ExitStack() as ctx:
        t = Tools(nc, ctx, "la")
        rows = t.sb("rows", [P, M2, WT, C])
        w = t.sb("w", [P, C, MODES, MODES])
        four = t.sb("four", [C, M2, M2])
        xr = t.sb("xr", [C, MODES, MODES])
        xi = t.sb("xi", [C, MODES, MODES])
        xm = t.sb("xm", [P, MODES * MODES, 2])
        mean_in = t.sb("mean_in", [C, 1])
        sq_in = t.sb("sq_in", [C, 1])
        sums = t.sb("sums", [C, 2])
        v = t.sb("v", [C, 8])
        root = t.sb("root", [C, 1])
        z = t.sb("z", [C, MODES * MODES, 2])
        q = t.sb("q", [C, M2, M2])
        spectrum = t.sb("spectrum", [P, C, P])
        inv_rows = t.sb("inv_rows", [P, GR])
        inv_cols = t.sb("inv_cols", [P, NG, L])
        col = t.sb("col", [P, GR, C])
        xt = [t.sb(f"x{b}", [P, TR, WT, C]) for b in range(2)]
        yo = [t.sb(f"yo{b}", [P, TR, WT, C]) for b in range(2)]
        ps = [t.ps(f"ps{k}", [P, L]) for k in range(8)]
        f_ps = [ps[a][0:C, 0:NM * M2] for a in range(2)]
        s_ps = ps[2][0:C, :]
        z_ps = ps[3][0:C, 0:2 * NM * NM].rearrange("p (a r) -> p a r", r=2)
        q_ps = [ps[4 + a][0:M2, :].rearrange("m (n o) -> m n o", o=C) for a in range(3)]
        f_loaded = t.sem("f_loaded")
        w_loaded = t.sem("w_loaded")
        inv_loaded = t.sem("inv_loaded")
        loaded = [t.sem(f"loaded{b}") for b in range(2)]
        stored = [t.sem(f"stored{b}") for b in range(2)]
        step = t.sem("step")
        f_ready = t.sem("f_ready")
        sums_in = t.sem("sums_in")
        sums_ready = t.sem("sums_ready")
        root_in = t.sem("root_in")
        root_ready = t.sem("root_ready")
        x_ready = t.sem("x_ready")
        z_ready = t.sem("z_ready")
        q_in = t.sem("q_in")
        q_ready = t.sem("q_ready")
        cleared = t.sem("cleared")
        spectrum_dve = t.sem("spectrum_dve")
        spectrum_act = t.sem("spectrum_act")
        col_ready = t.sem("col_ready")
        col_dve = t.sem("col_dve")
        col_act = t.sem("col_act")
        y_ready = t.sem("y_ready")
        y_done = t.sem("y_done")
        x_v = x1_d.rearrange("(n r) (p t) c -> n p r t c", r=TR, t=WT)
        o_v = out.rearrange("a (n r) (p t) c -> (a n) p r t c", r=TR, t=WT)
        block = ctx.enter_context(nc.Block())

        def tiles(eng, body):
            for n in range(2):
                body(n, n, 0)
            with eng.Fori(1, NT // 2 - 1) as j:
                for b in range(2):
                    body(2 * j + b, b, j)
            for b in range(2):
                body(NT - 2 + b, b, NT // 2 - 1)

        def is_first(n):
            return isinstance(n, int) and n < 2

        def fill_spectrum(copy, a):
            for g in range(NG):
                at = GP * g + 8 * a
                last = copy(spectrum[GP * g:GP * g + M2, :, at:at + 8], q_ps[a].rearrange("m n o -> m o n"))
            return last

        def copy_col(copy, i):
            return copy(col[:, :, CB * i:CB * i + CB], ps[i % 4].rearrange("p (c r) -> p r c", c=CB))

        @block.sync
        def _(sp):
            sp.dma_start(rows[:, :, :, :], fourier_d.rearrange("m (p t) c -> p m t c", t=WT)).then_inc(f_loaded, DMA)
            sp.dma_start(w[0:C, :, :, :], w_real).then_inc(w_loaded, DMA)
            sp.dma_start(w[C:P, :, :, :], w_imag).then_inc(w_loaded, DMA)
            sp.dma_start(inv_rows[:, :], inverse_rows).then_inc(inv_loaded, DMA)
            sp.dma_start(inv_cols[:, :, :], inverse_columns).then_inc(inv_loaded, DMA)
            for b in range(2):
                sp.dma_start(xt[b][:, :, :, :], x_v[b]).then_inc(loaded[b], DMA)

            def body(n, b, j):
                sp.wait_ge(y_done, WT * n + WT)
                if not (isinstance(n, int) and n >= NT - 2):
                    sp.dma_start(xt[b][:, :, :, :], x_v[n + 2]).then_inc(loaded[b], DMA)
                sp.dma_start(o_v[n], yo[b][:, :, :, :]).then_inc(stored[b], DMA)

            tiles(sp, body)
            for b in range(2):
                sp.wait_ge(stored[b], DMA * (NT // 2))

        @block.gpsimd
        def _(pool):
            pool.memset(spectrum[:, :, :], 0.0).then_inc(cleared, 1)

        @block.tensor
        def _(pe):
            pe.wait_ge(f_loaded, DMA)
            for n in range(M2):
                for k in range(WT):
                    last = pe.matmul(f_ps[n // NM][:, M2 * (n % NM):M2 * (n % NM) + M2],
                                     rows[:, n, k, :],
                                     keep.basis[:, k, :], start=(k == 0), stop=(k == WT - 1))
            last.then_inc(f_ready, 1)
            pe.wait_ge(sums_in, 1)
            pe.matmul(s_ps[:, 0:1], keep.pair[:, :], mean_in[:, :], start=True, stop=True)
            pe.matmul(s_ps[:, 1:2], keep.pair[:, :], sq_in[:, :], start=True, stop=True).then_inc(sums_ready, 1)
            pe.wait_ge(w_loaded, 2 * DMA)
            pe.wait_ge(x_ready, 1)
            for n in range(NM):
                for m in range(NM):
                    last = pe.matmul(z_ps[:, n * NM + m, :], w[:, :, m, n], xm[:, n * NM + m, :],
                                     start=True, stop=True)
            last.then_inc(z_ready, 1)
            pe.wait_ge(q_in, 1)
            for n in range(M2):
                last = pe.transpose(q_ps[n // 8][:, n % 8, :], q[:, n, :], keep.ident[0:C, 0:C])
            last.then_inc(q_ready, 1)
            pe.wait_ge(inv_loaded, 2 * DMA)
            pe.wait_ge(spectrum_dve, 2)
            pe.wait_ge(spectrum_act, 1)
            for i in range(C // CB):
                if i >= 4:
                    pe.wait_ge(col_dve if i % 2 == 0 else col_act, (i - 4) // 2 + 1)
                for o in range(CB):
                    last = pe.matmul(ps[i % 4][:, GR * o:GR * o + GR], spectrum[:, CB * i + o, :], inv_rows[:, :],
                                     start=True, stop=True)
                last.then_inc(col_ready, 1)
            pe.wait_ge(col_dve, C // CB // 2)
            pe.wait_ge(col_act, C // CB // 2)

            def tile(n, b, g):
                for k in range(WT):
                    if not is_first(n):
                        pe.wait_ge(y_done, WT * (n - 2) + k + 1)
                    pe.matmul(ps[WT * b + k][:, :], inv_cols[:, g, k:L:WT],
                              col[:, bass.ds(TR * n - GR * g, TR), :].rearrange("m r c -> m (r c)"),
                              start=True, stop=True).then_inc(y_ready, 1)

            for b in range(2):
                tile(b, b, 0)
            for g in range(NG):
                with pe.Fori(max(g * GT // 2, 1), (g + 1) * GT // 2) as j:
                    for b in range(2):
                        tile(2 * j + b, b, g)

        @block.scalar
        def _(act):
            act.wait_ge(root_in, 1)
            act.activation(root[:, :], v[:, 5:6], ACT.Sqrt).then_inc(root_ready, 1)

            def copy(dst, src):
                return act.activation(dst, src, ACT.Copy)

            act.wait_ge(cleared, 1)
            act.wait_ge(q_ready, 1)
            fill_spectrum(copy, 2).then_inc(spectrum_act, 1)
            for i in range(1, C // CB, 2):
                act.wait_ge(col_ready, i + 1)
                copy_col(copy, i).then_inc(col_act, 1)

        @block.vector
        def _(dve):
            link = chained(dve, step)
            dve.wait_ge(f_ready, 1)
            for a in range(2):
                last = dve.tensor_copy(four[:, NM * a:NM * a + NM, :].rearrange("p n m -> p (n m)"), f_ps[a])
            link(last)
            dve.tensor_tensor(xr[:, :, :], four[:, 0:NM, 0:NM], four[:, NM:M2, NM:M2], ALU.subtract)
            dve.tensor_tensor(xi[:, :, :], four[:, 0:NM, NM:M2], four[:, NM:M2, 0:NM], ALU.add)
            dve.tensor_scalar(mean_in[:, :], four[:, 0, 0:1], 1.0 / TOK, None, ALU.mult)
            dve.tensor_scalar(sq_in[:, :], keep.sum_sq[:, :], 1.0 / TOK, None, ALU.mult).then_inc(sums_in, 1)
            dve.wait_ge(sums_ready, 1)
            link(dve.tensor_copy(sums[:, :], s_ps[:, 0:2]))
            link(dve.tensor_tensor(v[:, 0:1], sums[:, 0:1], sums[:, 0:1], ALU.mult))
            link(dve.tensor_tensor(v[:, 1:2], sums[:, 1:2], v[:, 0:1], ALU.subtract))
            dve.tensor_scalar(v[:, 5:6], v[:, 1:2], 0.0, EPS, ALU.max, ALU.add).then_inc(root_in, 1)
            link(dve.tensor_scalar(v[:, 2:3], sums[:, 0:1], float(TOK), None, ALU.mult))
            dve.wait_ge(root_ready, 1)
            link(dve.reciprocal(v[:, 3:4], root[:, :]))
            link(dve.tensor_tensor(xr[:, 0, 0:1], xr[:, 0, 0:1], v[:, 2:3], ALU.subtract))
            link(dve.tensor_scalar(v[:, 4:5], v[:, 3:4], -1.0, None, ALU.mult))
            xr_f = xr[:, :, :].rearrange("p n m -> p (n m)")
            xi_f = xi[:, :, :].rearrange("p n m -> p (n m)")
            dve.tensor_scalar(xm[0:C, :, 0], xr_f, v[:, 3:4], None, ALU.mult)
            dve.tensor_scalar(xm[0:C, :, 1], xi_f, v[:, 4:5], None, ALU.mult)
            dve.tensor_scalar(xm[C:P, :, 0], xi_f, v[:, 3:4], None, ALU.mult)
            dve.tensor_scalar(xm[C:P, :, 1], xr_f, v[:, 3:4], None, ALU.mult).then_inc(x_ready, 1)
            dve.wait_ge(z_ready, 1)
            link(dve.tensor_copy(z[:, :, :], z_ps[:, :, :]))
            zr = z[:, :, 0].rearrange("o (n m) -> o n m", m=NM)
            zi = z[:, :, 1].rearrange("o (n m) -> o n m", m=NM)
            dve.tensor_copy(q[:, 0:NM, 0:NM], zr)
            dve.tensor_scalar(q[:, 0:NM, NM:M2], zi, -1.0, None, ALU.mult)
            dve.tensor_scalar(q[:, NM:M2, 0:NM], zi, -1.0, None, ALU.mult)
            dve.tensor_scalar(q[:, NM:M2, NM:M2], zr, -1.0, None, ALU.mult).then_inc(q_in, 1)
            dve.wait_ge(q_ready, 1)
            dve.wait_ge(cleared, 1)
            for a in range(2):
                fill_spectrum(dve.tensor_copy, a).then_inc(spectrum_dve, 1)
            for i in range(0, C // CB, 2):
                dve.wait_ge(col_ready, i + 1)
                copy_col(dve.tensor_copy, i).then_inc(col_dve, 1)

            def body(n, b, j):
                dve.wait_ge(loaded[b], DMA * j + DMA)
                if not is_first(n):
                    dve.wait_ge(stored[b], DMA * j)
                for k in range(WT):
                    dve.wait_ge(y_ready, WT * n + k + 1)
                    dve.tensor_tensor(yo[b][:, :, k, :], ps[WT * b + k][:, :].rearrange("p (r c) -> p r c", c=C),
                                      xt[b][:, :, k, :], ALU.add).then_inc(y_done, 1)

            tiles(dve, body)


class Keep:
    pass


def program(nc, ins, tab, out):
    x = ins["x"]
    left_d = nc.dram_tensor("left_d", [2, C, L, H], F32, kind="Internal").ap()
    right_d = nc.dram_tensor("right_d", [2, C, L, H], F32, kind="Internal").ap()
    mixed_d = nc.dram_tensor("mixed_d", [2, C, L, H], F32, kind="Internal").ap()
    gate_d = nc.dram_tensor("gate_d", [2, C, L, H], F32, kind="Internal").ap()
    x1_d = nc.dram_tensor("x1_d", [L, L, C], F32, kind="Internal").ap()
    fourier_d = nc.dram_tensor("fourier_d", [M2, L, C], F32, kind="Internal").ap()
    with ExitStack() as ctx:
        t = Tools(nc, ctx, "keep")
        k = Keep()
        k.ident = t.sb("ident", [P, P])
        k.basis = t.sb("basis", [P, WT, M2])
        k.pair = t.sb("pair", [C, C])
        k.sum_sq = t.sb("sum_sq", [C, 1])
        with ExitStack() as layer0:
            t = Tools(nc, layer0, "layer0")
            k.gn_scale = t.sb("gn_scale", [P, C])
            k.gn_shift = t.sb("gn_shift", [P, C])
            k.w_high = t.sb("w_high", [P, 5, P], F32R)
            k.w_low = t.sb("w_low", [P, 5, P], F32R)
            k.bias = t.sb("bias", [P, 5])
            k.w2_bd = t.sb("w2_bd", [P, P])
            k.c_row = t.sb("c_row", [P, C])
            k.ones = t.sb("ones", [P, C])
            k.mask_sq = t.sb("mask_sq", [P, WT])
            k.mask_tok = t.sb("mask_tok", [P, NT * 32])
            k.mask_tok_sq = t.sb("mask_tok_sq", [P, NT * 32])
            k.token_root = k.mask_tok_sq
            prepare(nc, x, ins, tab, k)
            project(nc, x, left_d, right_d, gate_d, k)
            contract(nc, left_d, right_d, mixed_d, k)
            finish_layer0(nc, x, mixed_d, gate_d, x1_d, fourier_d, k)
        layer1(nc, fourier_d, x1_d, ins["L1_conv_w_real"], ins["L1_conv_w_imag"], tab["t_inverse_rows"],
               tab["t_inverse_columns"], out, k)


def kernel(**inputs):
    import concourse.bacc as bacc
    from concourse.bass_utils import run_bass_kernel_spmd

    nc = bacc.Bacc("TRN2", target_bir_lowering=False, num_devices=1)
    arrays, ins, tab = {}, {}, {}
    for name, value in inputs.items():
        a = np.ascontiguousarray(value)
        arrays[f"in_{name}"] = a
        ins[name] = nc.dram_tensor(f"in_{name}", a.shape, mybir.dt.from_np(a.dtype), kind="ExternalInput").ap()
    for name, a in host_tables().items():
        a = np.ascontiguousarray(a)
        arrays[name] = a
        tab[name] = nc.dram_tensor(name, a.shape, mybir.dt.from_np(a.dtype), kind="ExternalInput").ap()
    out = nc.dram_tensor("out_0", (1, L, L, C), F32, kind="ExternalOutput").ap()
    program(nc, ins, tab, out)
    r = run_bass_kernel_spmd(nc, [arrays], core_ids=[0])
    return r.results[0]["out_0"]
```
